# Optimizing a Trainium2 kernel written in Bass

```python
import numpy as np
import jax
import jax.numpy as jnp

def _softmax(x, axis=-1):
    return jax.nn.softmax(x, axis=axis)

def _gelu(x):
    return jax.nn.gelu(x, approximate=True)

def _silu(x):
    return jax.nn.silu(x)

def _sigmoid(x):
    return jax.nn.sigmoid(x)

def _layernorm(x, axis=-1, eps=1e-05):
    m = jnp.mean(x, axis=axis, keepdims=True)
    v = jnp.var(x, axis=axis, keepdims=True)
    return (x - m) / jnp.sqrt(v + eps)

def _scatter_add(tgt, idx, src, axis=0):
    return tgt.at[idx].add(src)

def _segment_sum(src, seg, n):
    return jax.ops.segment_sum(src, seg, n)
kernel_name = 'mk_prb_d1_jaxref_r8_a4035f'

def setup_inputs(seed: int=0):
    np.random.seed(seed)
    _w = jnp.asarray

    def _L0_attn_setup():
        import jax, jax.numpy as jnp
        import numpy as np
        NUM_LANDMARKS = 64
        key = jax.random.key(seed)
        ks = jax.random.split(key, 4)
        B, S, D = (4, 512, 128)
        init = 0.02
        return {'hidden_states': jax.random.normal(ks[0], (B, S, D), dtype=jnp.float32), 'Wq': jax.random.normal(ks[1], (D, D), dtype=jnp.float32) * init, 'bq': jnp.zeros((D,), dtype=jnp.float32), 'Wk': jax.random.normal(ks[2], (D, D), dtype=jnp.float32) * init, 'bk': jnp.zeros((D,), dtype=jnp.float32), 'Wv': jax.random.normal(ks[3], (D, D), dtype=jnp.float32) * init, 'bv': jnp.zeros((D,), dtype=jnp.float32)}
    _L0_attn_in = _L0_attn_setup()

    def _L0_ffn_setup():
        import jax, jax.numpy as jnp
        import numpy as np
        D_MODEL = 128
        N_HEADS = 16
        HEAD_DIM = D_MODEL // N_HEADS
        KV_LATENT = 64
        N_EXPERTS = 4
        D_HIDDEN = 4 * D_MODEL
        B, T = (2, 128)

        def rmsnorm(x, w, eps=1e-06):
            return w * (x * jax.lax.rsqrt(jnp.mean(x * x, axis=-1, keepdims=True) + eps))

        def layernorm(x, g, b, eps=1e-05):
            mu = jnp.mean(x, axis=-1, keepdims=True)
            var = jnp.mean((x - mu) ** 2, axis=-1, keepdims=True)
            return (x - mu) * jax.lax.rsqrt(var + eps) * g + b

        def apply_rope(x):
            t, d = (x.shape[2], x.shape[3])
            half = d // 2
            pos = jnp.arange(t, dtype=x.dtype)[:, None]
            inv_freq = 1.0 / 10000.0 ** (jnp.arange(half, dtype=x.dtype) / half)
            ang = pos * inv_freq[None, :]
            sin, cos = (jnp.sin(ang), jnp.cos(ang))
            x1, x2 = (x[..., :half], x[..., half:])
            return jnp.concatenate([x1 * cos - x2 * sin, x1 * sin + x2 * cos], axis=-1)

        def mla_attention(x, Wq, Wdkv, Wuk, Wuv, Wo, ln_g, ln_b):
            b, t, _ = x.shape
            q = (x @ Wq.T).reshape(b, t, N_HEADS, HEAD_DIM).transpose(0, 2, 1, 3)
            latent = layernorm(x @ Wdkv.T, ln_g, ln_b)
            k = (latent @ Wuk.T).reshape(b, t, N_HEADS, HEAD_DIM).transpose(0, 2, 1, 3)
            v = (latent @ Wuv.T).reshape(b, t, N_HEADS, HEAD_DIM).transpose(0, 2, 1, 3)
            q = apply_rope(q)
            k = apply_rope(k)
            scores = jnp.einsum('bhqd,bhkd->bhqk', q, k) / np.sqrt(HEAD_DIM)
            causal = jnp.tril(jnp.ones((t, t), dtype=bool))
            scores = jnp.where(causal, scores, -jnp.inf)
            attn = jax.nn.softmax(scores, axis=-1)
            out = jnp.einsum('bhqk,bhkd->bhqd', attn, v).transpose(0, 2, 1, 3).reshape(b, t, D_MODEL)
            return out @ Wo.T

        def moe(x, gate_w, gate_b, W1, b1, W2, b2):
            logits = x @ gate_w.T + gate_b
            top = jnp.argmax(logits, axis=-1)
            onehot = jax.nn.one_hot(top, N_EXPERTS, dtype=x.dtype)
            h = jax.nn.relu(jnp.einsum('btd,ehd->bteh', x, W1) + b1)
            y = jnp.einsum('bteh,edh->bted', h, W2) + b2
            return jnp.einsum('bted,bte->btd', y, onehot)
        key = jax.random.key(seed)
        ks = jax.random.split(key, 16)
        s = lambda fan_in: 1.0 / np.sqrt(fan_in)
        return {'x': jax.random.normal(ks[0], (B, T, D_MODEL), jnp.float32), 'norm1_w': jnp.ones((D_MODEL,), jnp.float32), 'norm2_w': jnp.ones((D_MODEL,), jnp.float32), 'Wq': jax.random.normal(ks[1], (D_MODEL, D_MODEL), jnp.float32) * s(D_MODEL), 'Wdkv': jax.random.normal(ks[2], (KV_LATENT, D_MODEL), jnp.float32) * s(D_MODEL), 'Wuk': jax.random.normal(ks[3], (D_MODEL, KV_LATENT), jnp.float32) * s(KV_LATENT), 'Wuv': jax.random.normal(ks[4], (D_MODEL, KV_LATENT), jnp.float32) * s(KV_LATENT), 'Wo': jax.random.normal(ks[5], (D_MODEL, D_MODEL), jnp.float32) * s(D_MODEL), 'ln_g': jnp.ones((KV_LATENT,), jnp.float32), 'ln_b': jnp.zeros((KV_LATENT,), jnp.float32), 'gate_w': jax.random.normal(ks[6], (N_EXPERTS, D_MODEL), jnp.float32) * s(D_MODEL), 'gate_b': jnp.zeros((N_EXPERTS,), jnp.float32), 'W1': jax.random.normal(ks[7], (N_EXPERTS, D_HIDDEN, D_MODEL), jnp.float32) * s(D_MODEL), 'b1': jnp.zeros((N_EXPERTS, D_HIDDEN), jnp.float32), 'W2': jax.random.normal(ks[8], (N_EXPERTS, D_MODEL, D_HIDDEN), jnp.float32) * s(D_HIDDEN), 'b2': jnp.zeros((N_EXPERTS, D_MODEL), jnp.float32)}
    _L0_ffn_in = _L0_ffn_setup()
    _d = {'L0_attn_hidden_states': _L0_attn_in['hidden_states'], 'L0_attn_Wq': _L0_attn_in['Wq'], 'L0_attn_bq': _L0_attn_in['bq'], 'L0_attn_Wk': _L0_attn_in['Wk'], 'L0_attn_bk': _L0_attn_in['bk'], 'L0_attn_Wv': _L0_attn_in['Wv'], 'L0_attn_bv': _L0_attn_in['bv'], 'L0_ffn_norm1_w': _L0_ffn_in['norm1_w'], 'L0_ffn_norm2_w': _L0_ffn_in['norm2_w'], 'L0_ffn_Wq': _L0_ffn_in['Wq'], 'L0_ffn_Wdkv': _L0_ffn_in['Wdkv'], 'L0_ffn_Wuk': _L0_ffn_in['Wuk'], 'L0_ffn_Wuv': _L0_ffn_in['Wuv'], 'L0_ffn_Wo': _L0_ffn_in['Wo'], 'L0_ffn_ln_g': _L0_ffn_in['ln_g'], 'L0_ffn_ln_b': _L0_ffn_in['ln_b'], 'L0_ffn_gate_w': _L0_ffn_in['gate_w'], 'L0_ffn_gate_b': _L0_ffn_in['gate_b'], 'L0_ffn_W1': _L0_ffn_in['W1'], 'L0_ffn_b1': _L0_ffn_in['b1'], 'L0_ffn_W2': _L0_ffn_in['W2'], 'L0_ffn_b2': _L0_ffn_in['b2']}
    _x0 = _d['L0_attn_hidden_states']
    _d['L0_attn_hidden_states'] = jax.random.normal(jax.random.fold_in(jax.random.key(seed), 1), (16, 256, 128), dtype=_x0.dtype)
    del _x0
    return _d

def reference(L0_attn_hidden_states, L0_attn_Wq, L0_attn_bq, L0_attn_Wk, L0_attn_bk, L0_attn_Wv, L0_attn_bv, L0_ffn_norm1_w, L0_ffn_norm2_w, L0_ffn_Wq, L0_ffn_Wdkv, L0_ffn_Wuk, L0_ffn_Wuv, L0_ffn_Wo, L0_ffn_ln_g, L0_ffn_ln_b, L0_ffn_gate_w, L0_ffn_gate_b, L0_ffn_W1, L0_ffn_b1, L0_ffn_W2, L0_ffn_b2):

    def _L0_attn_ref(hidden_states, Wq, bq, Wk, bk, Wv, bv):
        import jax, jax.numpy as jnp
        import numpy as np
        NUM_LANDMARKS = 64
        B, S, D = hidden_states.shape
        L = NUM_LANDMARKS
        q = hidden_states @ Wq + bq
        k = hidden_states @ Wk + bk
        v = hidden_states @ Wv + bv
        q = jax.nn.softmax(q, axis=-1)
        k = jax.nn.softmax(k, axis=-1)
        k_landmarks = k.reshape(B, L, S // L, D).mean(axis=2)
        kernel_1 = jnp.einsum('bqd,bkd->bqk', q, k_landmarks)
        kernel_2 = jnp.einsum('bkd,bld->bkl', k_landmarks, k)
        kernel_3 = k * v
        mid = jnp.einsum('bkl,bld->bkd', kernel_2, kernel_3)
        output = jnp.einsum('bqk,bkd->bqd', kernel_1, mid)
        return output

    def _L0_ffn_ref(x, norm1_w, norm2_w, Wq, Wdkv, Wuk, Wuv, Wo, ln_g, ln_b, gate_w, gate_b, W1, b1, W2, b2):
        import jax, jax.numpy as jnp
        import numpy as np
        D_MODEL = 128
        N_HEADS = 16
        HEAD_DIM = D_MODEL // N_HEADS
        KV_LATENT = 64
        N_EXPERTS = 4
        D_HIDDEN = 4 * D_MODEL
        B, T = (2, 128)

        def rmsnorm(x, w, eps=1e-06):
            return w * (x * jax.lax.rsqrt(jnp.mean(x * x, axis=-1, keepdims=True) + eps))

        def layernorm(x, g, b, eps=1e-05):
            mu = jnp.mean(x, axis=-1, keepdims=True)
            var = jnp.mean((x - mu) ** 2, axis=-1, keepdims=True)
            return (x - mu) * jax.lax.rsqrt(var + eps) * g + b

        def apply_rope(x):
            t, d = (x.shape[2], x.shape[3])
            half = d // 2
            pos = jnp.arange(t, dtype=x.dtype)[:, None]
            inv_freq = 1.0 / 10000.0 ** (jnp.arange(half, dtype=x.dtype) / half)
            ang = pos * inv_freq[None, :]
            sin, cos = (jnp.sin(ang), jnp.cos(ang))
            x1, x2 = (x[..., :half], x[..., half:])
            return jnp.concatenate([x1 * cos - x2 * sin, x1 * sin + x2 * cos], axis=-1)

        def mla_attention(x, Wq, Wdkv, Wuk, Wuv, Wo, ln_g, ln_b):
            b, t, _ = x.shape
            q = (x @ Wq.T).reshape(b, t, N_HEADS, HEAD_DIM).transpose(0, 2, 1, 3)
            latent = layernorm(x @ Wdkv.T, ln_g, ln_b)
            k = (latent @ Wuk.T).reshape(b, t, N_HEADS, HEAD_DIM).transpose(0, 2, 1, 3)
            v = (latent @ Wuv.T).reshape(b, t, N_HEADS, HEAD_DIM).transpose(0, 2, 1, 3)
            q = apply_rope(q)
            k = apply_rope(k)
            scores = jnp.einsum('bhqd,bhkd->bhqk', q, k) / np.sqrt(HEAD_DIM)
            causal = jnp.tril(jnp.ones((t, t), dtype=bool))
            scores = jnp.where(causal, scores, -jnp.inf)
            attn = jax.nn.softmax(scores, axis=-1)
            out = jnp.einsum('bhqk,bhkd->bhqd', attn, v).transpose(0, 2, 1, 3).reshape(b, t, D_MODEL)
            return out @ Wo.T

        def moe(x, gate_w, gate_b, W1, b1, W2, b2):
            logits = x @ gate_w.T + gate_b
            top = jnp.argmax(logits, axis=-1)
            onehot = jax.nn.one_hot(top, N_EXPERTS, dtype=x.dtype)
            h = jax.nn.relu(jnp.einsum('btd,ehd->bteh', x, W1) + b1)
            y = jnp.einsum('bteh,edh->bted', h, W2) + b2
            return jnp.einsum('bted,bte->btd', y, onehot)
        x = x + mla_attention(rmsnorm(x, norm1_w), Wq, Wdkv, Wuk, Wuv, Wo, ln_g, ln_b)
        x = x + moe(rmsnorm(x, norm2_w), gate_w, gate_b, W1, b1, W2, b2)
        return x
    x = L0_attn_hidden_states
    xn = _layernorm(x, axis=-1)
    x = x + _L0_attn_ref(xn, L0_attn_Wq, L0_attn_bq, L0_attn_Wk, L0_attn_bk, L0_attn_Wv, L0_attn_bv) + _L0_ffn_ref(xn, L0_ffn_norm1_w, L0_ffn_norm2_w, L0_ffn_Wq, L0_ffn_Wdkv, L0_ffn_Wuk, L0_ffn_Wuv, L0_ffn_Wo, L0_ffn_ln_g, L0_ffn_ln_b, L0_ffn_gate_w, L0_ffn_gate_b, L0_ffn_W1, L0_ffn_b1, L0_ffn_W2, L0_ffn_b2)
    return x

_drawn_inputs = setup_inputs


def setup_inputs(seed=0):
    import zlib

    import numpy as np

    out = dict(_drawn_inputs(seed))
    spreads = {'L0_attn_bq': (0.0, 2.0),
     'L0_attn_bk': (0.0, 2.0),
     'L0_attn_bv': (0.0, 2.0),
     'L0_ffn_norm1_w': (1.0, 0.2),
     'L0_ffn_norm2_w': (1.0, 0.2),
     'L0_ffn_ln_g': (1.0, 0.2),
     'L0_ffn_ln_b': (0.0, 0.1),
     'L0_ffn_gate_b': (0.0, 0.1),
     'L0_ffn_b1': (0.0, 0.1),
     'L0_ffn_b2': (0.0, 0.1)}
    factors = {'L0_attn_Wq': 64.0, 'L0_attn_Wk': 64.0, 'L0_attn_Wv': 64.0}
    for name, (base, spread) in spreads.items():
        noise = np.random.default_rng([zlib.crc32(name.encode()), seed]).standard_normal(out[name].shape)
        drawn = base * np.exp(spread * noise) if base else spread * noise
        out[name] = jnp.asarray(drawn.astype(out[name].dtype))
    for name, factor in factors.items():
        out[name] = (out[name] * factor).astype(out[name].dtype)
    return out
```

```python
import numpy as np

import concourse.bass as bass
from concourse import mybir
from contextlib import ExitStack

B, S, D = 16, 256, 128
P = 128
T = S // P
H, HD = 16, 8
L = 64
E, F = 4, 512
FC = F // P
PARTS = 3
STACK = PARTS * PARTS * HD
ROWS = STACK + PARTS
HG = H // 2
NTOK = B * S
GT = 512
MASKED = -1e38


def build(nc, dram, out):
    f32, bf16 = mybir.dt.float32, mybir.dt.bfloat16
    ALU, ACT, AX = mybir.AluOpType, mybir.ActivationFunctionType, mybir.AxisListType
    ctx = ExitStack()
    with ctx:
        def sb(name, shape, dt=f32):
            return ctx.enter_context(nc.sbuf_tensor(name, shape, dt))

        def two(name, shape, dt=f32):
            return [sb(f"{name}{i}", shape, dt) for i in range(2)]

        def sem(name):
            return ctx.enter_context(nc.semaphore(name))

        def spread(ap, n):
            return ap.unsqueeze(len(ap.shape)).broadcast_to(tuple(ap.shape) + (n,))

        def past(v):
            return max(v, 0) if isinstance(v, int) else v

        ident = sb("ident", [P, P])
        ident16 = sb("ident16", [P, P], bf16)
        mask_raw = sb("mask_raw", [P, 2, P])
        mask16 = sb("mask16", [P, 2, P], bf16)
        pool4 = sb("pool4", [P, T, P])
        rope = sb("rope", [P, 2, 2, T, 64])
        wa = sb("wa", [P, 3 * D])
        wb = sb("wb", [P, D + L])
        wkv = sb("wkv", [L + 1, 2 * D])
        ln_g = sb("ln_g", [L, 1])
        ln_b = sb("ln_b", [L, L + 1])
        n1w = sb("n1w", [P, 1])
        n2w = sb("n2w", [P, 1])
        wo = sb("wo", [P, D])
        gate = sb("gate", [P, E])
        gate_b = sb("gate_b", [P, E])
        w1 = sb("w1", [P, E, F])
        w2 = sb("w2", [P, E, FC, D])
        part_row = sb("part_row", [PARTS, PARTS])
        ones16 = sb("ones16", [PARTS, P], bf16)
        NBIAS = 3 * D + E * D
        brow = sb("brow", [PARTS, NBIAS])
        btmp = sb("btmp", [PARTS, 2, NBIAS])
        bpart = sb("bpart", [PARTS, PARTS, NBIAS], bf16)
        bias16 = sb("bias16", [PARTS, NBIAS], bf16)
        b1c = sb("b1c", [P, E, FC])
        zero = sb("zero", [P, 1])
        mhalf = sb("mhalf", [P, T])
        eps5 = sb("eps5", [P, T])
        eps6 = sb("eps6", [P, T])

        x_in = two("x_in", [P, T, D])
        xn = two("xn", [P, T, D])
        xnl = two("xnl", [P, T, D])
        bn = two("bn", [P, T, 6])
        mv = two("mv", [P, T, 2])
        ln = two("ln", [P, 6, T])
        xnT = two("xnT", [P, S])
        qkv = two("qkv", [P, T, 3 * D])
        qy = two("qy", [P, T, D + L])
        ybn = two("ybn", [P, T, 6])
        ymv = two("ymv", [P, T, 2])
        yln = two("yln", [P, 5, T])
        lat = two("lat", [P, T, P])
        latT = two("latT", [L + 1, S])
        kraw = two("kraw", [P, T, D])
        vaug = two("vaug", [P, T, H, HD + 1])
        qs = two("qs", [P, T, D])
        ra = two("ra", [P, T, D])
        rb = two("rb", [P, T, D])
        qrot = two("qrot", [P, T, D])
        krot = two("krot", [P, T, D])
        part = two("part", [P, PARTS, 2 * S], bf16)
        res = two("res", [P, 2 * S])
        qst = two("qst", [ROWS, H * S], bf16)
        kst = two("kst", [ROWS, H * S], bf16)
        nmax = two("nmax", [P, HG, T])
        mres = two("mres", [P, HG * T])
        nmp = two("nmp", [P, P], bf16)
        mT = two("mT", [PARTS * HG * T, P], bf16)
        prob = two("prob", [P, HG, S + P])
        rden = two("rden", [P, T, HG])
        o = two("o", [P, T, H, HD])
        oT = two("oT", [P, S])
        x1 = two("x1", [P, T, D])
        x1bn = two("x1bn", [P, T, 6])
        x1mv = two("x1mv", [P, T, 2])
        x1ln = two("x1ln", [P, 4, T])
        z = two("z", [P, T, D])
        nqk = two("nqk", [P, T, 2])
        qks = two("qks", [P, T, 2 * D])
        eqk = two("eqk", [P, T, 2 * D])
        sqk = two("sqk", [P, 2, T, 2])
        kh = two("kh", [P, T, D])
        k3 = two("k3", [P, T, D])
        eqT = two("eqT", [P, S])
        klC = two("klC", [P, 2 * D])
        gram = two("gram", [P, D])
        mid = two("mid", [P, D])
        accx = two("accx", [P, T, D])
        acc_all = sb("acc_all", [P, B * T, D])
        zT_all = sb("zT_all", [P, NTOK])

        NG, GTILES = NTOK // GT, GT // P
        zg = [qkv[i][:, :, :].rearrange("p t n -> p (t n)")[:, 0:GT] for i in range(2)]
        hT = [prob[i][:, :, :].rearrange("p h q -> p (h q)")[:, k * GT:(k + 1) * GT] for i in range(2) for k in range(6)]
        hT += [t_[i][:, :, :].rearrange("p t n -> p (t n)") for t_ in (eqk, qks) for i in range(2)]
        lg = sb("lg", [P, GTILES, E])
        lmax = sb("lmax", [P, GTILES])
        hit = sb("hit", [P, GTILES, E])
        open_ = sb("open_", [P, GTILES, E])
        top = sb("top", [P, GTILES, E])

        ps_max = [ctx.enter_context(nc.psum_tensor(f"ps_max{i}", [P, 512], f32)) for i in range(2)]
        ps_exp = [ctx.enter_context(nc.psum_tensor(f"ps_exp{i}", [P, 2, 512], f32)) for i in range(2)]
        m0 = ctx.enter_context(nc.psum_tensor("m0", [P, 512], f32))
        m1 = ctx.enter_context(nc.psum_tensor("m1", [P, 512], f32))
        m1h = m1[:, :].bitcast(bf16)

        w_loaded = sem("w_loaded")
        w_ready = sem("w_ready")
        bias_ready = sem("bias_ready")
        x_loaded = sem("x_loaded")
        bn_ready = sem("bn_ready")
        mv_ready = sem("mv_ready")
        ln_ready = sem("ln_ready")
        xn_ready = sem("xn_ready")
        xnT_filled = sem("xnT_filled")
        xnT_ready = sem("xnT_ready")
        projA_filled = sem("projA_filled")
        projA_ready = sem("projA_ready")
        projB_filled = sem("projB_filled")
        projB_ready = sem("projB_ready")
        ybn_ready = sem("ybn_ready")
        ymv_ready = sem("ymv_ready")
        yln_ready = sem("yln_ready")
        lat_ready = sem("lat_ready")
        latT_filled = sem("latT_filled")
        latT_ready = sem("latT_ready")
        kv_filled = sem("kv_filled")
        k_ready = sem("k_ready")
        v_ready = sem("v_ready")
        qrope_ready = sem("qrope_ready")
        krope_ready = sem("krope_ready")
        qkT_filled = sem("qkT_filled")
        part1_ready = sem("part1_ready")
        res1_ready = sem("res1_ready")
        part2_ready = sem("part2_ready")
        part3_ready = sem("part3_ready")
        q_spread = sem("q_spread")
        k_spread = sem("k_spread")
        max_filled = sem("max_filled")
        max_read = sem("max_read")
        msplit_ready = sem("msplit_ready")
        mT_filled = sem("mT_filled")
        mT_ready = sem("mT_ready")
        m_spread = sem("m_spread")
        exp_filled = sem("exp_filled")
        exp_ready = sem("exp_ready")
        pv_filled = sem("pv_filled")
        rden_ready = sem("rden_ready")
        o_ready = sem("o_ready")
        oT_filled = sem("oT_filled")
        oT_ready = sem("oT_ready")
        wo_filled = sem("wo_filled")
        x1_ready = sem("x1_ready")
        x1bn_ready = sem("x1bn_ready")
        x1mv_ready = sem("x1mv_ready")
        x1ln_ready = sem("x1ln_ready")
        z_ready = sem("z_ready")
        acc_ready = sem("acc_ready")
        zT_filled = sem("zT_filled")
        zT_ready = sem("zT_ready")
        nqk_ready = sem("nqk_ready")
        qks_ready = sem("qks_ready")
        eqk_ready = sem("eqk_ready")
        sqk_ready = sem("sqk_ready")
        kh_ready = sem("kh_ready")
        k3_ready = sem("k3_ready")
        eqT_filled = sem("eqT_filled")
        eqT_ready = sem("eqT_ready")
        klC_filled = sem("klC_filled")
        klC_ready = sem("klC_ready")
        gram_filled = sem("gram_filled")
        gram_ready = sem("gram_ready")
        mid_filled = sem("mid_filled")
        mid_ready = sem("mid_ready")
        l0_filled = sem("l0_filled")
        l0_ready = sem("l0_ready")
        xnl_ready = sem("xnl_ready")
        setup = sem("setup")
        out_stored = sem("out_stored")
        bias_ready_v = sem("bias_ready_v")
        lnb_filled = sem("lnb_filled")
        zg_ready = sem("zg_ready")
        gate_filled = sem("gate_filled")
        lg_ready = sem("lg_ready")
        top_ready = sem("top_ready")
        up_filled = sem("up_filled")
        relu_a = sem("relu_a")
        relu_v = sem("relu_v")
        down_filled = sem("down_filled")
        mix_ready = sem("mix_ready")

        NW = 19
        block = ctx.enter_context(nc.Block())

        def steps(eng, slot0, slot1, prologue, last):
            prologue()
            for b in (0, 1):
                slot0(b, b % 2)
                slot1(b, b % 2)
            with eng.Fori(1, B // 2 - 1, 1) as i:
                for k in (0, 1):
                    b = 2 * i + k
                    slot0(b, k)
                    slot1(b, k)
            for b in (B - 2, B - 1):
                slot0(b, b % 2)
                slot1(b, b % 2)
            last()

        def there(b, ahead):
            return not isinstance(b, int) or 0 <= b + ahead < B

        @block.sync
        def _(sp):
            pairs = [(ident, "ident"), (mask_raw, "mask"), (pool4, "pool4"), (rope, "rope"), (wa, "wa"), (wb, "wb"),
                     (n1w, "n1w"), (n2w, "n2w"), (wo, "wo"), (gate, "gate"), (gate_b, "gate_b"), (w1, "w1"), (w2, "w2"),
                     (part_row, "part_row"), (brow, "brow"), (b1c, "b1c"), (ln_g, "ln_g"), (ln_b, "ln_b")]

            def load_x(b, p):
                sp.wait_ge(l0_ready, past(2 * (b - 1)))
                sp.dma_start(x_in[p][:, :, :], dram["x"][bass.ds(b, 1)].rearrange("o (t p) d -> p (o t) d", p=P)
                             if not isinstance(b, int) else dram["x"][b].rearrange("(t p) d -> p t d", p=P)
                             ).then_inc(x_loaded, 16)

            def spread_qk(b, p):
                sp.wait_ge(part3_ready, b + 1)
                for i in range(PARTS):
                    for j in range(PARTS):
                        r = HD * (PARTS * i + j)
                        sp.dma_start(qst[p][r:r + HD, :], part[p][:, i, 0:S]).then_inc(q_spread, 16)
                        sp.dma_start(kst[p][r:r + HD, :], part[p][:, j, S:2 * S]).then_inc(k_spread, 16)

            def spread_m(b, p, g):
                sp.wait_ge(mT_ready, 2 * b + g + 1)
                sp.dma_start(qst[p][STACK:ROWS, g * HG * S:(g + 1) * HG * S], mT[g][:, :]).then_inc(m_spread, 16)

            def prologue():
                load_x(0, 0)
                load_x(1, 1)
                for t, n in pairs:
                    sp.dma_start(t[tuple(slice(None) for _ in t.shape)], dram[n]).then_inc(w_loaded, 16)
                sp.dma_start(wkv[0:L, :], dram["wkv"]).then_inc(w_loaded, 16)
                spread_qk(0, 0)
                spread_m(0, 0, 0)

            def slot0(b, p):
                if there(b, 2):
                    load_x(b + 2, p)
                if there(b, 1):
                    spread_qk(b + 1, 1 - p)
                spread_m(b, p, 1)

            def slot1(b, p):
                if there(b, 1):
                    spread_m(b + 1, 1 - p, 0)

            def last():
                pass

            steps(sp, slot0, slot1, prologue, last)
            out_t = out.rearrange("b (t p) d -> p (b t) d", p=P)
            with sp.Fori(0, NG, 1) as g:
                sp.wait_ge(mix_ready, (g + 1) * GTILES * E)
                sp.dma_start(out_t[:, bass.ds(g * GTILES, GTILES), :],
                             acc_all[:, bass.ds(g * GTILES, GTILES), :]).then_inc(out_stored, 16)
            sp.wait_ge(out_stored, 16 * NG)

        @block.gpsimd
        def _(pool):
            def tt(o_, a, c, op):
                return pool.tensor_tensor(o_, a, c, op)

            def layer_norm(b, p):
                n = 6 * b
                pool.wait_ge(mv_ready, 2 * b + 2)
                tt(ln[p][:, 0], mv[p][:, :, 1], eps5[:, :], ALU.add).then_inc(ln_ready, 1)
                pool.wait_ge(ln_ready, n + 1)
                tt(ln[p][:, 1], ln[p][:, 0], mhalf[:, :], ALU.pow).then_inc(ln_ready, 1)
                pool.wait_ge(ln_ready, n + 2)
                tt(ln[p][:, 2], mv[p][:, :, 1], ln[p][:, 1], ALU.mult).then_inc(ln_ready, 1)
                pool.wait_ge(ln_ready, n + 3)
                tt(ln[p][:, 3], ln[p][:, 2], ln[p][:, 1], ALU.mult).then_inc(ln_ready, 1)
                pool.wait_ge(ln_ready, n + 4)
                tt(ln[p][:, 4], ln[p][:, 3], eps6[:, :], ALU.add).then_inc(ln_ready, 1)
                pool.wait_ge(ln_ready, n + 5)
                tt(ln[p][:, 5], ln[p][:, 4], mhalf[:, :], ALU.pow).then_inc(ln_ready, 1)

            def latent_scale(b, p):
                n = 5 * b
                pool.wait_ge(ln_ready, 6 * b + 6)
                tt(yln[p][:, 0], ln[p][:, 5], ln[p][:, 5], ALU.mult).then_inc(yln_ready, 1)
                pool.wait_ge(yln_ready, n + 1)
                pool.wait_ge(ymv_ready, 2 * b + 2)
                tt(yln[p][:, 1], yln[p][:, 0], ymv[p][:, :, 1], ALU.mult).then_inc(yln_ready, 1)
                pool.wait_ge(yln_ready, n + 2)
                tt(yln[p][:, 2], yln[p][:, 1], eps5[:, :], ALU.add).then_inc(yln_ready, 1)
                pool.wait_ge(yln_ready, n + 3)
                tt(yln[p][:, 3], yln[p][:, 2], mhalf[:, :], ALU.pow).then_inc(yln_ready, 1)
                pool.wait_ge(yln_ready, n + 4)
                tt(yln[p][:, 4], yln[p][:, 3], ln[p][:, 5], ALU.mult).then_inc(yln_ready, 1)

            def rotate(src, dst, which, ready, n, p):
                c = rope[:, which, 0, :, :].unsqueeze(2).broadcast_to((P, T, 2, 64))
                v = src[:, :, :].rearrange("p t (a c) -> p t a c", a=2)
                w = rb[p][:, :, :].rearrange("p t (a c) -> p t a c", a=2)
                tt(ra[p][:, :, :].rearrange("p t (a c) -> p t a c", a=2), v, c, ALU.mult)
                tt(w[:, :, 1, :], v[:, :, 0, :], rope[:, which, 1, :, :], ALU.mult)
                tt(w[:, :, 0, :], v[:, :, 1, :], rope[:, which, 1, :, :], ALU.mult).then_inc(ready, 1)
                pool.wait_ge(ready, n)
                d = dst[:, :, :].rearrange("p t (a c) -> p t a c", a=2)
                u = ra[p][:, :, :].rearrange("p t (a c) -> p t a c", a=2)
                tt(d[:, :, 0, :], u[:, :, 0, :], w[:, :, 0, :], ALU.subtract)
                tt(d[:, :, 1, :], u[:, :, 1, :], w[:, :, 1, :], ALU.add).then_inc(ready, 1)

            def rope_q(b, p):
                pool.wait_ge(projB_ready, b + 1)
                pool.wait_ge(qkT_filled, past(b - 1))
                tt(qs[p][:, :, :], qy[p][:, :, 0:D], spread(ln[p][:, 5], D), ALU.mult).then_inc(qrope_ready, 1)
                pool.wait_ge(qrope_ready, 3 * b + 1)
                rotate(qs[p], qrot[p], 0, qrope_ready, 3 * b + 2, p)

            def rope_k(b, p):
                pool.wait_ge(k_ready, b + 1)
                pool.wait_ge(qrope_ready, 3 * b + 3)
                rotate(kraw[p], krot[p], 1, krope_ready, 2 * b + 1, p)

            def parts(b, p):
                pool.wait_ge(res1_ready, b + 1)
                pool.wait_ge(k_spread, past(9 * 16 * (b - 1)))
                tt(part[p][:, 1, :], res[p][:, :], zero[:, 0:1].broadcast_to((P, 2 * S)), ALU.add).then_inc(part2_ready, 1)
                pool.wait_ge(part2_ready, b + 1)
                pool.wait_ge(exp_filled, past(6 * (b - 1)))
                tt(part[p][:, 2, :], res[p][:, :], part[p][:, 1, :], ALU.subtract).then_inc(part3_ready, 1)

            def soft_shift(b, p):
                pool.wait_ge(nqk_ready, b + 1)
                v = lambda t_, w_: t_[:, :, 0:2 * D].rearrange("p t (j d) -> p t j d", j=2)
                tt(v(qks[p], 0), v(qkv[p], 0), spread(nqk[p][:, :, :], D), ALU.add).then_inc(qks_ready, 1)

            def soft_k(b, p):
                pool.wait_ge(sqk_ready, 2 * b + 2)
                tt(kh[p][:, :, :], eqk[p][:, :, D:2 * D], spread(sqk[p][:, 1, :, 1], D), ALU.mult).then_inc(kh_ready, 1)
                pool.wait_ge(kh_ready, b + 1)
                tt(k3[p][:, :, :], kh[p][:, :, :], qkv[p][:, :, 2 * D:3 * D], ALU.mult).then_inc(k3_ready, 1)

            def late_xn(b, p):
                pool.wait_ge(x1_ready, past(b - 1))
                pool.wait_ge(xn_ready, 2 * b + 2)
                tt(xnl[p][:, :, :], xn[p][:, :, :], zero[:, 0:1].unsqueeze(2).broadcast_to((P, T, D)), ALU.add).then_inc(xnl_ready, 1)

            def finish(b, p):
                n = 4 * b
                pool.wait_ge(x1mv_ready, 2 * b + 2)
                tt(x1ln[p][:, 0], x1mv[p][:, :, 0], x1mv[p][:, :, 0], ALU.mult).then_inc(x1ln_ready, 1)
                pool.wait_ge(x1ln_ready, n + 1)
                tt(x1ln[p][:, 1], x1ln[p][:, 0], x1mv[p][:, :, 1], ALU.add).then_inc(x1ln_ready, 1)
                pool.wait_ge(x1ln_ready, n + 2)
                tt(x1ln[p][:, 2], x1ln[p][:, 1], eps6[:, :], ALU.add).then_inc(x1ln_ready, 1)
                pool.wait_ge(x1ln_ready, n + 3)
                tt(x1ln[p][:, 3], x1ln[p][:, 2], mhalf[:, :], ALU.pow).then_inc(x1ln_ready, 1)
                pool.wait_ge(x1ln_ready, n + 4)
                tt(z[p][:, :, :], x1[p][:, :, :], spread(x1ln[p][:, 3], D), ALU.mult).then_inc(z_ready, 1)
                pool.wait_ge(l0_ready, 2 * b + 2)
                tt(acc_all[:, bass.ds(b * T, T), :], accx[p][:, :, :], x1[p][:, :, :], ALU.add).then_inc(acc_ready, 1)

            def slot0(b, p):
                if there(b, 1):
                    rope_q(b + 1, 1 - p)
                    soft_shift(b + 1, 1 - p)
                if there(b, 2):
                    layer_norm(b + 2, p)
                if there(b, 1):
                    rope_k(b + 1, 1 - p)
                if there(b, -1):
                    finish(b - 1, 1 - p)
                if there(b, 1):
                    parts(b + 1, 1 - p)
                    soft_k(b + 1, 1 - p)

            def slot1(b, p):
                if there(b, 1):
                    late_xn(b + 1, 1 - p)
                if there(b, 2):
                    latent_scale(b + 2, p)

            def prologue():
                for t_, v in ((zero, 0.0), (mhalf, -0.5), (eps5, 1e-5), (eps6, 1e-6)):
                    pool.memset(t_[:, :], v).then_inc(setup, 1)
                pool.wait_ge(setup, 4)
                pool.wait_ge(w_loaded, 16 * NW)
                layer_norm(0, 0)
                latent_scale(0, 0)
                rope_q(0, 0)
                soft_shift(0, 0)
                layer_norm(1, 1)
                rope_k(0, 0)
                parts(0, 0)
                soft_k(0, 0)
                late_xn(0, 0)
                latent_scale(1, 1)

            def last():
                finish(B - 1, 1)

            steps(pool, slot0, slot1, prologue, last)

        @block.scalar
        def _(act):
            def copy(dst, src):
                return act.activation(dst, src, ACT.Copy)

            def kv(b, p):
                act.wait_ge(kv_filled, b + 1)
                act.wait_ge(krope_ready, past(2 * (b - 1)))
                copy(kraw[p][:, :, :], m0[:, :].rearrange("p (t n) -> p t n", t=T)[:, :, 0:D]).then_inc(k_ready, 1)
                act.wait_ge(pv_filled, past(2 * (b - 1)))
                for t in range(T):
                    ins = copy(vaug[p][:, t, :, 0:HD], m0[:, t * 2 * D + D:(t + 1) * 2 * D].rearrange("p (h d) -> p h d", d=HD))
                ins.then_inc(v_ready, 1)

            def part1(b, p):
                act.wait_ge(qkT_filled, b + 1)
                act.wait_ge(k_spread, past(9 * 16 * (b - 1)))
                act.wait_ge(q_spread, past(9 * 16 * (b - 1)))
                copy(part[p][:, 0, :], m0[:, :]).then_inc(part1_ready, 1)

            def evac(b, filled, ready, dst, src, n=1, k=0):
                act.wait_ge(filled, n * b + k + 1)
                copy(dst, src).then_inc(ready, 1)

            def exp_chunk(b, p, g, c):
                n = 6 * b + 3 * g + c
                act.wait_ge(exp_filled, n + 1)
                if c == 0:
                    act.wait_ge(pv_filled, past(2 * (b - 1) + g + 1))
                bank = ps_exp[(3 * g + c) % 2]
                if c < 2:
                    dst = prob[g][:, 4 * c:4 * c + 4, 0:S]
                    src = bank[:, :, :].rearrange("p a (h q) -> p (a h) q", h=2)
                else:
                    dst = prob[g][:, :, S:S + P]
                    src = bank[:, :, :].rearrange("p a (h q) -> p (a h) q", h=4)
                act.activation(dst, src, ACT.Exp).then_inc(exp_ready, 1)

            def soft_exp(b, p):
                act.wait_ge(qks_ready, b + 1)
                act.activation(eqk[p][:, :, :], qks[p][:, :, :], ACT.Exp).then_inc(eqk_ready, 1)

            def slot0(b, p):
                exp_chunk(b, p, 0, 0)
                if there(b, 1):
                    kv(b + 1, 1 - p)
                if there(b, -1):
                    evac(b - 1, oT_filled, oT_ready, oT[1 - p][:, :], m1[:, 0:S])
                exp_chunk(b, p, 0, 1)
                exp_chunk(b, p, 0, 2)
                if there(b, 1):
                    soft_exp(b + 1, 1 - p)
                    part1(b + 1, 1 - p)
                if there(b, -1):
                    evac(b - 1, zT_filled, zT_ready, zT_all[:, bass.ds((b - 1) * S, S)], m1[:, 0:S])
                evac(b, mT_filled, mT_ready, mT[1][:, :], m1h[0:PARTS * HG * T, 0:P], 2, 1)

            def slot1(b, p):
                q, r = 1 - p, p
                if there(b, 2):
                    evac(b + 2, xnT_filled, xnT_ready, xnT[p][:, :], m0[:, 0:S])
                    evac(b + 2, projA_filled, projA_ready, qkv[p][:, 0, :], m0[:, 0:3 * D], 2, 0)
                if there(b, 1):
                    evac(b + 1, eqT_filled, eqT_ready, eqT[q][:, :], m1[:, 0:S])
                exp_chunk(b, p, 1, 0)
                if there(b, 2):
                    evac(b + 2, projA_filled, projA_ready, qkv[p][:, 1, :], m0[:, 0:3 * D], 2, 1)
                if there(b, 1):
                    evac(b + 1, klC_filled, klC_ready, klC[q][:, :], m1[:, 0:2 * D])
                exp_chunk(b, p, 1, 1)
                if there(b, 2):
                    evac(b + 2, projB_filled, projB_ready, qy[p][:, :, :], m0[:, 0:T * (D + L)].rearrange("p (t n) -> p t n", t=T))
                if there(b, 1):
                    evac(b + 1, gram_filled, gram_ready, gram[q][:, :], m1[:, 0:D])
                exp_chunk(b, p, 1, 2)
                if there(b, 1):
                    evac(b + 1, mid_filled, mid_ready, mid[q][:, :], m1[:, 0:D])
                if there(b, 2):
                    evac(b + 2, latT_filled, latT_ready, latT[p][:, :], m0[0:L + 1, 0:S])
                if there(b, 1):
                    evac(b + 1, mT_filled, mT_ready, mT[0][:, :], m1h[0:PARTS * HG * T, 0:P], 2, 0)

            def front(b, p):
                evac(b, xnT_filled, xnT_ready, xnT[p][:, :], m0[:, 0:S])
                for t in range(T):
                    evac(b, projA_filled, projA_ready, qkv[p][:, t, :], m0[:, 0:3 * D], 2, t)
                evac(b, projB_filled, projB_ready, qy[p][:, :, :], m0[:, 0:T * (D + L)].rearrange("p (t n) -> p t n", t=T))
                evac(b, latT_filled, latT_ready, latT[p][:, :], m0[0:L + 1, 0:S])

            def prologue():
                act.wait_ge(lnb_filled, 1)
                copy(wkv[L:L + 1, :], m0[L:L + 1, 0:2 * D]).then_inc(bias_ready, 1)
                front(0, 0)
                kv(0, 0)
                soft_exp(0, 0)
                part1(0, 0)
                front(1, 1)
                evac(0, eqT_filled, eqT_ready, eqT[0][:, :], m1[:, 0:S])
                evac(0, klC_filled, klC_ready, klC[0][:, :], m1[:, 0:2 * D])
                evac(0, gram_filled, gram_ready, gram[0][:, :], m1[:, 0:D])
                evac(0, mid_filled, mid_ready, mid[0][:, :], m1[:, 0:D])
                evac(0, mT_filled, mT_ready, mT[0][:, :], m1h[0:PARTS * HG * T, 0:P], 2, 0)

            def last():
                evac(B - 1, oT_filled, oT_ready, oT[1][:, :], m1[:, 0:S])
                evac(B - 1, zT_filled, zT_ready, zT_all[:, (B - 1) * S:B * S], m1[:, 0:S])

            steps(act, slot0, slot1, prologue, last)

            def experts(g, p):
                act.wait_ge(zT_ready, B)
                act.wait_ge(up_filled, past((g - 1) * E * FC))
                copy(zg[p], zT_all[:, bass.ds(g * GT, GT)]).then_inc(zg_ready, 1)
                for n in range(0, E * FC, 2):
                    act.wait_ge(up_filled, g * E * FC + n + 1)
                    if n == 0:
                        act.wait_ge(down_filled, g * GTILES)
                    act.activation(hT[n], ps_exp[(n // 2) % 2][:, 0, :], ACT.Relu,
                                   bias=b1c[:, n // FC, n % FC:n % FC + 1]).then_inc(relu_a, 1)

            experts(0, 0)
            experts(1, 1)
            with act.Fori(1, NG // 2, 1) as i:
                experts(2 * i, 0)
                experts(2 * i + 1, 1)

        @block.vector
        def _(dve):
            def stats(src, st, st_ready, src_ready, v):
                dve.wait_ge(src_ready, past(v))
                for t in range(T):
                    dve.bn_stats(st[:, t, :], src[:, t, :]).then_inc(st_ready, 1)

            def aggregate(st, agg, agg_ready):
                for t in range(T):
                    dve.bn_aggr(agg[:, t, :], st[:, t, :]).then_inc(agg_ready, 1)

            def normalise(b, p):
                dve.wait_ge(ln_ready, 6 * b + 2)
                dve.wait_ge(xnl_ready, past(b - 1))
                for t in range(T):
                    dve.tensor_scalar(xn[p][:, t, :], x_in[p][:, t, :], mv[p][:, t, 0:1], ln[p][:, 1, t:t + 1],
                                      ALU.subtract, ALU.mult).then_inc(xn_ready, 1)

            def latent(b, p):
                dve.wait_ge(yln_ready, 5 * b + 5)
                for t in range(T):
                    dve.tensor_scalar(lat[p][:, t, 0:L], qy[p][:, t, D:D + L], ymv[p][:, t, 0:1], yln[p][:, 4, t:t + 1],
                                      ALU.subtract, ALU.mult).then_inc(lat_ready, 1)

            def soft_max(b, p):
                dve.wait_ge(projA_ready, 2 * b + 2)
                dve.tensor_reduce(nqk[p][:, :, :], qkv[p][:, :, 0:2 * D].rearrange("p t (j d) -> p t j d", j=2),
                                  axis=AX.X, op=ALU.max, negate=True).then_inc(nqk_ready, 1)

            def soft_sum(b, p):
                dve.wait_ge(eqk_ready, b + 1)
                dve.tensor_reduce(sqk[p][:, 0, :, :], eqk[p][:, :, :].rearrange("p t (j d) -> p t j d", j=2),
                                  axis=AX.X, op=ALU.add).then_inc(sqk_ready, 1)
                dve.wait_ge(sqk_ready, 2 * b + 1)
                dve.reciprocal(sqk[p][:, 1, :, :], sqk[p][:, 0, :, :]).then_inc(sqk_ready, 1)

            def max_chunk(b, g, c, also=None, v=0):
                if also is not None:
                    dve.wait_ge(also, past(v))
                dve.wait_ge(max_filled, 12 * b + 6 * g + c + 1)
                if c == 0:
                    dve.wait_ge(msplit_ready, past(4 * (2 * b + g - 1)))
                if c < 2:
                    dst, src = nmax[g][:, 4 * c:4 * c + 4, 0], ps_max[c % 2][:, :].rearrange("p (h k) -> p h k", h=4)
                else:
                    dst, src = nmax[g][:, 2 * c - 4:2 * c - 2, 1], ps_max[c % 2][:, :].rearrange("p (h k) -> p h k", h=2)
                dve.tensor_reduce(dst, src, axis=AX.X, op=ALU.max, negate=True).then_inc(max_read, 1)

            def split_max(b, g):
                n = 4 * (2 * b + g)
                nm = nmax[g][:, :, :].rearrange("p h t -> p (h t)")
                dve.wait_ge(max_read, 12 * b + 6 * g + 6)
                dve.wait_ge(mT_filled, past(2 * b + g - 1))
                dve.tensor_copy(nmp[g][:, 0 * HG * T:1 * HG * T], nm).then_inc(msplit_ready, 1)
                dve.wait_ge(msplit_ready, n + 1)
                dve.tensor_tensor(mres[g][:, :], nm, nmp[g][:, 0 * HG * T:1 * HG * T], ALU.subtract).then_inc(msplit_ready, 1)
                dve.wait_ge(msplit_ready, n + 2)
                dve.tensor_copy(nmp[g][:, 1 * HG * T:2 * HG * T], mres[g][:, :]).then_inc(msplit_ready, 1)
                dve.wait_ge(msplit_ready, n + 3)
                dve.tensor_tensor(nmp[g][:, 2 * HG * T:3 * HG * T], mres[g][:, :], nmp[g][:, 1 * HG * T:2 * HG * T], ALU.subtract).then_inc(msplit_ready, 1)

            def pv_norm(b, p, g):
                v = m1[:, 0:T * HG * (HD + 1)].rearrange("p (t h e) -> p t h e", t=T, h=HG)
                dve.wait_ge(pv_filled, 2 * b + g + 1)
                dve.reciprocal(rden[g][:, :, :], v[:, :, :, HD]).then_inc(rden_ready, 1)
                dve.wait_ge(rden_ready, 2 * b + g + 1)
                dve.tensor_tensor(o[p][:, :, g * HG:(g + 1) * HG, :], v[:, :, :, 0:HD], spread(rden[g][:, :, :], HD),
                                  ALU.mult).then_inc(o_ready, 1)

            def residual(b, p):
                dve.wait_ge(wo_filled, b + 1)
                dve.wait_ge(xnl_ready, b + 1)
                dve.wait_ge(acc_ready, past(b - 1))
                dve.tensor_tensor(x1[p][:, :, :], m1[:, 0:S].rearrange("p (t n) -> p t n", t=T), xnl[p][:, :, :],
                                  ALU.add).then_inc(x1_ready, 1)
                stats(x1[p], x1bn[p], x1bn_ready, x1_ready, b + 1)

            def residue1(b, p):
                dve.wait_ge(part1_ready, b + 1)
                dve.tensor_tensor(res[p][:, :], m0[:, :], part[p][:, 0, :], ALU.subtract).then_inc(res1_ready, 1)

            def landmark_out(b, p):
                dve.wait_ge(l0_filled, b + 1)
                dve.wait_ge(sqk_ready, 2 * b + 2)
                for t in range(T):
                    dve.scalar_tensor_tensor(accx[p][:, t, :], m1[:, t * D:(t + 1) * D], sqk[p][:, 1, t, 0:1],
                                             x_in[p][:, t, :], ALU.mult, ALU.add).then_inc(l0_ready, 1)

            def slot0(b, p):
                q = 1 - p
                if there(b, -1):
                    pv_norm(b - 1, q, 1)
                if there(b, 1):
                    soft_max(b + 1, q)
                max_chunk(b, 1, 0)
                if there(b, 2):
                    stats(x_in[p], bn[p], bn_ready, x_loaded, 16 * (b + 3))
                    max_chunk(b, 1, 1, bn_ready, 2 * (b + 3))
                    aggregate(bn[p], mv[p], mv_ready)
                else:
                    max_chunk(b, 1, 1)
                max_chunk(b, 1, 2)
                if there(b, -1):
                    residual(b - 1, q)
                    max_chunk(b, 1, 3, x1bn_ready, 2 * b)
                    aggregate(x1bn[q], x1mv[q], x1mv_ready)
                else:
                    max_chunk(b, 1, 3)
                if there(b, 1):
                    residue1(b + 1, q)
                max_chunk(b, 1, 4)
                if there(b, 2):
                    normalise(b + 2, p)
                max_chunk(b, 1, 5)
                if there(b, 1):
                    soft_sum(b + 1, q)
                split_max(b, 1)

            def slot1(b, p):
                q = 1 - p
                pv_norm(b, p, 0)
                if there(b, 1):
                    for c in range(3):
                        max_chunk(b + 1, 0, c)
                if there(b, 2):
                    stats(qy[p][:, :, D:D + L], ybn[p], ybn_ready, projB_ready, b + 3)
                    max_chunk(b + 1, 0, 3, ybn_ready, 2 * (b + 3))
                    aggregate(ybn[p], ymv[p], ymv_ready)
                    max_chunk(b + 1, 0, 4)
                    latent(b + 2, p)
                elif there(b, 1):
                    max_chunk(b + 1, 0, 3)
                    max_chunk(b + 1, 0, 4)
                if there(b, 1):
                    landmark_out(b + 1, q)
                    max_chunk(b + 1, 0, 5)
                    split_max(b + 1, 0)

            def front(b, p):
                stats(x_in[p], bn[p], bn_ready, x_loaded, 16 * (b + 1))
                dve.wait_ge(bn_ready, 2 * b + 2)
                aggregate(bn[p], mv[p], mv_ready)
                normalise(b, p)

            def back(b, p):
                stats(qy[p][:, :, D:D + L], ybn[p], ybn_ready, projB_ready, b + 1)
                dve.wait_ge(ybn_ready, 2 * b + 2)
                aggregate(ybn[p], ymv[p], ymv_ready)
                latent(b, p)

            def prologue():
                dve.wait_ge(w_loaded, 16 * NW)
                for t_ in vaug:
                    dve.memset(t_[:, :, :, :], 1.0)
                for t_ in kst + qst:
                    dve.memset(t_[64:ROWS, :], 1.0)
                for t_ in lat:
                    dve.memset(t_[:, :, L:P], 1.0)
                for t_ in nmp:
                    dve.memset(t_[:, :], 0.0)
                dve.memset(ones16[:, :], 1.0)
                dve.tensor_copy(ident16[:, :], ident[:, :])
                dve.tensor_copy(mask16[:, :, :], mask_raw[:, :, :])
                dve.tensor_scalar(wb[:, :], wb[:, :], n1w[:, 0:1], None, ALU.mult)
                dve.tensor_scalar(gate[:, :], gate[:, :], n2w[:, 0:1], None, ALU.mult)
                dve.tensor_scalar(w1[:, :, :], w1[:, :, :], n2w[:, 0:1], None, ALU.mult)
                chain = [0]

                def link(ins):
                    chain[0] += 1
                    ins.then_inc(bias_ready_v, 1)
                    dve.wait_ge(bias_ready_v, chain[0])

                link(dve.tensor_copy(bpart[:, 0, :], brow[:, :]))
                link(dve.tensor_tensor(btmp[:, 0, :], brow[:, :], bpart[:, 0, :], ALU.subtract))
                link(dve.tensor_copy(bpart[:, 1, :], btmp[:, 0, :]))
                link(dve.tensor_tensor(bpart[:, 2, :], btmp[:, 0, :], bpart[:, 1, :], ALU.subtract))
                link(dve.tensor_scalar(btmp[:, 0, :], bpart[:, 0, :], part_row[:, 0:1], None, ALU.mult))
                link(dve.scalar_tensor_tensor(btmp[:, 1, :], bpart[:, 1, :], part_row[:, 1:2], btmp[:, 0, :], ALU.mult, ALU.add))
                dve.scalar_tensor_tensor(bias16[:, :], bpart[:, 2, :], part_row[:, 2:3], btmp[:, 1, :], ALU.mult,
                                         ALU.add).then_inc(w_ready, 1)
                front(0, 0)
                dve.wait_ge(bias_ready, 1)
                dve.tensor_scalar(wkv[0:L, :], wkv[0:L, :], ln_g[:, 0:1], None, ALU.mult).then_inc(w_ready, 1)
                back(0, 0)
                soft_max(0, 0)
                front(1, 1)
                residue1(0, 0)
                soft_sum(0, 0)
                back(1, 1)
                landmark_out(0, 0)
                for c in range(6):
                    max_chunk(0, 0, c)
                split_max(0, 0)

            def last():
                pv_norm(B - 1, 1, 1)
                residual(B - 1, 1)
                dve.wait_ge(x1bn_ready, 2 * B)
                aggregate(x1bn[1], x1mv[1], x1mv_ready)

            steps(dve, slot0, slot1, prologue, last)

            def experts(g):
                n = 7 * g
                dve.wait_ge(gate_filled, g + 1)
                dve.tensor_tensor(lg[:, :, :], m0[:, 0:GTILES * E].rearrange("p (t e) -> p t e", e=E),
                                  gate_b[:, :].unsqueeze(1).broadcast_to((P, GTILES, E)), ALU.add).then_inc(top_ready, 1)
                dve.wait_ge(top_ready, n + 1)
                dve.tensor_reduce(lmax[:, :], lg[:, :, :], axis=AX.X, op=ALU.max).then_inc(top_ready, 1)
                dve.wait_ge(top_ready, n + 2)
                dve.tensor_tensor(hit[:, :, :], lg[:, :, :], spread(lmax[:, :], E), ALU.is_ge).then_inc(top_ready, 1)
                dve.wait_ge(top_ready, n + 3)
                dve.tensor_scalar(open_[:, :, 1], hit[:, :, 0], -1.0, 1.0, ALU.mult, ALU.add).then_inc(top_ready, 1)
                for e in (2, 3):
                    dve.wait_ge(top_ready, n + 2 + e)
                    dve.tensor_tensor(open_[:, :, e], open_[:, :, e - 1], hit[:, :, e - 1], ALU.is_gt).then_inc(top_ready, 1)
                dve.wait_ge(top_ready, n + 6)
                dve.tensor_tensor(top[:, :, :], hit[:, :, :], open_[:, :, :], ALU.mult).then_inc(top_ready, 1)
                for k in range(1, E * FC, 2):
                    dve.wait_ge(up_filled, g * E * FC + k + 1)
                    if k == 1:
                        dve.wait_ge(down_filled, g * GTILES)
                    dve.tensor_scalar(hT[k], ps_exp[(k // 2) % 2][:, 1, :], b1c[:, k // FC, k % FC:k % FC + 1], 0.0,
                                      ALU.add, ALU.max).then_inc(relu_v, 1)
                for t in range(GTILES):
                    dve.wait_ge(down_filled, g * GTILES + t + 1)
                    if t == 0:
                        dve.wait_ge(top_ready, n + 7)
                    for e in range(E):
                        if not (t == 0 and e == 0):
                            dve.wait_ge(mix_ready, (g * GTILES + t) * E + e)
                        a = acc_all[:, bass.ds(g * GTILES + t, 1), :].rearrange("p o d -> p (o d)")
                        dve.scalar_tensor_tensor(a, ps_max[t % 2][:, e * D:(e + 1) * D], top[:, t, e:e + 1], a,
                                                 ALU.mult, ALU.add).then_inc(mix_ready, 1)

            dve.wait_ge(acc_ready, B)
            dve.memset(open_[:, :, 0], 1.0)
            experts(0)
            with dve.Fori(1, NG, 1) as g:
                experts(g)

        @block.tensor
        def _(pe):
            def mm(o_, lhsT, rhs, start=True, stop=True):
                return pe.matmul(o_, lhsT, rhs, start=start, stop=stop)

            def xnT_(b, p):
                pe.wait_ge(xn_ready, 2 * b + 2)
                pe.wait_ge(res1_ready, b)
                for t in range(T):
                    ins = pe.transpose(m0[:, t * P:(t + 1) * P], xn[p][:, t, :], ident[:, :])
                ins.then_inc(xnT_filled, 1)

            def projA(b, p, t):
                pe.wait_ge(xnT_ready, b + 1)
                pe.wait_ge(projA_ready, 2 * b + t)
                mm(m0[:, 0:3 * D], xnT[p][:, t * P:(t + 1) * P], wa[:, :], stop=False)
                mm(m0[:, 0:3 * D], ones16[:, :], bias16[:, 0:3 * D], start=False).then_inc(projA_filled, 1)

            def projB(b, p):
                pe.wait_ge(projA_ready, 2 * b + 2)
                for t in range(T):
                    ins = mm(m0[:, t * (D + L):(t + 1) * (D + L)], xnT[p][:, t * P:(t + 1) * P], wb[:, :])
                ins.then_inc(projB_filled, 1)

            def latT_(b, p):
                pe.wait_ge(lat_ready, 2 * b + 2)
                for t in range(T):
                    ins = pe.transpose(m0[:, t * P:(t + 1) * P], lat[p][:, t, :], ident[:, :])
                ins.then_inc(latT_filled, 1)

            def kv(b, p):
                pe.wait_ge(latT_ready, b + 1)
                for t in range(T):
                    ins = mm(m0[:, t * 2 * D:(t + 1) * 2 * D], latT[p][:, t * P:(t + 1) * P], wkv[:, :])
                ins.then_inc(kv_filled, 1)

            def qkT(b, p):
                pe.wait_ge(v_ready, b + 1)
                pe.wait_ge(qrope_ready, 3 * b + 3)
                pe.wait_ge(krope_ready, 2 * b + 2)
                for t in range(T):
                    pe.transpose(m0[:, t * P:(t + 1) * P], qrot[p][:, t, :], ident[:, :])
                for t in range(T):
                    ins = pe.transpose(m0[:, S + t * P:S + (t + 1) * P], krot[p][:, t, :], ident[:, :])
                ins.then_inc(qkT_filled, 1)

            def max_chunk(b, p, g, c):
                n = 12 * b + 6 * g + c
                if c == 0:
                    pe.wait_ge(q_spread, 9 * 16 * (b + 1))
                    pe.wait_ge(k_spread, 9 * 16 * (b + 1))
                pe.wait_ge(max_read, past(n - 1))
                bank = ps_max[c % 2]
                t, nh, h0 = (0, 4, 4 * c) if c < 2 else (1, 2, 2 * c - 4)
                w = 512 // nh
                v = bank[:, :].rearrange("p (h k) -> p h k", h=nh)
                for i in range(nh):
                    col = (g * HG + h0 + i) * S
                    mm(bank[:, i * w:(i + 1) * w], qst[p][0:STACK, col + t * P:col + (t + 1) * P],
                             kst[p][0:STACK, col:col + w], start=(i == 0), stop=False)
                mm(v[:, :, t * P:(t + 1) * P], ident16[:, :], mask16[:, 0:1, :].broadcast_to((P, nh, P)),
                   start=False).then_inc(max_filled, 1)

            def exp_chunk(b, p, g, c):
                n = 6 * b + 3 * g + c
                if c == 0:
                    pe.wait_ge(m_spread, 16 * (2 * b + g + 1))
                pe.wait_ge(exp_ready, past(n - 1))
                bank = ps_exp[(3 * g + c) % 2]
                for a in range(2):
                    kt, nh, h0 = (0, 2, 4 * c + 2 * a) if c < 2 else (1, 4, 4 * a)
                    w = 512 // nh
                    v = bank[:, a, :].rearrange("p (h q) -> p h q", h=nh)
                    for i in range(nh):
                        col = (g * HG + h0 + i) * S
                        mm(bank[:, a, i * w:(i + 1) * w], kst[p][:, col + kt * P:col + (kt + 1) * P],
                                 qst[p][:, col + kt * P:col + S], start=(i == 0), stop=False)
                    ins = mm(v[:, :, 0:P], ident16[:, :], mask16[:, 1:2, :].broadcast_to((P, nh, P)), start=False)
                ins.then_inc(exp_filled, 1)

            def pv(b, p, g, bank_free, v):
                pe.wait_ge(bank_free, past(v))
                pe.wait_ge(exp_ready, 6 * b + 3 * g + 3)
                pe.wait_ge(v_ready, b + 1)
                out_ = m1[:, 0:T * HG * (HD + 1)].rearrange("p (t h e) -> p t h e", t=T, h=HG)
                first = True
                for h in range(HG):
                    for t, kt, col in ((0, 0, 0), (1, 0, P), (1, 1, S)):
                        ins = mm(out_[:, t, h, :], prob[g][:, h, col:col + P], vaug[p][:, kt, g * HG + h, :],
                                 start=first, stop=(h == HG - 1 and col == S))
                        first = False
                ins.then_inc(pv_filled, 1)

            def oT_(b, p):
                pe.wait_ge(o_ready, 2 * b + 2)
                for t in range(T):
                    ins = pe.transpose(m1[:, t * P:(t + 1) * P], o[p][:, t, :, :].rearrange("p h d -> p (h d)"), ident[:, :])
                ins.then_inc(oT_filled, 1)

            def wo_(b, p):
                pe.wait_ge(oT_ready, b + 1)
                for t in range(T):
                    ins = mm(m1[:, t * D:(t + 1) * D], oT[p][:, t * P:(t + 1) * P], wo[:, :])
                ins.then_inc(wo_filled, 1)

            def zT_(b, p):
                pe.wait_ge(z_ready, b + 1)
                for t in range(T):
                    ins = pe.transpose(m1[:, t * P:(t + 1) * P], z[p][:, t, :], ident[:, :])
                ins.then_inc(zT_filled, 1)

            def mT_(b, g, bank_free, v):
                pe.wait_ge(bank_free, past(v))
                pe.wait_ge(msplit_ready, 4 * (2 * b + g + 1))
                pe.transpose(m1h[:, 0:P], nmp[g][:, :], ident16[:, :]).then_inc(mT_filled, 1)

            def eqT_(b, p):
                pe.wait_ge(o_ready, past(2 * b - 1))
                pe.wait_ge(eqk_ready, b + 1)
                for t in range(T):
                    ins = pe.transpose(m1[:, t * P:(t + 1) * P], eqk[p][:, t, 0:D], ident[:, :])
                ins.then_inc(eqT_filled, 1)

            def klC_(b, p):
                pe.wait_ge(eqT_ready, b + 1)
                pe.wait_ge(k3_ready, b + 1)
                for t in range(T):
                    mm(m1[:, 0:D], pool4[:, t, :], kh[p][:, t, :], start=(t == 0), stop=(t == T - 1))
                for t in range(T):
                    ins = mm(m1[:, D:2 * D], kh[p][:, t, :], k3[p][:, t, :], start=(t == 0), stop=(t == T - 1))
                ins.then_inc(klC_filled, 1)

            def gram_(b, p):
                pe.wait_ge(klC_ready, b + 1)
                mm(m1[:, 0:D], klC[p][:, 0:D], klC[p][:, 0:D]).then_inc(gram_filled, 1)

            def mid_(b, p):
                pe.wait_ge(gram_ready, b + 1)
                mm(m1[:, 0:D], gram[p][:, :], klC[p][:, D:2 * D]).then_inc(mid_filled, 1)

            def l0_(b, p):
                pe.wait_ge(mid_ready, b + 1)
                for t in range(T):
                    ins = mm(m1[:, t * D:(t + 1) * D], eqT[p][:, t * P:(t + 1) * P], mid[p][:, :])
                ins.then_inc(l0_filled, 1)

            def slot0(b, p):
                q = 1 - p
                if there(b, -1):
                    pv(b - 1, q, 1, mT_ready, 2 * b + 1)
                max_chunk(b, p, 1, 0)
                max_chunk(b, p, 1, 1)
                exp_chunk(b, p, 0, 0)
                if there(b, 1):
                    kv(b + 1, q)
                if there(b, -1):
                    oT_(b - 1, q)
                max_chunk(b, p, 1, 2)
                exp_chunk(b, p, 0, 1)
                if there(b, -1):
                    wo_(b - 1, q)
                max_chunk(b, p, 1, 3)
                exp_chunk(b, p, 0, 2)
                if there(b, 1):
                    qkT(b + 1, q)
                max_chunk(b, p, 1, 4)
                max_chunk(b, p, 1, 5)
                if there(b, -1):
                    zT_(b - 1, q)
                    mT_(b, 1, zT_ready, b)
                else:
                    mT_(b, 1, mT_ready, 2 * b + 1)

            def slot1(b, p):
                q = 1 - p
                pv(b, p, 0, mT_ready, 2 * b + 2)
                if there(b, 2):
                    xnT_(b + 2, p)
                if there(b, 1):
                    max_chunk(b + 1, q, 0, 0)
                    max_chunk(b + 1, q, 0, 1)
                if there(b, 2):
                    projA(b + 2, p, 0)
                if there(b, 1):
                    eqT_(b + 1, q)
                exp_chunk(b, p, 1, 0)
                if there(b, 2):
                    projA(b + 2, p, 1)
                if there(b, 1):
                    klC_(b + 1, q)
                    max_chunk(b + 1, q, 0, 2)
                exp_chunk(b, p, 1, 1)
                if there(b, 2):
                    projB(b + 2, p)
                if there(b, 1):
                    gram_(b + 1, q)
                    max_chunk(b + 1, q, 0, 3)
                exp_chunk(b, p, 1, 2)
                if there(b, 1):
                    mid_(b + 1, q)
                    max_chunk(b + 1, q, 0, 4)
                    l0_(b + 1, q)
                    max_chunk(b + 1, q, 0, 5)
                if there(b, 2):
                    latT_(b + 2, p)
                if there(b, 1):
                    mT_(b + 1, 0, l0_ready, 2 * (b + 2))

            def front(b, p):
                xnT_(b, p)
                projA(b, p, 0)
                projA(b, p, 1)
                projB(b, p)
                latT_(b, p)

            def prologue():
                pe.wait_ge(w_ready, 1)
                mm(m0[0:L + 1, 0:2 * D], ln_b[:, :], wkv[0:L, :]).then_inc(lnb_filled, 1)
                pe.wait_ge(bias_ready, 1)
                front(0, 0)
                pe.wait_ge(w_ready, 2)
                kv(0, 0)
                qkT(0, 0)
                front(1, 1)
                eqT_(0, 0)
                klC_(0, 0)
                gram_(0, 0)
                mid_(0, 0)
                l0_(0, 0)
                for c in range(6):
                    max_chunk(0, 0, 0, c)
                mT_(0, 0, l0_ready, 2)

            def last():
                pv(B - 1, 1, 1, o_ready, 2 * B - 1)
                oT_(B - 1, 1)
                wo_(B - 1, 1)
                zT_(B - 1, 1)

            steps(pe, slot0, slot1, prologue, last)

            def experts(g, p):
                pe.wait_ge(zg_ready, g + 1)
                pe.wait_ge(top_ready, 7 * g)
                for t in range(GTILES):
                    ins = mm(m0[:, t * E:(t + 1) * E], zg[p][:, t * P:(t + 1) * P], gate[:, :])
                ins.then_inc(gate_filled, 1)
                for n in range(E * FC):
                    k = g * (E * FC // 2) + n // 2 - 1
                    pe.wait_ge((relu_a, relu_v)[n % 2], past(k))
                    mm(ps_exp[(n // 2) % 2][:, n % 2, :], w1[:, n // FC, (n % FC) * P:(n % FC + 1) * P],
                       zg[p]).then_inc(up_filled, 1)
                pe.wait_ge(relu_a, (g + 1) * (E * FC // 2))
                pe.wait_ge(relu_v, (g + 1) * (E * FC // 2))
                for t in range(GTILES):
                    pe.wait_ge(mix_ready, past((g * GTILES + t - 1) * E))
                    bank = ps_max[t % 2]
                    for e in range(E):
                        o_ = bank[:, e * D:(e + 1) * D]
                        for c in range(FC):
                            mm(o_, hT[e * FC + c][:, t * P:(t + 1) * P], w2[:, e, c, :], start=(c == 0), stop=False)
                        ins = mm(o_, ones16[:, :], bias16[:, (3 + e) * D:(4 + e) * D], start=False)
                    ins.then_inc(down_filled, 1)

            experts(0, 0)
            experts(1, 1)
            with pe.Fori(1, NG // 2, 1) as i:
                experts(2 * i, 0)
                experts(2 * i + 1, 1)


def constants():
    f = np.float32
    half = HD // 2
    pos = np.arange(S, dtype=f)[:, None]
    inv = (f(1.0) / f(10000.0) ** (np.arange(half, dtype=f) / f(half))).astype(f)
    ang = (pos * inv[None, :]).astype(f)
    rope = np.zeros((P, 2, 2, T, 64), f)
    for t in range(T):
        for w, fn in ((0, np.cos), (1, np.sin)):
            tab = np.repeat(fn(ang[t * P:(t + 1) * P]).astype(f), H, axis=1)
            rope[:, 0, w, t] = tab * f(1.0 / np.sqrt(HD))
            rope[:, 1, w, t] = tab
    r, c = np.arange(P)[:, None], np.arange(P)[None, :]
    mask = np.stack([np.where(c > r, MASKED, 0.0), np.where(r > c, MASKED, 0.0)], 1).astype(f)
    pool4 = np.zeros((P, T, P), f)
    for t in range(T):
        pool4[np.arange(P), t, (t * P + np.arange(P)) // (S // L)] = L / S
    return {"ident": np.eye(P, dtype=f), "mask": mask, "pool4": pool4, "rope": rope,
            "part_row": np.eye(PARTS, dtype=f)}


def kernel(**inputs):
    import concourse.bacc as _bacc
    from concourse.bass_utils import run_bass_kernel_spmd as _run

    g = {k.replace("L0_", ""): np.asarray(v) for k, v in inputs.items()}
    by_dim = np.arange(D).reshape(H, HD).T.reshape(-1)
    rows = lambda a, n: np.broadcast_to(a.reshape(1, -1), (n, a.size))
    lnb = np.zeros((L, L + 1), np.float32)
    lnb[:, L] = g["ffn_ln_b"]
    a = constants()
    a.update({
        "x": g["attn_hidden_states"],
        "wa": np.concatenate([g["attn_Wq"], g["attn_Wk"], g["attn_Wv"]], 1),
        "wb": np.concatenate([g["ffn_Wq"].T[:, by_dim], g["ffn_Wdkv"].T], 1),
        "wkv": np.concatenate([g["ffn_Wuk"].T[:, by_dim], g["ffn_Wuv"].T], 1),
        "n1w": g["ffn_norm1_w"][:, None], "n2w": g["ffn_norm2_w"][:, None],
        "ln_g": g["ffn_ln_g"][:, None], "ln_b": lnb,
        "wo": g["ffn_Wo"].T, "gate": g["ffn_gate_w"].T, "gate_b": rows(g["ffn_gate_b"], P),
        "w1": g["ffn_W1"].transpose(2, 0, 1),
        "w2": g["ffn_W2"].reshape(E, D, FC, P).transpose(3, 0, 2, 1),
        "b1c": g["ffn_b1"].reshape(E, FC, P).transpose(2, 0, 1),
        "brow": rows(np.concatenate([g["attn_bq"], g["attn_bk"], g["attn_bv"], g["ffn_b2"].reshape(-1)]), PARTS),
    })
    nc = _bacc.Bacc("TRN2", target_bir_lowering=False, num_devices=1)
    arrays, dram = {}, {}
    for n, v in a.items():
        v = np.ascontiguousarray(v)
        arrays[f"in_{n}"] = v
        dram[n] = nc.dram_tensor(f"in_{n}", v.shape, mybir.dt.from_np(v.dtype), kind="ExternalInput").ap()
    out = nc.dram_tensor("out_0", (B, S, D), mybir.dt.float32, kind="ExternalOutput").ap()
    build(nc, dram, out)
    r = _run(nc, [arrays], core_ids=[0])
    return r.results[0]["out_0"]
```

```python
import numpy as np

import concourse.bass as bass
from concourse import mybir
from contextlib import ExitStack

B, S, D = 16, 256, 128
P = 128
T = S // P
H, HD = 16, 8
L = 64
E, F = 4, 512
FC = F // P
PARTS = 3
STACK = PARTS * PARTS * HD
ROWS = STACK + PARTS
HG = H // 2
VW = P // HG
NTOK = B * S
GT = 512
MASKED = -1e38
SAVES = 3 * 16


def build(nc, dram, out):
    f32, bf16 = mybir.dt.float32, mybir.dt.bfloat16
    ALU, ACT, AX = mybir.AluOpType, mybir.ActivationFunctionType, mybir.AxisListType
    ctx = ExitStack()
    with ctx:
        def sb(name, shape, dt=f32):
            return ctx.enter_context(nc.sbuf_tensor(name, shape, dt))

        def two(name, shape, dt=f32):
            return [sb(f"{name}{i}", shape, dt) for i in range(2)]

        def sem(name):
            return ctx.enter_context(nc.semaphore(name))

        def spread(ap, n):
            return ap.unsqueeze(len(ap.shape)).broadcast_to(tuple(ap.shape) + (n,))

        def past(v):
            return max(v, 0) if isinstance(v, int) else v

        ident = sb("ident", [P, P])
        ident16 = sb("ident16", [P, P], bf16)
        mask16 = sb("mask16", [P, 2, P], bf16)
        pool4 = sb("pool4", [P, T, P])
        rope = sb("rope", [P, 2, 2, T, 64])
        wa = sb("wa", [P, 3 * D])
        wb = sb("wb", [P, D + L])
        wkv = sb("wkv", [L + 1, 2 * D])
        ln_g = sb("ln_g", [L, 1])
        ln_b = sb("ln_b", [L, L + 1])
        n1w = sb("n1w", [P, 1])
        n2w = sb("n2w", [P, 1])
        wo = sb("wo", [P, D])
        gate = sb("gate", [P, E])
        gate_b = sb("gate_b", [P, E])
        part_row = sb("part_row", [PARTS, PARTS])
        ones16 = sb("ones16", [PARTS, P], bf16)
        NBIAS = 3 * D + E * D
        bias16 = sb("bias16", [PARTS, NBIAS], bf16)
        b1c = sb("b1c", [P, E, FC])
        zero = sb("zero", [P, 1])
        mhalf = sb("mhalf", [P, T])
        eps5 = sb("eps5", [P, T])
        eps6 = sb("eps6", [P, T])

        x_in = two("x_in", [P, T, D])
        xn = two("xn", [P, T, D])
        xnl = two("xnl", [P, T, D])
        bn = two("bn", [P, T, 6])
        mv = two("mv", [P, T, 2])
        ln = two("ln", [P, 6, T])
        xnT = two("xnT", [P, S])
        qkv = two("qkv", [P, T, 3 * D])
        qy = two("qy", [P, T, D + L])
        ybn = two("ybn", [P, T, 6])
        ymv = two("ymv", [P, T, 2])
        yln = two("yln", [P, 5, T])
        lat = two("lat", [P, T, P])
        latT = two("latT", [L + 1, S])
        kraw = two("kraw", [P, T, D])
        vals = two("vals", [P, T, H, P])
        pvs = two("pvs", [P, S])
        qs = two("qs", [P, T, D])
        ra = two("ra", [P, T, D])
        rb = two("rb", [P, T, D])
        qrot = two("qrot", [P, T, D])
        krot = two("krot", [P, T, D])
        part = two("part", [P, PARTS, 2 * S], bf16)
        res = two("res", [P, 2 * S])
        qst = two("qst", [ROWS, H * S], bf16)
        kst = two("kst", [ROWS, H * S], bf16)
        nmax = two("nmax", [P, HG, T])
        mres = two("mres", [P, HG * T])
        nmp = two("nmp", [P, P], bf16)
        mT = two("mT", [PARTS * HG * T, P], bf16)
        prob = two("prob", [P, HG, S + P])
        early = [t_[:, :, :].rearrange("p h q -> p (h q)") for t_ in prob]
        brow = early[0][0:PARTS, 0:NBIAS]
        btmp = early[0][0:PARTS, NBIAS:3 * NBIAS].rearrange("p (i n) -> p i n", i=2)
        mask_raw = early[1][:, 0:2 * P].rearrange("p (i n) -> p i n", i=2)
        bpart = early[1][0:PARTS, 2 * P:2 * P + PARTS * NBIAS // 2].bitcast(bf16).rearrange("p (i n) -> p i n", i=PARTS)
        rden = two("rden", [P, T, HG])
        o = two("o", [P, T, H, HD])
        oT = two("oT", [P, S])
        x1 = two("x1", [P, T, D])
        x1bn = two("x1bn", [P, T, 6])
        x1mv = two("x1mv", [P, T, 2])
        x1ln = two("x1ln", [P, 4, T])
        z = two("z", [P, T, D])
        nqk = two("nqk", [P, T, 2])
        qks = two("qks", [P, T, 2 * D])
        eqk = two("eqk", [P, T, 2 * D])
        sqk = two("sqk", [P, 2, T, 2])
        kh = two("kh", [P, T, D])
        k3 = two("k3", [P, T, D])
        eqT = two("eqT", [P, S])
        klC = two("klC", [P, 2 * D])
        gram = two("gram", [P, D])
        mid = two("mid", [P, D])
        accx = two("accx", [P, T, D])
        acc_all = sb("acc_all", [P, B * T, D])
        zT_all = sb("zT_all", [P, NTOK])

        NG, GTILES = NTOK // GT, GT // P
        zg = [qkv[i][:, :, :].rearrange("p t n -> p (t n)")[:, 0:GT] for i in range(2)]
        hT = [prob[i][:, :, :].rearrange("p h q -> p (h q)")[:, k * GT:(k + 1) * GT] for i in range(2) for k in range(6)]
        experts_w = vals[0][:, :, :, :].rearrange("p t h n -> p (t h n)")
        w1 = experts_w[:, 0:E * F].rearrange("p (e f) -> p e f", e=E)
        w2 = experts_w[:, E * F:2 * E * F].rearrange("p (e c d) -> p e c d", e=E, c=FC)
        hT += [t_[i][:, :, :].rearrange("p t n -> p (t n)") for t_ in (eqk, qks) for i in range(2)]
        lg = sb("lg", [P, GTILES, E])
        lmax = sb("lmax", [P, GTILES])
        hit = sb("hit", [P, GTILES, E])
        open_ = sb("open_", [P, GTILES, E])
        top = sb("top", [P, GTILES, E])

        ps_max = [ctx.enter_context(nc.psum_tensor(f"ps_max{i}", [P, 512], f32)) for i in range(2)]
        ps_exp = [ctx.enter_context(nc.psum_tensor(f"ps_exp{i}", [P, 512], f32)) for i in range(2)]
        m0 = ctx.enter_context(nc.psum_tensor("m0", [P, 512], f32))
        m1 = ctx.enter_context(nc.psum_tensor("m1", [P, 512], f32))
        m2 = ctx.enter_context(nc.psum_tensor("m2", [P, 512], f32))
        ps_pv = ctx.enter_context(nc.psum_tensor("ps_pv", [P, 512], f32))
        m1h = m1[:, :].bitcast(bf16)

        up_banks = [ps_exp[0], ps_exp[1], m2, ps_pv]

        w_loaded = sem("w_loaded")
        w_ready = sem("w_ready")
        moe_loaded = sem("moe_loaded")
        bias_ready = sem("bias_ready")
        x_loaded = sem("x_loaded")
        bn_ready = sem("bn_ready")
        mv_ready = sem("mv_ready")
        ln_ready = sem("ln_ready")
        xn_ready = sem("xn_ready")
        xnT_filled = sem("xnT_filled")
        xnT_ready = sem("xnT_ready")
        projA_filled = sem("projA_filled")
        projA_ready = sem("projA_ready")
        projB_filled = sem("projB_filled")
        projB_ready = sem("projB_ready")
        ybn_ready = sem("ybn_ready")
        ymv_ready = sem("ymv_ready")
        yln_ready = sem("yln_ready")
        lat_ready = sem("lat_ready")
        latT_filled = sem("latT_filled")
        latT_ready = sem("latT_ready")
        k_filled = sem("k_filled")
        v_filled = sem("v_filled")
        pvs_ready = sem("pvs_ready")
        pvT_filled = sem("pvT_filled")
        k_ready = sem("k_ready")
        v_ready = sem("v_ready")
        qrope_ready = sem("qrope_ready")
        krope_ready = sem("krope_ready")
        qkT_filled = sem("qkT_filled")
        part1_ready = sem("part1_ready")
        res1_ready = sem("res1_ready")
        part2_ready = sem("part2_ready")
        part3_ready = sem("part3_ready")
        qk_saved = sem("qk_saved")
        q_spread = sem("q_spread")
        k_spread = sem("k_spread")
        max_filled = sem("max_filled")
        max_read = sem("max_read")
        msplit_ready = sem("msplit_ready")
        mT_filled = sem("mT_filled")
        mT_ready = sem("mT_ready")
        m_spread = sem("m_spread")
        exp_filled = sem("exp_filled")
        exp_ready = sem("exp_ready")
        pv_filled = sem("pv_filled")
        rden_ready = sem("rden_ready")
        o_ready = sem("o_ready")
        oT_filled = sem("oT_filled")
        oT_ready = sem("oT_ready")
        wo_filled = sem("wo_filled")
        x1_ready = sem("x1_ready")
        x1bn_ready = sem("x1bn_ready")
        x1mv_ready = sem("x1mv_ready")
        x1ln_ready = sem("x1ln_ready")
        z_ready = sem("z_ready")
        acc_ready = sem("acc_ready")
        zT_filled = sem("zT_filled")
        zT_ready = sem("zT_ready")
        nqk_ready = sem("nqk_ready")
        qks_ready = sem("qks_ready")
        eqk_ready = sem("eqk_ready")
        sqk_ready = sem("sqk_ready")
        kh_ready = sem("kh_ready")
        k3_ready = sem("k3_ready")
        eqT_filled = sem("eqT_filled")
        eqT_ready = sem("eqT_ready")
        klC_filled = sem("klC_filled")
        klC_ready = sem("klC_ready")
        gram_filled = sem("gram_filled")
        gram_ready = sem("gram_ready")
        mid_filled = sem("mid_filled")
        mid_ready = sem("mid_ready")
        l0_filled = sem("l0_filled")
        l0_ready = sem("l0_ready")
        xnl_ready = sem("xnl_ready")
        setup = sem("setup")
        out_stored = sem("out_stored")
        bias_ready_v = sem("bias_ready_v")
        lnb_filled = sem("lnb_filled")
        zg_ready = sem("zg_ready")
        gate_filled = sem("gate_filled")
        lg_ready = sem("lg_ready")
        top_ready = sem("top_ready")
        up_filled = sem("up_filled")
        relu_a = sem("relu_a")
        relu_v = sem("relu_v")
        down_filled = sem("down_filled")
        mix_ready = sem("mix_ready")

        NW = 17
        block = ctx.enter_context(nc.Block())

        def steps(eng, step, prologue, last):
            prologue()
            for b in (0, 1):
                step(b, b % 2)
            with eng.Fori(1, B // 2 - 1, 1) as i:
                for k in (0, 1):
                    b = 2 * i + k
                    step(b, k)
            for b in (B - 2, B - 1):
                step(b, b % 2)
            last()

        def there(b, ahead):
            return not isinstance(b, int) or 0 <= b + ahead < B

        @block.sync
        def _(sp):
            pairs = [(ident, "ident"), (mask_raw, "mask"), (pool4, "pool4"), (rope, "rope"), (wa, "wa"), (wb, "wb"),
                     (n1w, "n1w"), (n2w, "n2w"), (wo, "wo"), (gate, "gate"), (gate_b, "gate_b"),
                     (part_row, "part_row"), (brow, "brow"), (b1c, "b1c"), (ln_g, "ln_g"), (ln_b, "ln_b")]

            def load_x(b, p):
                sp.wait_ge(l0_ready, past(2 * (b - 1)))
                sp.dma_start(x_in[p][:, :, :], dram["x"][bass.ds(b, 1)].rearrange("o (t p) d -> p (o t) d", p=P)
                             if not isinstance(b, int) else dram["x"][b].rearrange("(t p) d -> p t d", p=P)
                             ).then_inc(x_loaded, 16)

            def spread_qk(b, p):
                sp.wait_ge(part3_ready, b + 1)
                to_rows = "i (r t) -> r i t"
                sp.dma_start(dram["q_parts"][p, 0:PARTS].rearrange(to_rows, t=S), part[p][:, :, 0:S]).then_inc(qk_saved, 16)
                sp.dma_start(dram["q_parts"][p, PARTS:2 * PARTS - 1].rearrange(to_rows, t=S),
                             part[p][:, 0:PARTS - 1, 0:S]).then_inc(qk_saved, 16)
                sp.dma_start(dram["k_parts"][p].rearrange(to_rows, t=S), part[p][:, :, S:2 * S]).then_inc(qk_saved, 16)
                sp.wait_ge(qk_saved, SAVES * (b + 1))
                for a in range(PARTS):
                    to = slice(PARTS * HD * a, PARTS * HD * (a + 1))
                    sp.dma_start(qst[p][to, :], dram["q_parts"][p, a:a + PARTS].rearrange("i (d n) -> (i d) n", d=HD)
                                 ).then_inc(q_spread, 16)
                    sp.dma_start(kst[p][to, :], dram["k_parts"][p].rearrange("i (d n) -> (i d) n", d=HD)
                                 ).then_inc(k_spread, 16)

            def spread_m(b, p, g):
                sp.wait_ge(mT_ready, 2 * b + g + 1)
                sp.dma_start(qst[p][STACK:ROWS, g * HG * S:(g + 1) * HG * S], mT[g][:, :]).then_inc(m_spread, 16)

            def prologue():
                load_x(0, 0)
                load_x(1, 1)
                for t, n in pairs:
                    sp.dma_start(t[tuple(slice(None) for _ in t.shape)], dram[n]).then_inc(w_loaded, 16)
                sp.dma_start(wkv[0:L, :], dram["wkv"]).then_inc(w_loaded, 16)
                spread_qk(0, 0)

            def step(b, p):
                if there(b, 2):
                    load_x(b + 2, p)
                if there(b, 1):
                    spread_qk(b + 1, 1 - p)
                spread_m(b, p, 0)
                spread_m(b, p, 1)

            def last():
                sp.wait_ge(pv_filled, 2 * B - 2)
                sp.dma_start(w1, dram["w1"]).then_inc(moe_loaded, 16)
                sp.dma_start(w2, dram["w2"]).then_inc(moe_loaded, 16)

            steps(sp, step, prologue, last)
            out_t = out.rearrange("b (t p) d -> p (b t) d", p=P)
            with sp.Fori(0, NG, 1) as g:
                sp.wait_ge(mix_ready, (g + 1) * GTILES * E)
                sp.dma_start(out_t[:, bass.ds(g * GTILES, GTILES), :],
                             acc_all[:, bass.ds(g * GTILES, GTILES), :]).then_inc(out_stored, 16)
            sp.wait_ge(out_stored, 16 * NG)

        @block.gpsimd
        def _(pool):
            def tt(o_, a, c, op):
                return pool.tensor_tensor(o_, a, c, op)

            def layer_norm(b, p):
                n = 6 * b
                pool.wait_ge(mv_ready, 2 * b + 2)
                tt(ln[p][:, 0], mv[p][:, :, 1], eps5[:, :], ALU.add).then_inc(ln_ready, 1)
                pool.wait_ge(ln_ready, n + 1)
                tt(ln[p][:, 1], ln[p][:, 0], mhalf[:, :], ALU.pow).then_inc(ln_ready, 1)
                pool.wait_ge(ln_ready, n + 2)
                tt(ln[p][:, 2], mv[p][:, :, 1], ln[p][:, 1], ALU.mult).then_inc(ln_ready, 1)
                pool.wait_ge(ln_ready, n + 3)
                tt(ln[p][:, 3], ln[p][:, 2], ln[p][:, 1], ALU.mult).then_inc(ln_ready, 1)
                pool.wait_ge(ln_ready, n + 4)
                tt(ln[p][:, 4], ln[p][:, 3], eps6[:, :], ALU.add).then_inc(ln_ready, 1)
                pool.wait_ge(ln_ready, n + 5)
                tt(ln[p][:, 5], ln[p][:, 4], mhalf[:, :], ALU.pow).then_inc(ln_ready, 1)

            def latent_scale(b, p):
                n = 5 * b
                pool.wait_ge(ln_ready, 6 * b + 6)
                tt(yln[p][:, 0], ln[p][:, 5], ln[p][:, 5], ALU.mult).then_inc(yln_ready, 1)
                pool.wait_ge(yln_ready, n + 1)
                pool.wait_ge(ymv_ready, 2 * b + 2)
                tt(yln[p][:, 1], yln[p][:, 0], ymv[p][:, :, 1], ALU.mult).then_inc(yln_ready, 1)
                pool.wait_ge(yln_ready, n + 2)
                tt(yln[p][:, 2], yln[p][:, 1], eps5[:, :], ALU.add).then_inc(yln_ready, 1)
                pool.wait_ge(yln_ready, n + 3)
                tt(yln[p][:, 3], yln[p][:, 2], mhalf[:, :], ALU.pow).then_inc(yln_ready, 1)
                pool.wait_ge(yln_ready, n + 4)
                tt(yln[p][:, 4], yln[p][:, 3], ln[p][:, 5], ALU.mult).then_inc(yln_ready, 1)

            def rotate(src, dst, which, ready, n, p):
                c = rope[:, which, 0, :, :].unsqueeze(2).broadcast_to((P, T, 2, 64))
                v = src[:, :, :].rearrange("p t (a c) -> p t a c", a=2)
                w = rb[p][:, :, :].rearrange("p t (a c) -> p t a c", a=2)
                tt(ra[p][:, :, :].rearrange("p t (a c) -> p t a c", a=2), v, c, ALU.mult)
                tt(w[:, :, 1, :], v[:, :, 0, :], rope[:, which, 1, :, :], ALU.mult)
                tt(w[:, :, 0, :], v[:, :, 1, :], rope[:, which, 1, :, :], ALU.mult).then_inc(ready, 1)
                pool.wait_ge(ready, n)
                d = dst[:, :, :].rearrange("p t (a c) -> p t a c", a=2)
                u = ra[p][:, :, :].rearrange("p t (a c) -> p t a c", a=2)
                tt(d[:, :, 0, :], u[:, :, 0, :], w[:, :, 0, :], ALU.subtract)
                tt(d[:, :, 1, :], u[:, :, 1, :], w[:, :, 1, :], ALU.add).then_inc(ready, 1)

            def rope_q(b, p):
                pool.wait_ge(projB_ready, b + 1)
                pool.wait_ge(qkT_filled, past(b - 1))
                tt(qs[p][:, :, :], qy[p][:, :, 0:D], spread(ln[p][:, 5], D), ALU.mult).then_inc(qrope_ready, 1)
                pool.wait_ge(qrope_ready, 3 * b + 1)
                rotate(qs[p], qrot[p], 0, qrope_ready, 3 * b + 2, p)

            def rope_k(b, p):
                pool.wait_ge(k_ready, b + 1)
                pool.wait_ge(qrope_ready, 3 * b + 3)
                rotate(kraw[p], krot[p], 1, krope_ready, 2 * b + 1, p)

            def parts(b, p):
                pool.wait_ge(res1_ready, b + 1)
                pool.wait_ge(qk_saved, past(SAVES * (b - 1)))
                tt(part[p][:, 1, :], res[p][:, :], zero[:, 0:1].broadcast_to((P, 2 * S)), ALU.add).then_inc(part2_ready, 1)
                pool.wait_ge(part2_ready, b + 1)
                pool.wait_ge(exp_filled, past(12 * (b - 1)))
                tt(part[p][:, 2, :], res[p][:, :], part[p][:, 1, :], ALU.subtract).then_inc(part3_ready, 1)

            def soft_shift(b, p):
                pool.wait_ge(nqk_ready, b + 1)
                v = lambda t_, w_: t_[:, :, 0:2 * D].rearrange("p t (j d) -> p t j d", j=2)
                tt(v(qks[p], 0), v(qkv[p], 0), spread(nqk[p][:, :, :], D), ALU.add).then_inc(qks_ready, 1)

            def soft_k(b, p):
                pool.wait_ge(sqk_ready, 2 * b + 2)
                tt(kh[p][:, :, :], eqk[p][:, :, D:2 * D], spread(sqk[p][:, 1, :, 1], D), ALU.mult).then_inc(kh_ready, 1)
                pool.wait_ge(kh_ready, b + 1)
                tt(k3[p][:, :, :], kh[p][:, :, :], qkv[p][:, :, 2 * D:3 * D], ALU.mult).then_inc(k3_ready, 1)

            def late_xn(b, p):
                pool.wait_ge(x1_ready, past(b - 1))
                pool.wait_ge(xn_ready, 2 * b + 2)
                tt(xnl[p][:, :, :], xn[p][:, :, :], zero[:, 0:1].unsqueeze(2).broadcast_to((P, T, D)), ALU.add).then_inc(xnl_ready, 1)

            def finish(b, p):
                n = 4 * b
                pool.wait_ge(x1mv_ready, 2 * b + 2)
                tt(x1ln[p][:, 0], x1mv[p][:, :, 0], x1mv[p][:, :, 0], ALU.mult).then_inc(x1ln_ready, 1)
                pool.wait_ge(x1ln_ready, n + 1)
                tt(x1ln[p][:, 1], x1ln[p][:, 0], x1mv[p][:, :, 1], ALU.add).then_inc(x1ln_ready, 1)
                pool.wait_ge(x1ln_ready, n + 2)
                tt(x1ln[p][:, 2], x1ln[p][:, 1], eps6[:, :], ALU.add).then_inc(x1ln_ready, 1)
                pool.wait_ge(x1ln_ready, n + 3)
                tt(x1ln[p][:, 3], x1ln[p][:, 2], mhalf[:, :], ALU.pow).then_inc(x1ln_ready, 1)
                pool.wait_ge(x1ln_ready, n + 4)
                tt(z[p][:, :, :], x1[p][:, :, :], spread(x1ln[p][:, 3], D), ALU.mult).then_inc(z_ready, 1)
                pool.wait_ge(l0_ready, 2 * b + 2)
                tt(acc_all[:, bass.ds(b * T, T), :], accx[p][:, :, :], x1[p][:, :, :], ALU.add).then_inc(acc_ready, 1)

            def step(b, p):
                q = 1 - p
                if there(b, 2):
                    layer_norm(b + 2, p)
                if there(b, 1):
                    parts(b + 1, q)
                    soft_k(b + 1, q)
                if there(b, -1):
                    finish(b - 1, q)
                if there(b, 2):
                    latent_scale(b + 2, p)
                    rope_q(b + 2, p)
                    soft_shift(b + 2, p)
                if there(b, 1):
                    late_xn(b + 1, q)
                if there(b, 2):
                    rope_k(b + 2, p)

            def prologue():
                for t_, v in ((zero, 0.0), (mhalf, -0.5), (eps5, 1e-5), (eps6, 1e-6)):
                    pool.memset(t_[:, :], v).then_inc(setup, 1)
                for i in range(2):
                    pool.wait_ge(setup, 4 + i)
                    pool.memset(kst[i][64:ROWS, :], 1.0).then_inc(setup, 1)
                for i in range(2):
                    pool.wait_ge(setup, 6 + i)
                    pool.memset(vals[i][:, :, :, :], 0.0).then_inc(setup, 1)
                pool.wait_ge(setup, 8)
                for t_ in vals:
                    for g in range(2):
                        a = t_[:, :, g * HG:(g + 1) * HG, :]
                        ones_at = bass.AP(tensor=a.tensor, offset=a.offset + HD,
                                          ap=[list(a.ap[0]), [H * P, T], [P + VW, HG], [1, 1]])
                        pool.memset(ones_at, 1.0).then_inc(setup, 1)
                pool.wait_ge(w_loaded, 16 * NW)
                layer_norm(0, 0)
                latent_scale(0, 0)
                rope_q(0, 0)
                soft_shift(0, 0)
                layer_norm(1, 1)
                rope_k(0, 0)
                parts(0, 0)
                soft_k(0, 0)
                late_xn(0, 0)
                latent_scale(1, 1)
                rope_q(1, 1)
                soft_shift(1, 1)
                rope_k(1, 1)

            def last():
                finish(B - 1, 1)

            steps(pool, step, prologue, last)

        @block.scalar
        def _(act):
            def copy(dst, src, scale=1.0):
                return act.activation(dst, src, ACT.Copy, scale=scale)

            def k_copy(b, p):
                act.wait_ge(k_filled, b + 1)
                act.wait_ge(krope_ready, past(2 * (b - 1)))
                copy(kraw[p][:, :, :], m0[:, 0:S].rearrange("p (t n) -> p t n", t=T)).then_inc(k_ready, 1)

            def v_copy(b, p):
                act.wait_ge(v_filled, b + 1)
                act.wait_ge(pv_filled, past(2 * (b - 1)))
                for t in range(T):
                    for g in range(2):
                        a = vals[p][:, t, g * HG:(g + 1) * HG, :]
                        dst = bass.AP(tensor=a.tensor, offset=a.offset, ap=[list(a.ap[0]), [P + VW, HG], [1, HD]])
                        ins = copy(dst, m1[:, t * D + g * D // 2:t * D + (g + 1) * D // 2].rearrange("p (h d) -> p h d", d=HD))
                ins.then_inc(v_ready, 1)

            def part1(b, p):
                act.wait_ge(qkT_filled, b + 1)
                act.wait_ge(qk_saved, past(SAVES * (b - 1)))
                copy(part[p][:, 0, :], m0[:, :]).then_inc(part1_ready, 1)

            def evac(b, filled, ready, dst, src, n=1, k=0, scale=1.0):
                act.wait_ge(filled, n * b + k + 1)
                copy(dst, src, scale).then_inc(ready, 1)

            def exp_chunk(b, p, g, c):
                act.wait_ge(exp_filled, 12 * b + 6 * g + c + 1)
                if c == 0:
                    act.wait_ge(pv_filled, past(2 * (b - 1) + g + 1))
                bank = ps_exp[c % 2]
                if c < 4:
                    dst, src = prob[g][:, 2 * c:2 * c + 2, 0:S], bank[:, :].rearrange("p (h q) -> p h q", h=2)
                else:
                    dst, src = prob[g][:, 4 * c - 16:4 * c - 12, S:S + P], bank[:, :].rearrange("p (h q) -> p h q", h=4)
                act.activation(dst, src, ACT.Exp).then_inc(exp_ready, 1)

            def pv_copy(b, g):
                act.wait_ge(pv_filled, 2 * b + g + 1)
                act.wait_ge(pvT_filled, past(2 * b + g - 1))
                copy(pvs[g][:, :], ps_pv[:, 0:S]).then_inc(pvs_ready, 1)

            def soft_exp(b, p):
                act.wait_ge(qks_ready, b + 1)
                act.activation(eqk[p][:, :, :], qks[p][:, :, :], ACT.Exp).then_inc(eqk_ready, 1)

            def step(b, p):
                q = 1 - p
                if there(b, 1):
                    soft_exp(b + 1, q)
                    part1(b + 1, q)
                    v_copy(b + 1, q)
                if there(b, 2):
                    evac(b + 2, xnT_filled, xnT_ready, xnT[p][:, :], m0[:, 0:S])
                if there(b, -1):
                    pv_copy(b - 1, 1)
                evac(b, mT_filled, mT_ready, mT[0][:, :], m1h[0:PARTS * HG * T, 0:P], 2, 0)
                if there(b, 2):
                    evac(b + 2, projA_filled, projA_ready, qkv[p][:, 0, :], m0[:, 0:3 * D], 2, 0)
                if there(b, -1):
                    evac(b - 1, oT_filled, oT_ready, oT[q][:, :], m2[:, 0:S])
                if there(b, 2):
                    evac(b + 2, projA_filled, projA_ready, qkv[p][:, 1, :], m0[:, 0:3 * D], 2, 1)
                    evac(b + 2, projB_filled, projB_ready, qy[p][:, :, :],
                         m0[:, 0:T * (D + L)].rearrange("p (t n) -> p t n", t=T))
                exp_chunk(b, p, 0, 0)
                evac(b, mT_filled, mT_ready, mT[1][:, :], m1h[0:PARTS * HG * T, 0:P], 2, 1)
                exp_chunk(b, p, 0, 1)
                if there(b, 1):
                    evac(b + 1, eqT_filled, eqT_ready, eqT[q][:, :], m1[:, 0:S])
                exp_chunk(b, p, 0, 2)
                if there(b, 1):
                    evac(b + 1, klC_filled, klC_ready, klC[q][:, :], m1[:, 0:2 * D])
                exp_chunk(b, p, 0, 3)
                if there(b, 1):
                    evac(b + 1, gram_filled, gram_ready, gram[q][:, :], m1[:, 0:D])
                if there(b, -1):
                    evac(b - 1, zT_filled, zT_ready, zT_all[:, bass.ds((b - 1) * S, S)], m2[:, 0:S],
                         scale=n2w[:, 0:1])
                exp_chunk(b, p, 0, 4)
                if there(b, 1):
                    evac(b + 1, mid_filled, mid_ready, mid[q][:, :], m1[:, 0:D])
                exp_chunk(b, p, 0, 5)
                if there(b, 2):
                    evac(b + 2, latT_filled, latT_ready, latT[p][:, :], m0[0:L + 1, 0:S])
                exp_chunk(b, p, 1, 0)
                exp_chunk(b, p, 1, 1)
                if there(b, 2):
                    k_copy(b + 2, p)
                for c in range(2, 6):
                    exp_chunk(b, p, 1, c)
                pv_copy(b, 0)

            def front(b, p):
                evac(b, xnT_filled, xnT_ready, xnT[p][:, :], m0[:, 0:S])
                for t in range(T):
                    evac(b, projA_filled, projA_ready, qkv[p][:, t, :], m0[:, 0:3 * D], 2, t)
                evac(b, projB_filled, projB_ready, qy[p][:, :, :], m0[:, 0:T * (D + L)].rearrange("p (t n) -> p t n", t=T))
                evac(b, latT_filled, latT_ready, latT[p][:, :], m0[0:L + 1, 0:S])

            def prologue():
                act.wait_ge(lnb_filled, 1)
                copy(wkv[L:L + 1, :], m0[L:L + 1, 0:2 * D]).then_inc(bias_ready, 1)
                front(0, 0)
                k_copy(0, 0)
                v_copy(0, 0)
                soft_exp(0, 0)
                part1(0, 0)
                front(1, 1)
                k_copy(1, 1)
                evac(0, eqT_filled, eqT_ready, eqT[0][:, :], m1[:, 0:S])
                evac(0, klC_filled, klC_ready, klC[0][:, :], m1[:, 0:2 * D])
                evac(0, gram_filled, gram_ready, gram[0][:, :], m1[:, 0:D])
                evac(0, mid_filled, mid_ready, mid[0][:, :], m1[:, 0:D])

            def last():
                pv_copy(B - 1, 1)
                evac(B - 1, oT_filled, oT_ready, oT[1][:, :], m2[:, 0:S])
                evac(B - 1, zT_filled, zT_ready, zT_all[:, (B - 1) * S:B * S], m2[:, 0:S],
                     scale=n2w[:, 0:1])

            steps(act, step, prologue, last)

            def experts(g, p):
                act.wait_ge(zT_ready, B)
                act.wait_ge(up_filled, past((g - 1) * E * FC))
                copy(zg[p], zT_all[:, bass.ds(g * GT, GT)]).then_inc(zg_ready, 1)
                for n in range(0, E * FC, 2):
                    act.wait_ge(up_filled, g * E * FC + n + 1)
                    if n == 0:
                        act.wait_ge(down_filled, g * GTILES)
                    act.activation(hT[n], up_banks[n % 4][:, :], ACT.Relu,
                                   bias=b1c[:, n // FC, n % FC:n % FC + 1]).then_inc(relu_a, 1)

            experts(0, 0)
            experts(1, 1)
            with act.Fori(1, NG // 2, 1) as i:
                experts(2 * i, 0)
                experts(2 * i + 1, 1)

        @block.vector
        def _(dve):
            def stats(src, st, st_ready, src_ready, v):
                dve.wait_ge(src_ready, past(v))
                for t in range(T):
                    dve.bn_stats(st[:, t, :], src[:, t, :]).then_inc(st_ready, 1)

            def aggregate(st, agg, agg_ready):
                for t in range(T):
                    dve.bn_aggr(agg[:, t, :], st[:, t, :]).then_inc(agg_ready, 1)

            def normalise(b, p):
                dve.wait_ge(ln_ready, 6 * b + 2)
                dve.wait_ge(xnl_ready, past(b - 1))
                for t in range(T):
                    dve.tensor_scalar(xn[p][:, t, :], x_in[p][:, t, :], mv[p][:, t, 0:1], ln[p][:, 1, t:t + 1],
                                      ALU.subtract, ALU.mult).then_inc(xn_ready, 1)

            def latent(b, p):
                dve.wait_ge(yln_ready, 5 * b + 5)
                for t in range(T):
                    dve.tensor_scalar(lat[p][:, t, 0:L], qy[p][:, t, D:D + L], ymv[p][:, t, 0:1], yln[p][:, 4, t:t + 1],
                                      ALU.subtract, ALU.mult).then_inc(lat_ready, 1)

            def soft_max(b, p):
                dve.wait_ge(ybn_ready, past(2 * b + 2))
                dve.wait_ge(projA_ready, 2 * b + 2)
                dve.tensor_reduce(nqk[p][:, :, :], qkv[p][:, :, 0:2 * D].rearrange("p t (j d) -> p t j d", j=2),
                                  axis=AX.X, op=ALU.max, negate=True).then_inc(nqk_ready, 1)

            def soft_sum(b, p):
                dve.wait_ge(eqk_ready, b + 1)
                dve.tensor_reduce(sqk[p][:, 0, :, :], eqk[p][:, :, :].rearrange("p t (j d) -> p t j d", j=2),
                                  axis=AX.X, op=ALU.add).then_inc(sqk_ready, 1)
                dve.wait_ge(sqk_ready, 2 * b + 1)
                dve.reciprocal(sqk[p][:, 1, :, :], sqk[p][:, 0, :, :]).then_inc(sqk_ready, 1)

            def max_chunk(b, g, c, also=None, v=0):
                if also is not None:
                    dve.wait_ge(also, past(v))
                dve.wait_ge(max_filled, 12 * b + 6 * g + c + 1)
                if c == 0:
                    dve.wait_ge(msplit_ready, past(4 * (2 * b + g - 1)))
                if c < 2:
                    dst, src = nmax[g][:, 4 * c:4 * c + 4, 0], ps_max[c % 2][:, :].rearrange("p (h k) -> p h k", h=4)
                else:
                    dst, src = nmax[g][:, 2 * c - 4:2 * c - 2, 1], ps_max[c % 2][:, :].rearrange("p (h k) -> p h k", h=2)
                dve.tensor_reduce(dst, src, axis=AX.X, op=ALU.max, negate=True).then_inc(max_read, 1)

            def split_max(b, g):
                n = 4 * (2 * b + g)
                nm = nmax[g][:, :, :].rearrange("p h t -> p (h t)")
                dve.wait_ge(max_read, 12 * b + 6 * g + 6)
                dve.wait_ge(mT_filled, past(2 * b + g - 1))
                dve.tensor_copy(nmp[g][:, 0 * HG * T:1 * HG * T], nm).then_inc(msplit_ready, 1)
                dve.wait_ge(msplit_ready, n + 1)
                dve.tensor_tensor(mres[g][:, :], nm, nmp[g][:, 0 * HG * T:1 * HG * T], ALU.subtract).then_inc(msplit_ready, 1)
                dve.wait_ge(msplit_ready, n + 2)
                dve.tensor_copy(nmp[g][:, 1 * HG * T:2 * HG * T], mres[g][:, :]).then_inc(msplit_ready, 1)
                dve.wait_ge(msplit_ready, n + 3)
                dve.tensor_tensor(nmp[g][:, 2 * HG * T:3 * HG * T], mres[g][:, :], nmp[g][:, 1 * HG * T:2 * HG * T], ALU.subtract).then_inc(msplit_ready, 1)

            def pv_norm(b, p, g):
                v = m2[:, 0:S].rearrange("p (t h e) -> p t h e", t=T, h=HG)
                dve.wait_ge(pvT_filled, 2 * b + g + 1)
                dve.reciprocal(rden[g][:, :, :], v[:, :, :, HD]).then_inc(rden_ready, 1)
                dve.wait_ge(rden_ready, 2 * b + g + 1)
                dve.tensor_tensor(o[p][:, :, g * HG:(g + 1) * HG, :], v[:, :, :, 0:HD], spread(rden[g][:, :, :], HD),
                                  ALU.mult).then_inc(o_ready, 1)

            def residual(b, p):
                dve.wait_ge(wo_filled, b + 1)
                dve.wait_ge(xnl_ready, b + 1)
                dve.wait_ge(acc_ready, past(b - 1))
                dve.tensor_tensor(x1[p][:, :, :], m2[:, 0:S].rearrange("p (t n) -> p t n", t=T), xnl[p][:, :, :],
                                  ALU.add).then_inc(x1_ready, 1)
                stats(x1[p], x1bn[p], x1bn_ready, x1_ready, b + 1)

            def residue1(b, p):
                dve.wait_ge(part1_ready, b + 1)
                dve.tensor_tensor(res[p][:, :], m0[:, :], part[p][:, 0, :], ALU.subtract).then_inc(res1_ready, 1)

            def landmark_out(b, p):
                dve.wait_ge(l0_filled, b + 1)
                dve.wait_ge(sqk_ready, 2 * b + 2)
                dve.wait_ge(acc_ready, past(b - 1))
                for t in range(T):
                    dve.scalar_tensor_tensor(accx[p][:, t, :], m1[:, t * D:(t + 1) * D], sqk[p][:, 1, t, 0:1],
                                             x_in[p][:, t, :], ALU.mult, ALU.add).then_inc(l0_ready, 1)

            def step(b, p):
                q = 1 - p
                max_chunk(b, 0, 0)
                if there(b, 2):
                    stats(x_in[p], bn[p], bn_ready, x_loaded, 16 * (b + 3))
                    max_chunk(b, 0, 1, bn_ready, 2 * (b + 3))
                    aggregate(bn[p], mv[p], mv_ready)
                else:
                    max_chunk(b, 0, 1)
                if there(b, 1):
                    residue1(b + 1, q)
                for c in range(2, 6):
                    max_chunk(b, 0, c)
                split_max(b, 0)
                if there(b, 2):
                    normalise(b + 2, p)
                max_chunk(b, 1, 0)
                max_chunk(b, 1, 1)
                max_chunk(b, 1, 2)
                if there(b, 1):
                    soft_sum(b + 1, q)
                if there(b, -1):
                    pv_norm(b - 1, q, 1)
                max_chunk(b, 1, 3)
                max_chunk(b, 1, 4)
                if there(b, -1):
                    residual(b - 1, q)
                    max_chunk(b, 1, 5, x1bn_ready, 2 * b)
                    aggregate(x1bn[q], x1mv[q], x1mv_ready)
                else:
                    max_chunk(b, 1, 5)
                split_max(b, 1)
                if there(b, 2):
                    stats(qy[p][:, :, D:D + L], ybn[p], ybn_ready, projB_ready, b + 3)
                    soft_max(b + 2, p)
                    aggregate(ybn[p], ymv[p], ymv_ready)
                    latent(b + 2, p)
                if there(b, 1):
                    landmark_out(b + 1, q)
                pv_norm(b, p, 0)

            def front(b, p):
                stats(x_in[p], bn[p], bn_ready, x_loaded, 16 * (b + 1))
                dve.wait_ge(bn_ready, 2 * b + 2)
                aggregate(bn[p], mv[p], mv_ready)
                normalise(b, p)

            def back(b, p):
                stats(qy[p][:, :, D:D + L], ybn[p], ybn_ready, projB_ready, b + 1)
                dve.wait_ge(ybn_ready, 2 * b + 2)
                aggregate(ybn[p], ymv[p], ymv_ready)
                latent(b, p)

            def prologue():
                dve.wait_ge(w_loaded, 16 * NW)
                for t_ in lat:
                    dve.memset(t_[:, :, L:P], 1.0)
                for t_ in nmp:
                    dve.memset(t_[:, :], 0.0)
                dve.memset(ones16[:, :], 1.0)
                dve.tensor_copy(ident16[:, :], ident[:, :])
                dve.tensor_copy(mask16[:, :, :], mask_raw[:, :, :])
                dve.tensor_scalar(wb[:, :], wb[:, :], n1w[:, 0:1], None, ALU.mult)
                chain = [0]

                def link(ins):
                    chain[0] += 1
                    ins.then_inc(bias_ready_v, 1)
                    dve.wait_ge(bias_ready_v, chain[0])

                link(dve.tensor_copy(bpart[:, 0, :], brow[:, :]))
                link(dve.tensor_tensor(btmp[:, 0, :], brow[:, :], bpart[:, 0, :], ALU.subtract))
                link(dve.tensor_copy(bpart[:, 1, :], btmp[:, 0, :]))
                link(dve.tensor_tensor(bpart[:, 2, :], btmp[:, 0, :], bpart[:, 1, :], ALU.subtract))
                link(dve.tensor_scalar(btmp[:, 0, :], bpart[:, 0, :], part_row[:, 0:1], None, ALU.mult))
                link(dve.scalar_tensor_tensor(btmp[:, 1, :], bpart[:, 1, :], part_row[:, 1:2], btmp[:, 0, :], ALU.mult, ALU.add))
                dve.scalar_tensor_tensor(bias16[:, :], bpart[:, 2, :], part_row[:, 2:3], btmp[:, 1, :], ALU.mult,
                                         ALU.add).then_inc(w_ready, 1)
                front(0, 0)
                dve.wait_ge(bias_ready, 1)
                dve.tensor_scalar(wkv[0:L, :], wkv[0:L, :], ln_g[:, 0:1], None, ALU.mult).then_inc(w_ready, 1)
                back(0, 0)
                soft_max(0, 0)
                front(1, 1)
                residue1(0, 0)
                soft_sum(0, 0)
                back(1, 1)
                soft_max(1, 1)
                landmark_out(0, 0)

            def last():
                pv_norm(B - 1, 1, 1)
                residual(B - 1, 1)
                dve.wait_ge(x1bn_ready, 2 * B)
                aggregate(x1bn[1], x1mv[1], x1mv_ready)

            steps(dve, step, prologue, last)

            def experts(g):
                n = 7 * g
                dve.wait_ge(gate_filled, g + 1)
                dve.tensor_tensor(lg[:, :, :], m0[:, 0:GTILES * E].rearrange("p (t e) -> p t e", e=E),
                                  gate_b[:, :].unsqueeze(1).broadcast_to((P, GTILES, E)), ALU.add).then_inc(top_ready, 1)
                dve.wait_ge(top_ready, n + 1)
                dve.tensor_reduce(lmax[:, :], lg[:, :, :], axis=AX.X, op=ALU.max).then_inc(top_ready, 1)
                dve.wait_ge(top_ready, n + 2)
                dve.tensor_tensor(hit[:, :, :], lg[:, :, :], spread(lmax[:, :], E), ALU.is_ge).then_inc(top_ready, 1)
                dve.wait_ge(top_ready, n + 3)
                dve.tensor_scalar(open_[:, :, 1], hit[:, :, 0], -1.0, 1.0, ALU.mult, ALU.add).then_inc(top_ready, 1)
                for e in (2, 3):
                    dve.wait_ge(top_ready, n + 2 + e)
                    dve.tensor_tensor(open_[:, :, e], open_[:, :, e - 1], hit[:, :, e - 1], ALU.is_gt).then_inc(top_ready, 1)
                dve.wait_ge(top_ready, n + 6)
                dve.tensor_tensor(top[:, :, :], hit[:, :, :], open_[:, :, :], ALU.mult).then_inc(top_ready, 1)
                for k in range(1, E * FC, 2):
                    dve.wait_ge(up_filled, g * E * FC + k + 1)
                    if k == 1:
                        dve.wait_ge(down_filled, g * GTILES)
                    dve.tensor_scalar(hT[k], up_banks[k % 4][:, :], b1c[:, k // FC, k % FC:k % FC + 1], 0.0,
                                      ALU.add, ALU.max).then_inc(relu_v, 1)
                for t in range(GTILES):
                    dve.wait_ge(down_filled, g * GTILES + t + 1)
                    if t == 0:
                        dve.wait_ge(top_ready, n + 7)
                    for e in range(E):
                        if not (t == 0 and e == 0):
                            dve.wait_ge(mix_ready, (g * GTILES + t) * E + e)
                        a = acc_all[:, bass.ds(g * GTILES + t, 1), :].rearrange("p o d -> p (o d)")
                        dve.scalar_tensor_tensor(a, ps_max[t % 2][:, e * D:(e + 1) * D], top[:, t, e:e + 1], a,
                                                 ALU.mult, ALU.add).then_inc(mix_ready, 1)

            dve.wait_ge(acc_ready, B)
            dve.memset(open_[:, :, 0], 1.0)
            experts(0)
            with dve.Fori(1, NG, 1) as g:
                experts(g)

        @block.tensor
        def _(pe):
            def mm(o_, lhsT, rhs, start=True, stop=True):
                return pe.matmul(o_, lhsT, rhs, start=start, stop=stop)

            def xnT_(b, p):
                pe.wait_ge(xn_ready, 2 * b + 2)
                pe.wait_ge(res1_ready, b)
                for t in range(T):
                    ins = pe.transpose(m0[:, t * P:(t + 1) * P], xn[p][:, t, :], ident[:, :])
                ins.then_inc(xnT_filled, 1)

            def projA(b, p, t):
                pe.wait_ge(xnT_ready, b + 1)
                pe.wait_ge(projA_ready, 2 * b + t)
                mm(m0[:, 0:3 * D], xnT[p][:, t * P:(t + 1) * P], wa[:, :], stop=False)
                mm(m0[:, 0:3 * D], ones16[:, :], bias16[:, 0:3 * D], start=False).then_inc(projA_filled, 1)

            def projB(b, p):
                pe.wait_ge(projA_ready, 2 * b + 2)
                for t in range(T):
                    ins = mm(m0[:, t * (D + L):(t + 1) * (D + L)], xnT[p][:, t * P:(t + 1) * P], wb[:, :])
                ins.then_inc(projB_filled, 1)

            def latT_(b, p):
                pe.wait_ge(lat_ready, 2 * b + 2)
                for t in range(T):
                    ins = pe.transpose(m0[:, t * P:(t + 1) * P], lat[p][:, t, :], ident[:, :])
                ins.then_inc(latT_filled, 1)

            def k_(b, p):
                pe.wait_ge(latT_ready, b + 1)
                for t in range(T):
                    ins = mm(m0[:, t * D:(t + 1) * D], latT[p][:, t * P:(t + 1) * P], wkv[:, 0:D])
                ins.then_inc(k_filled, 1)

            def qkT(b, p):
                pe.wait_ge(qrope_ready, 3 * b + 3)
                pe.wait_ge(krope_ready, 2 * b + 2)
                for t in range(T):
                    pe.transpose(m0[:, t * P:(t + 1) * P], qrot[p][:, t, :], ident[:, :])
                for t in range(T):
                    ins = pe.transpose(m0[:, S + t * P:S + (t + 1) * P], krot[p][:, t, :], ident[:, :])
                ins.then_inc(qkT_filled, 1)

            def max_chunk(b, p, g, c):
                n = 12 * b + 6 * g + c
                if c == 0:
                    pe.wait_ge(q_spread, PARTS * 16 * (b + 1))
                    pe.wait_ge(k_spread, PARTS * 16 * (b + 1))
                pe.wait_ge(max_read, past(n - 1))
                bank = ps_max[c % 2]
                t, nh, h0 = (0, 4, 4 * c) if c < 2 else (1, 2, 2 * c - 4)
                w = 512 // nh
                v = bank[:, :].rearrange("p (h k) -> p h k", h=nh)
                for i in range(nh):
                    col = (g * HG + h0 + i) * S
                    mm(bank[:, i * w:(i + 1) * w], qst[p][0:STACK, col + t * P:col + (t + 1) * P],
                             kst[p][0:STACK, col:col + w], start=(i == 0), stop=False)
                mm(v[:, :, t * P:(t + 1) * P], ident16[:, :], mask16[:, 0:1, :].broadcast_to((P, nh, P)),
                   start=False).then_inc(max_filled, 1)

            def exp_chunk(b, p, g, c):
                n = 12 * b + 6 * g + c
                if c == 0:
                    pe.wait_ge(m_spread, 16 * (2 * b + g + 1))
                pe.wait_ge(exp_ready, past(n - 1))
                bank = ps_exp[c % 2]
                kt, nh, h0 = (0, 2, 2 * c) if c < 4 else (1, 4, 4 * c - 16)
                w = 512 // nh
                v = bank[:, :].rearrange("p (h q) -> p h q", h=nh)
                for i in range(nh):
                    col = (g * HG + h0 + i) * S
                    mm(bank[:, i * w:(i + 1) * w], kst[p][:, col + kt * P:col + (kt + 1) * P],
                       qst[p][:, col + kt * P:col + S], start=(i == 0), stop=False)
                mm(v[:, :, 0:P], ident16[:, :], mask16[:, 1:2, :].broadcast_to((P, nh, P)),
                   start=False).then_inc(exp_filled, 1)

            def pv(b, p, g, heads):
                if heads[0] == 0:
                    pe.wait_ge(pvs_ready, 2 * b + g)
                    pe.wait_ge(exp_ready, 12 * b + 6 * g + 6)
                    pe.wait_ge(v_ready, b + 1)
                for h in heads:
                    mm(ps_pv[:, 0:S], vals[p][:, 0, g * HG + h, :], prob[g][:, h, 0:S], start=(h == 0), stop=False)
                    ins = mm(ps_pv[:, P:S], vals[p][:, 1, g * HG + h, :], prob[g][:, h, S:S + P], start=False,
                             stop=(h == HG - 1))
                if heads[-1] == HG - 1:
                    ins.then_inc(pv_filled, 1)

            def v_(b, p):
                pe.wait_ge(l0_ready, 2 * b)
                pe.wait_ge(latT_ready, b + 1)
                for t in range(T):
                    ins = mm(m1[:, t * D:(t + 1) * D], latT[p][:, t * P:(t + 1) * P], wkv[:, D:2 * D])
                ins.then_inc(v_filled, 1)

            def pvT_(b, g):
                if g == 0:
                    pe.wait_ge(zT_ready, b)
                else:
                    pe.wait_ge(o_ready, 2 * b + 1)
                pe.wait_ge(pvs_ready, 2 * b + g + 1)
                for t in range(T):
                    ins = pe.transpose(m2[:, t * P:(t + 1) * P], pvs[g][:, t * P:(t + 1) * P], ident[:, :])
                ins.then_inc(pvT_filled, 1)

            def oT_(b, p):
                pe.wait_ge(o_ready, 2 * b + 2)
                for t in range(T):
                    ins = pe.transpose(m2[:, t * P:(t + 1) * P], o[p][:, t, :, :].rearrange("p h d -> p (h d)"), ident[:, :])
                ins.then_inc(oT_filled, 1)

            def wo_(b, p):
                pe.wait_ge(oT_ready, b + 1)
                for t in range(T):
                    ins = mm(m2[:, t * D:(t + 1) * D], oT[p][:, t * P:(t + 1) * P], wo[:, :])
                ins.then_inc(wo_filled, 1)

            def zT_(b, p):
                pe.wait_ge(z_ready, b + 1)
                for t in range(T):
                    ins = pe.transpose(m2[:, t * P:(t + 1) * P], z[p][:, t, :], ident[:, :])
                ins.then_inc(zT_filled, 1)

            def mT_(b, g):
                pe.wait_ge(v_ready, (b + 2) if there(b, 1) else B)
                pe.wait_ge(l0_ready, 2 * (b + 1))
                pe.wait_ge(mT_ready, 2 * b + g)
                pe.wait_ge(msplit_ready, 4 * (2 * b + g + 1))
                pe.transpose(m1h[:, 0:P], nmp[g][:, :], ident16[:, :]).then_inc(mT_filled, 1)

            def eqT_(b, p):
                pe.wait_ge(v_ready, b + 1)
                pe.wait_ge(mT_ready, 2 * b)
                pe.wait_ge(eqk_ready, b + 1)
                for t in range(T):
                    ins = pe.transpose(m1[:, t * P:(t + 1) * P], eqk[p][:, t, 0:D], ident[:, :])
                ins.then_inc(eqT_filled, 1)

            def klC_(b, p):
                pe.wait_ge(eqT_ready, b + 1)
                pe.wait_ge(k3_ready, b + 1)
                for t in range(T):
                    mm(m1[:, 0:D], pool4[:, t, :], kh[p][:, t, :], start=(t == 0), stop=(t == T - 1))
                for t in range(T):
                    ins = mm(m1[:, D:2 * D], kh[p][:, t, :], k3[p][:, t, :], start=(t == 0), stop=(t == T - 1))
                ins.then_inc(klC_filled, 1)

            def gram_(b, p):
                pe.wait_ge(klC_ready, b + 1)
                mm(m1[:, 0:D], klC[p][:, 0:D], klC[p][:, 0:D]).then_inc(gram_filled, 1)

            def mid_(b, p):
                pe.wait_ge(gram_ready, b + 1)
                mm(m1[:, 0:D], gram[p][:, :], klC[p][:, D:2 * D]).then_inc(mid_filled, 1)

            def l0_(b, p):
                pe.wait_ge(mid_ready, b + 1)
                for t in range(T):
                    ins = mm(m1[:, t * D:(t + 1) * D], eqT[p][:, t * P:(t + 1) * P], mid[p][:, :])
                ins.then_inc(l0_filled, 1)

            def step(b, p):
                q = 1 - p
                for c in range(6):
                    max_chunk(b, p, 0, c)
                    if c == 1 and there(b, 1):
                        qkT(b + 1, q)
                    if there(b, -1):
                        pv(b - 1, q, 1, (c,))
                max_chunk(b, p, 1, 0)
                if there(b, -1):
                    pv(b - 1, q, 1, (6,))
                max_chunk(b, p, 1, 1)
                if there(b, -1):
                    pv(b - 1, q, 1, (7,))
                if there(b, 1):
                    v_(b + 1, q)
                if there(b, 2):
                    xnT_(b + 2, p)
                max_chunk(b, p, 1, 2)
                mT_(b, 0)
                if there(b, -1):
                    pvT_(b - 1, 1)
                if there(b, 2):
                    projA(b + 2, p, 0)
                max_chunk(b, p, 1, 3)
                if there(b, -1):
                    oT_(b - 1, q)
                if there(b, 2):
                    projA(b + 2, p, 1)
                max_chunk(b, p, 1, 4)
                if there(b, -1):
                    wo_(b - 1, q)
                if there(b, 2):
                    projB(b + 2, p)
                max_chunk(b, p, 1, 5)
                exp_chunk(b, p, 0, 0)
                mT_(b, 1)
                exp_chunk(b, p, 0, 1)
                if there(b, 1):
                    eqT_(b + 1, q)
                exp_chunk(b, p, 0, 2)
                if there(b, 1):
                    klC_(b + 1, q)
                exp_chunk(b, p, 0, 3)
                if there(b, 1):
                    gram_(b + 1, q)
                if there(b, -1):
                    zT_(b - 1, q)
                exp_chunk(b, p, 0, 4)
                if there(b, 1):
                    mid_(b + 1, q)
                exp_chunk(b, p, 0, 5)
                if there(b, 1):
                    l0_(b + 1, q)
                if there(b, 2):
                    latT_(b + 2, p)
                exp_chunk(b, p, 1, 0)
                exp_chunk(b, p, 1, 1)
                if there(b, 2):
                    k_(b + 2, p)
                for c, heads in ((2, (0, 1)), (3, (2, 3)), (4, (4, 5)), (5, (6, 7))):
                    pv(b, p, 0, heads)
                    exp_chunk(b, p, 1, c)
                pvT_(b, 0)

            def front(b, p):
                xnT_(b, p)
                projA(b, p, 0)
                projA(b, p, 1)
                projB(b, p)
                latT_(b, p)

            def prologue():
                pe.wait_ge(w_ready, 1)
                mm(m0[0:L + 1, 0:2 * D], ln_b[:, :], wkv[0:L, :]).then_inc(lnb_filled, 1)
                pe.wait_ge(bias_ready, 1)
                front(0, 0)
                pe.wait_ge(w_ready, 2)
                k_(0, 0)
                v_(0, 0)
                qkT(0, 0)
                front(1, 1)
                k_(1, 1)
                eqT_(0, 0)
                klC_(0, 0)
                gram_(0, 0)
                mid_(0, 0)
                l0_(0, 0)

            def last():
                pv(B - 1, 1, 1, tuple(range(HG)))
                pvT_(B - 1, 1)
                oT_(B - 1, 1)
                wo_(B - 1, 1)
                zT_(B - 1, 1)

            steps(pe, step, prologue, last)

            def experts(g, p):
                pe.wait_ge(zg_ready, g + 1)
                pe.wait_ge(top_ready, 7 * g)
                for t in range(GTILES):
                    ins = mm(m0[:, t * E:(t + 1) * E], zg[p][:, t * P:(t + 1) * P], gate[:, :])
                ins.then_inc(gate_filled, 1)
                pe.wait_ge(moe_loaded, 2 * 16)
                for n in range(E * FC):
                    k = g * (E * FC // 2) + n // 2 - 1
                    pe.wait_ge((relu_a, relu_v)[n % 2], past(k))
                    mm(up_banks[n % 4][:, :], w1[:, n // FC, (n % FC) * P:(n % FC + 1) * P],
                       zg[p]).then_inc(up_filled, 1)
                pe.wait_ge(relu_a, (g + 1) * (E * FC // 2))
                pe.wait_ge(relu_v, (g + 1) * (E * FC // 2))
                for t in range(GTILES):
                    pe.wait_ge(mix_ready, past((g * GTILES + t - 1) * E))
                    bank = ps_max[t % 2]
                    for e in range(E):
                        o_ = bank[:, e * D:(e + 1) * D]
                        for c in range(FC):
                            mm(o_, hT[e * FC + c][:, t * P:(t + 1) * P], w2[:, e, c, :], start=(c == 0), stop=False)
                        ins = mm(o_, ones16[:, :], bias16[:, (3 + e) * D:(4 + e) * D], start=False)
                    ins.then_inc(down_filled, 1)

            experts(0, 0)
            experts(1, 1)
            with pe.Fori(1, NG // 2, 1) as i:
                experts(2 * i, 0)
                experts(2 * i + 1, 1)


def constants():
    f = np.float32
    half = HD // 2
    pos = np.arange(S, dtype=f)[:, None]
    inv = (f(1.0) / f(10000.0) ** (np.arange(half, dtype=f) / f(half))).astype(f)
    ang = (pos * inv[None, :]).astype(f)
    rope = np.zeros((P, 2, 2, T, 64), f)
    for t in range(T):
        for w, fn in ((0, np.cos), (1, np.sin)):
            tab = np.repeat(fn(ang[t * P:(t + 1) * P]).astype(f), H, axis=1)
            rope[:, 0, w, t] = tab * f(1.0 / np.sqrt(HD))
            rope[:, 1, w, t] = tab
    r, c = np.arange(P)[:, None], np.arange(P)[None, :]
    mask = np.stack([np.where(c > r, MASKED, 0.0), np.where(r > c, MASKED, 0.0)], 1).astype(f)
    pool4 = np.zeros((P, T, P), f)
    for t in range(T):
        pool4[np.arange(P), t, (t * P + np.arange(P)) // (S // L)] = L / S
    return {"ident": np.eye(P, dtype=f), "mask": mask, "pool4": pool4, "rope": rope,
            "part_row": np.eye(PARTS, dtype=f)}


def kernel(**inputs):
    import concourse.bacc as _bacc
    from concourse.bass_utils import run_bass_kernel_spmd as _run

    g = {k.replace("L0_", ""): np.asarray(v) for k, v in inputs.items()}
    by_dim = np.arange(D).reshape(H, HD).T.reshape(-1)
    rows = lambda a, n: np.broadcast_to(a.reshape(1, -1), (n, a.size))
    lnb = np.zeros((L, L + 1), np.float32)
    lnb[:, L] = g["ffn_ln_b"]
    a = constants()
    a.update({
        "x": g["attn_hidden_states"],
        "wa": np.concatenate([g["attn_Wq"], g["attn_Wk"], g["attn_Wv"]], 1),
        "wb": np.concatenate([g["ffn_Wq"].T[:, by_dim], g["ffn_Wdkv"].T], 1),
        "wkv": np.concatenate([g["ffn_Wuk"].T[:, by_dim], g["ffn_Wuv"].T], 1),
        "n1w": g["ffn_norm1_w"][:, None], "n2w": g["ffn_norm2_w"][:, None],
        "ln_g": g["ffn_ln_g"][:, None], "ln_b": lnb,
        "wo": g["ffn_Wo"].T, "gate": g["ffn_gate_w"].T, "gate_b": rows(g["ffn_gate_b"], P),
        "w1": g["ffn_W1"].transpose(2, 0, 1),
        "w2": g["ffn_W2"].reshape(E, D, FC, P).transpose(3, 0, 2, 1),
        "b1c": g["ffn_b1"].reshape(E, FC, P).transpose(2, 0, 1),
        "brow": rows(np.concatenate([g["attn_bq"], g["attn_bk"], g["attn_bv"], g["ffn_b2"].reshape(-1)]), PARTS),
    })
    nc = _bacc.Bacc("TRN2", target_bir_lowering=False, num_devices=1)
    arrays, dram = {}, {}
    for n, v in a.items():
        v = np.ascontiguousarray(v)
        arrays[f"in_{n}"] = v
        dram[n] = nc.dram_tensor(f"in_{n}", v.shape, mybir.dt.from_np(v.dtype), kind="ExternalInput").ap()
    for n, parts in (("q_parts", 2 * PARTS - 1), ("k_parts", PARTS)):
        dram[n] = nc.dram_tensor(n, (2, parts, P * S), mybir.dt.bfloat16, kind="Internal").ap()
    out = nc.dram_tensor("out_0", (B, S, D), mybir.dt.float32, kind="ExternalOutput").ap()
    build(nc, dram, out)
    r = _run(nc, [arrays], core_ids=[0])
    return r.results[0]["out_0"]
```

```python
import numpy as np

import concourse.bass as bass
from concourse import mybir
from contextlib import ExitStack

B, S, D = 16, 256, 128
P = 128
T = S // P
H, HD = 16, 8
L = 64
E, F = 4, 512
FC = F // P
PARTS = 3
STACK = PARTS * PARTS * HD
ROWS = STACK + PARTS
HG = H // 2
VW = P // HG
NTOK = B * S
REGION = NTOK + P
NT = NTOK // P + E - 1
ROW = 2 * D + 1
NOBODY = 2 * NTOK
MASKED = -1e38
DEEP = 4
PLAN = 16
SAVES = 3 * 16


def build(nc, dram, out):
    f32, bf16, u32 = mybir.dt.float32, mybir.dt.bfloat16, mybir.dt.uint32
    ALU, ACT, AX = mybir.AluOpType, mybir.ActivationFunctionType, mybir.AxisListType
    ctx = ExitStack()
    with ctx:
        def sb(name, shape, dt=f32):
            return ctx.enter_context(nc.sbuf_tensor(name, shape, dt))

        def two(name, shape, dt=f32):
            return [sb(f"{name}{i}", shape, dt) for i in range(2)]

        def sem(name):
            return ctx.enter_context(nc.semaphore(name))

        def spread(ap, n):
            return ap.unsqueeze(len(ap.shape)).broadcast_to(tuple(ap.shape) + (n,))

        def past(v):
            return max(v, 0) if isinstance(v, int) else v

        ident = sb("ident", [P, P])
        ident16 = sb("ident16", [P, P], bf16)
        mask16 = sb("mask16", [P, 2, P], bf16)
        pool4 = sb("pool4", [P, T, P])
        rope = sb("rope", [P, 2, 2, T, 64])
        wa = sb("wa", [P, 3 * D])
        wb = sb("wb", [P, D + L])
        wkv = sb("wkv", [L + 1, 2 * D])
        ln_g = sb("ln_g", [L, 1])
        ln_b = sb("ln_b", [L, L + 1])
        n1w = sb("n1w", [P, 1])
        n2w = sb("n2w", [P, 1])
        wo = sb("wo", [P, D])
        gate = sb("gate", [P, E])
        gate_b = sb("gate_b", [P, E])
        b2b = sb("b2b", [P, E, D])
        tri16 = sb("tri16", [P, P], bf16)
        all16 = sb("all16", [P, P], bf16)
        first = sb("first", [P, E])
        region = sb("region", [P, E])
        taken = sb("taken", [P, E])
        token = sb("token", [P, B * T], u32)
        steps128 = sb("steps128", [P, NTOK // P])
        tile_no = sb("tile_no", [P, NT])
        pad_row = sb("pad_row", [P, ROW])
        part_row = sb("part_row", [PARTS, PARTS])
        ones16 = sb("ones16", [PARTS, P], bf16)
        NBIAS = 3 * D
        bias16 = sb("bias16", [PARTS, NBIAS], bf16)
        b1c = sb("b1c", [P, E, FC])
        zero = sb("zero", [P, 1])
        none = sb("none", [P, 1], u32)
        mhalf = sb("mhalf", [P, T])
        eps5 = sb("eps5", [P, T])
        eps6 = sb("eps6", [P, T])

        x_in = two("x_in", [P, T, D])
        xn = two("xn", [P, T, D])
        xnl = two("xnl", [P, T, D])
        bn = two("bn", [P, T, 6])
        mv = two("mv", [P, T, 2])
        ln = two("ln", [P, 6, T])
        xnT = two("xnT", [P, S])
        qkv = two("qkv", [P, T, 3 * D])
        qy = two("qy", [P, T, D + L])
        ybn = two("ybn", [P, T, 6])
        ymv = two("ymv", [P, T, 2])
        yln = two("yln", [P, 5, T])
        lat = two("lat", [P, T, P])
        latT = two("latT", [L + 1, S])
        kraw = two("kraw", [P, T, D])
        vals = two("vals", [P, T, H, P])
        pvs = two("pvs", [P, S])
        qs = two("qs", [P, T, D])
        ra = two("ra", [P, T, D])
        rb = two("rb", [P, T, D])
        qrot = two("qrot", [P, T, D])
        krot = two("krot", [P, T, D])
        part = two("part", [P, PARTS, 2 * S], bf16)
        res = two("res", [P, 2 * S])
        qst = two("qst", [ROWS, H * S], bf16)
        kst = two("kst", [ROWS, H * S], bf16)
        nmax = two("nmax", [P, HG, T])
        mres = two("mres", [P, HG * T])
        nmp = two("nmp", [P, P], bf16)
        mT = two("mT", [PARTS * HG * T, P], bf16)
        prob = two("prob", [P, HG, S + P])
        early = [t_[:, :, :].rearrange("p h q -> p (h q)") for t_ in prob]
        brow = early[0][0:PARTS, 0:NBIAS]
        btmp = early[0][0:PARTS, NBIAS:3 * NBIAS].rearrange("p (i n) -> p i n", i=2)
        mask_raw = early[1][:, 0:2 * P].rearrange("p (i n) -> p i n", i=2)
        tri_raw = early[1][:, 2 * P + 2 * NBIAS:3 * P + 2 * NBIAS]
        bpart = early[1][0:PARTS, 2 * P:2 * P + PARTS * NBIAS // 2].bitcast(bf16).rearrange("p (i n) -> p i n", i=PARTS)
        rden = two("rden", [P, T, HG])
        o = two("o", [P, T, H, HD])
        oT = two("oT", [P, S])
        x1 = two("x1", [P, T, D])
        x1bn = two("x1bn", [P, T, 6])
        x1mv = two("x1mv", [P, T, 2])
        x1ln = two("x1ln", [P, 4, T])
        rows = two("rows", [P, T, ROW])
        zT = two("zT", [P, S])
        nqk = two("nqk", [P, T, 2])
        qks = two("qks", [P, T, 2 * D])
        eqk = two("eqk", [P, T, 2 * D])
        sqk = two("sqk", [P, 2, T, 2])
        kh = two("kh", [P, T, D])
        k3 = two("k3", [P, T, D])
        eqT = two("eqT", [P, S])
        klC = two("klC", [P, 2 * D])
        gram = two("gram", [P, D])
        mid = two("mid", [P, D])
        accx = two("accx", [P, T, D])
        lg = sb("lg", [P, T, E])
        lmax = sb("lmax", [P, T])
        hit = sb("hit", [P, T, E])
        pref = sb("pref", [P, T, E])
        pmax = sb("pmax", [P, T])
        top16 = two("top16", [P, T, E], bf16)
        cand = sb("cand", [P, T, E])
        chosen = sb("chosen", [P, T, E])
        slot = sb("slot", [P, T])
        slot_u = two("slot_u", [P, T], u32)
        count = sb("count", [P, E])
        over = sb("over", [P, E, NTOK // P])
        tiles = sb("tiles", [P, E])
        ends = sb("ends", [P, E])
        jump = sb("jump", [P, E])
        passed = sb("passed", [P, E, NT])
        jumps = sb("jumps", [P, E, NT])
        expert_f = sb("expert_f", [P, NT])
        jumped = sb("jumped", [P, NT])
        inside = sb("inside", [P, NT])
        expert_u = sb("expert_u", [P, NT], u32)
        start_u = sb("start_u", [P, NT], u32)
        pad_u = sb("pad_u", [P, E], u32)
        experts_w = vals[0][:, :, :, :].rearrange("p t h n -> p (t h n)")
        w1 = experts_w[:, 0:E * F].rearrange("p (e f) -> p e f", e=E)
        w2 = experts_w[:, E * F:2 * E * F].rearrange("p (e f) -> p e f", e=E)
        tile_in = [sb(f"tile_in{i}", [P, ROW]) for i in range(DEEP)]
        ztT = [sb(f"ztT{i}", [P, P]) for i in range(DEEP)]
        w1c = two("w1c", [P, F])
        b1x = two("b1x", [P, FC])
        w2c = two("w2c", [P, F])
        hT = two("hT", [P, FC, P])
        y = two("y", [P, D])
        sum_out = [sb(f"sum_out{i}", [P, D]) for i in range(DEEP)]
        out_row = [sb(f"out_row{i}", [P, 1], u32) for i in range(DEEP)]

        ps_max = [ctx.enter_context(nc.psum_tensor(f"ps_max{i}", [P, 512], f32)) for i in range(2)]
        ps_exp = [ctx.enter_context(nc.psum_tensor(f"ps_exp{i}", [P, 512], f32)) for i in range(2)]
        m0 = ctx.enter_context(nc.psum_tensor("m0", [P, 512], f32))
        m1 = ctx.enter_context(nc.psum_tensor("m1", [P, 512], f32))
        m2 = ctx.enter_context(nc.psum_tensor("m2", [P, 512], f32))
        ps_pv = ctx.enter_context(nc.psum_tensor("ps_pv", [P, 512], f32))
        m1h = m1[:, :].bitcast(bf16)

        w_loaded = sem("w_loaded")
        w_ready = sem("w_ready")
        moe_loaded = sem("moe_loaded")
        bias_ready = sem("bias_ready")
        x_loaded = sem("x_loaded")
        bn_ready = sem("bn_ready")
        mv_ready = sem("mv_ready")
        ln_ready = sem("ln_ready")
        xn_ready = sem("xn_ready")
        xnT_filled = sem("xnT_filled")
        xnT_ready = sem("xnT_ready")
        projA_filled = sem("projA_filled")
        projA_ready = sem("projA_ready")
        projB_filled = sem("projB_filled")
        projB_ready = sem("projB_ready")
        ybn_ready = sem("ybn_ready")
        ymv_ready = sem("ymv_ready")
        yln_ready = sem("yln_ready")
        lat_ready = sem("lat_ready")
        latT_filled = sem("latT_filled")
        latT_ready = sem("latT_ready")
        k_filled = sem("k_filled")
        v_filled = sem("v_filled")
        pvs_ready = sem("pvs_ready")
        pvT_filled = sem("pvT_filled")
        k_ready = sem("k_ready")
        v_ready = sem("v_ready")
        qrope_ready = sem("qrope_ready")
        krope_ready = sem("krope_ready")
        qkT_filled = sem("qkT_filled")
        part1_ready = sem("part1_ready")
        res1_ready = sem("res1_ready")
        part2_ready = sem("part2_ready")
        part3_ready = sem("part3_ready")
        qk_saved = sem("qk_saved")
        q_spread = sem("q_spread")
        k_spread = sem("k_spread")
        max_filled = sem("max_filled")
        max_read = sem("max_read")
        msplit_ready = sem("msplit_ready")
        mT_filled = sem("mT_filled")
        mT_ready = sem("mT_ready")
        m_spread = sem("m_spread")
        exp_filled = sem("exp_filled")
        exp_ready = sem("exp_ready")
        pv_filled = sem("pv_filled")
        rden_ready = sem("rden_ready")
        o_ready = sem("o_ready")
        oT_filled = sem("oT_filled")
        oT_ready = sem("oT_ready")
        wo_filled = sem("wo_filled")
        x1_ready = sem("x1_ready")
        x1bn_ready = sem("x1bn_ready")
        x1mv_ready = sem("x1mv_ready")
        x1ln_ready = sem("x1ln_ready")
        z_ready = sem("z_ready")
        acc_ready = sem("acc_ready")
        zT_filled = sem("zT_filled")
        zT_ready = sem("zT_ready")
        nqk_ready = sem("nqk_ready")
        qks_ready = sem("qks_ready")
        eqk_ready = sem("eqk_ready")
        sqk_ready = sem("sqk_ready")
        kh_ready = sem("kh_ready")
        k3_ready = sem("k3_ready")
        eqT_filled = sem("eqT_filled")
        eqT_ready = sem("eqT_ready")
        klC_filled = sem("klC_filled")
        klC_ready = sem("klC_ready")
        gram_filled = sem("gram_filled")
        gram_ready = sem("gram_ready")
        mid_filled = sem("mid_filled")
        mid_ready = sem("mid_ready")
        l0_filled = sem("l0_filled")
        l0_ready = sem("l0_ready")
        xnl_ready = sem("xnl_ready")
        setup = sem("setup")
        out_stored = sem("out_stored")
        bias_ready_v = sem("bias_ready_v")
        lnb_filled = sem("lnb_filled")
        gate_filled = sem("gate_filled")
        top_ready = sem("top_ready")
        rank_filled = sem("rank_filled")
        slot_ready = sem("slot_ready")
        row_scattered = sem("row_scattered")
        plan_ready = sem("plan_ready")
        pad_stored = sem("pad_stored")
        tile_loaded0 = sem("tile_loaded0")
        tile_loaded1 = sem("tile_loaded1")
        tile_loaded2 = sem("tile_loaded2")
        tile_loaded3 = sem("tile_loaded3")
        tile_loaded = (tile_loaded0, tile_loaded1, tile_loaded2, tile_loaded3)
        ztT_filled = sem("ztT_filled")
        ztT_ready = sem("ztT_ready")
        w1c_ready = sem("w1c_ready")
        w2c_ready = sem("w2c_ready")
        up_filled = sem("up_filled")
        relu_a = sem("relu_a")
        relu_v = sem("relu_v")
        down_filled = sem("down_filled")
        row_ready = sem("row_ready")
        y_ready = sem("y_ready")
        sum_ready = sem("sum_ready")

        NW = 25
        block = ctx.enter_context(nc.Block())

        def steps(eng, step, prologue, last):
            prologue()
            for b in (0, 1):
                step(b, b % 2)
            with eng.Fori(1, B // 2 - 1, 1) as i:
                for k in (0, 1):
                    b = 2 * i + k
                    step(b, k)
            for b in (B - 2, B - 1):
                step(b, b % 2)
            last()

        def tile_steps(eng, step):
            for t in range(DEEP):
                step(t, t, 0)
            with eng.Fori(1, NT // DEEP, 1) as i:
                for k in range(DEEP):
                    step(DEEP * i + k, k, i)
            for t in range(NT // DEEP * DEEP, NT):
                step(t, t % DEEP, t // DEEP)

        def more(t, n=1):
            return not isinstance(t, int) or t + n < NT

        def later(t, n):
            return not isinstance(t, int) or t >= n

        def there(b, ahead):
            return not isinstance(b, int) or 0 <= b + ahead < B

        @block.sync
        def _(sp):
            pairs = [(ident, "ident"), (mask_raw, "mask"), (tri_raw, "tri"), (b2b, "b2b"), (first, "first"),
                     (region, "region"), (taken, "region"), (token, "token"), (steps128, "steps128"), (tile_no, "tile_no"), (pool4, "pool4"), (rope, "rope"), (wa, "wa"), (wb, "wb"),
                     (n1w, "n1w"), (n2w, "n2w"), (wo, "wo"), (gate, "gate"), (gate_b, "gate_b"),
                     (part_row, "part_row"), (brow, "brow"), (b1c, "b1c"), (ln_g, "ln_g"), (ln_b, "ln_b")]

            def load_x(b, p):
                sp.wait_ge(l0_ready, past(2 * (b - 1)))
                sp.dma_start(x_in[p][:, :, :], dram["x"][bass.ds(b, 1)].rearrange("o (t p) d -> p (o t) d", p=P)
                             if not isinstance(b, int) else dram["x"][b].rearrange("(t p) d -> p t d", p=P)
                             ).then_inc(x_loaded, 16)

            def save_qk(b, p):
                sp.wait_ge(part3_ready, b + 1)
                to_rows = "i (r t) -> r i t"
                sp.dma_start(dram["q_parts"][p, 0:PARTS].rearrange(to_rows, t=S), part[p][:, :, 0:S]).then_inc(qk_saved, 16)
                sp.dma_start(dram["q_parts"][p, PARTS:2 * PARTS - 1].rearrange(to_rows, t=S),
                             part[p][:, 0:PARTS - 1, 0:S]).then_inc(qk_saved, 16)
                sp.dma_start(dram["k_parts"][p].rearrange(to_rows, t=S), part[p][:, :, S:2 * S]).then_inc(qk_saved, 16)

            def stack_qk(b, p):
                sp.wait_ge(qk_saved, SAVES * (b + 1))
                for a in range(PARTS):
                    to = slice(PARTS * HD * a, PARTS * HD * (a + 1))
                    sp.dma_start(qst[p][to, :], dram["q_parts"][p, a:a + PARTS].rearrange("i (d n) -> (i d) n", d=HD)
                                 ).then_inc(q_spread, 16)
                    sp.dma_start(kst[p][to, :], dram["k_parts"][p].rearrange("i (d n) -> (i d) n", d=HD)
                                 ).then_inc(k_spread, 16)

            def spread_m(b, p, g):
                sp.wait_ge(mT_ready, 2 * b + g + 1)
                sp.dma_start(qst[p][STACK:ROWS, g * HG * S:(g + 1) * HG * S], mT[g][:, :]).then_inc(m_spread, 16)

            def prologue():
                load_x(0, 0)
                load_x(1, 1)
                sp.wait_ge(setup, 2)
                sp.dma_start(dram["by_expert"][E * REGION:E * REGION + P, :], pad_row[:, :]).then_inc(pad_stored, 16)
                for t, n in pairs:
                    sp.dma_start(t[tuple(slice(None) for _ in t.shape)], dram[n]).then_inc(w_loaded, 16)
                sp.dma_start(wkv[0:L, :], dram["wkv"]).then_inc(w_loaded, 16)
                save_qk(0, 0)
                stack_qk(0, 0)

            def step(b, p):
                if there(b, 2):
                    load_x(b + 2, p)
                if there(b, 1):
                    save_qk(b + 1, 1 - p)
                spread_m(b, p, 0)
                if there(b, 1):
                    stack_qk(b + 1, 1 - p)
                spread_m(b, p, 1)

            def last():
                sp.wait_ge(pv_filled, 2 * B - 2)
                sp.dma_start(w1, dram["w1"]).then_inc(moe_loaded, 16)
                sp.dma_start(w2, dram["w2"]).then_inc(moe_loaded, 16)

            steps(sp, step, prologue, last)
            zs = dram["by_expert"]
            sp.wait_ge(plan_ready, PLAN)
            sp.wait_ge(row_scattered, 2 * 16 * B)
            for e in range(E // 2):
                pad = sp.value_load(pad_u[0:1, e:e + 1], min_val=0, max_val=E * REGION - P)
                sp.dma_start(zs[bass.ds(pad, P), :], pad_row[:, :]).then_inc(pad_stored, 16)
            sp.wait_ge(pad_stored, 16 * (E + 1))

            def load_tile(t, k, i):
                row = sp.value_load(start_u[0:1, bass.ds(t, 1)], min_val=0, max_val=E * REGION)
                if later(t, DEEP):
                    sp.wait_ge(row_ready, t - DEEP + 1)
                sp.dma_start(tile_in[k][:, :], zs[bass.ds(row, P), :]).then_inc(tile_loaded[k], 16)

            tile_steps(sp, load_tile)
            sp.wait_ge(out_stored, 16 * NT)

        @block.gpsimd
        def _(pool):
            def tt(o_, a, c, op):
                return pool.tensor_tensor(o_, a, c, op)

            def layer_norm(b, p):
                n = 6 * b
                pool.wait_ge(mv_ready, 2 * b + 2)
                tt(ln[p][:, 0], mv[p][:, :, 1], eps5[:, :], ALU.add).then_inc(ln_ready, 1)
                pool.wait_ge(ln_ready, n + 1)
                tt(ln[p][:, 1], ln[p][:, 0], mhalf[:, :], ALU.pow).then_inc(ln_ready, 1)
                pool.wait_ge(ln_ready, n + 2)
                tt(ln[p][:, 2], mv[p][:, :, 1], ln[p][:, 1], ALU.mult).then_inc(ln_ready, 1)
                pool.wait_ge(ln_ready, n + 3)
                tt(ln[p][:, 3], ln[p][:, 2], ln[p][:, 1], ALU.mult).then_inc(ln_ready, 1)
                pool.wait_ge(ln_ready, n + 4)
                tt(ln[p][:, 4], ln[p][:, 3], eps6[:, :], ALU.add).then_inc(ln_ready, 1)
                pool.wait_ge(ln_ready, n + 5)
                tt(ln[p][:, 5], ln[p][:, 4], mhalf[:, :], ALU.pow).then_inc(ln_ready, 1)

            def latent_scale(b, p):
                n = 5 * b
                pool.wait_ge(ln_ready, 6 * b + 6)
                tt(yln[p][:, 0], ln[p][:, 5], ln[p][:, 5], ALU.mult).then_inc(yln_ready, 1)
                pool.wait_ge(yln_ready, n + 1)
                pool.wait_ge(ymv_ready, 2 * b + 2)
                tt(yln[p][:, 1], yln[p][:, 0], ymv[p][:, :, 1], ALU.mult).then_inc(yln_ready, 1)
                pool.wait_ge(yln_ready, n + 2)
                tt(yln[p][:, 2], yln[p][:, 1], eps5[:, :], ALU.add).then_inc(yln_ready, 1)
                pool.wait_ge(yln_ready, n + 3)
                tt(yln[p][:, 3], yln[p][:, 2], mhalf[:, :], ALU.pow).then_inc(yln_ready, 1)
                pool.wait_ge(yln_ready, n + 4)
                tt(yln[p][:, 4], yln[p][:, 3], ln[p][:, 5], ALU.mult).then_inc(yln_ready, 1)

            def rotate(src, dst, which, ready, n, p):
                c = rope[:, which, 0, :, :].unsqueeze(2).broadcast_to((P, T, 2, 64))
                v = src[:, :, :].rearrange("p t (a c) -> p t a c", a=2)
                w = rb[p][:, :, :].rearrange("p t (a c) -> p t a c", a=2)
                tt(ra[p][:, :, :].rearrange("p t (a c) -> p t a c", a=2), v, c, ALU.mult)
                tt(w[:, :, 1, :], v[:, :, 0, :], rope[:, which, 1, :, :], ALU.mult)
                tt(w[:, :, 0, :], v[:, :, 1, :], rope[:, which, 1, :, :], ALU.mult).then_inc(ready, 1)
                pool.wait_ge(ready, n)
                d = dst[:, :, :].rearrange("p t (a c) -> p t a c", a=2)
                u = ra[p][:, :, :].rearrange("p t (a c) -> p t a c", a=2)
                tt(d[:, :, 0, :], u[:, :, 0, :], w[:, :, 0, :], ALU.subtract)
                tt(d[:, :, 1, :], u[:, :, 1, :], w[:, :, 1, :], ALU.add).then_inc(ready, 1)

            def rope_q(b, p):
                pool.wait_ge(projB_ready, b + 1)
                pool.wait_ge(qkT_filled, past(b - 1))
                tt(qs[p][:, :, :], qy[p][:, :, 0:D], spread(ln[p][:, 5], D), ALU.mult).then_inc(qrope_ready, 1)
                pool.wait_ge(qrope_ready, 3 * b + 1)
                rotate(qs[p], qrot[p], 0, qrope_ready, 3 * b + 2, p)

            def rope_k(b, p):
                pool.wait_ge(k_ready, b + 1)
                pool.wait_ge(qrope_ready, 3 * b + 3)
                rotate(kraw[p], krot[p], 1, krope_ready, 2 * b + 1, p)

            def parts(b, p):
                pool.wait_ge(res1_ready, b + 1)
                pool.wait_ge(qk_saved, past(SAVES * (b - 1)))
                tt(part[p][:, 1, :], res[p][:, :], zero[:, 0:1].broadcast_to((P, 2 * S)), ALU.add).then_inc(part2_ready, 1)
                pool.wait_ge(part2_ready, b + 1)
                pool.wait_ge(exp_filled, past(12 * (b - 1)))
                tt(part[p][:, 2, :], res[p][:, :], part[p][:, 1, :], ALU.subtract).then_inc(part3_ready, 1)

            def soft_shift(b, p):
                pool.wait_ge(nqk_ready, b + 1)
                v = lambda t_, w_: t_[:, :, 0:2 * D].rearrange("p t (j d) -> p t j d", j=2)
                tt(v(qks[p], 0), v(qkv[p], 0), spread(nqk[p][:, :, :], D), ALU.add).then_inc(qks_ready, 1)

            def soft_k(b, p):
                pool.wait_ge(sqk_ready, 2 * b + 2)
                tt(kh[p][:, :, :], eqk[p][:, :, D:2 * D], spread(sqk[p][:, 1, :, 1], D), ALU.mult).then_inc(kh_ready, 1)
                pool.wait_ge(kh_ready, b + 1)
                pool.wait_ge(slot_ready, past(5 * (b - 2)))
                pool.wait_ge(acc_ready, past(2 * (b - 2)))
                pool.wait_ge(row_scattered, past(2 * 16 * (b - 3)))
                tt(k3[p][:, :, :], kh[p][:, :, :], qkv[p][:, :, 2 * D:3 * D], ALU.mult).then_inc(k3_ready, 1)

            def late_xn(b, p):
                pool.wait_ge(x1_ready, past(b - 1))
                pool.wait_ge(xn_ready, 2 * b + 2)
                pool.wait_ge(row_scattered, past(2 * 16 * (b - 3) + 16))
                tt(xnl[p][:, :, :], xn[p][:, :, :], zero[:, 0:1].unsqueeze(2).broadcast_to((P, T, D)), ALU.add).then_inc(xnl_ready, 1)

            def finish(b, p):
                n = 4 * b
                pool.wait_ge(x1mv_ready, 2 * b + 2)
                tt(x1ln[p][:, 0], x1mv[p][:, :, 0], x1mv[p][:, :, 0], ALU.mult).then_inc(x1ln_ready, 1)
                pool.wait_ge(x1ln_ready, n + 1)
                tt(x1ln[p][:, 1], x1ln[p][:, 0], x1mv[p][:, :, 1], ALU.add).then_inc(x1ln_ready, 1)
                pool.wait_ge(x1ln_ready, n + 2)
                tt(x1ln[p][:, 2], x1ln[p][:, 1], eps6[:, :], ALU.add).then_inc(x1ln_ready, 1)
                pool.wait_ge(x1ln_ready, n + 3)
                tt(x1ln[p][:, 3], x1ln[p][:, 2], mhalf[:, :], ALU.pow).then_inc(x1ln_ready, 1)
                pool.wait_ge(x1ln_ready, n + 4)
                pool.wait_ge(row_scattered, past(2 * 16 * (b - 1)))
                tt(rows[p][:, :, 0:D], x1[p][:, :, :], spread(x1ln[p][:, 3], D), ALU.mult).then_inc(z_ready, 1)
                pool.wait_ge(l0_ready, 2 * b + 2)
                tt(rows[p][:, :, D:2 * D], accx[p][:, :, :], x1[p][:, :, :], ALU.add).then_inc(acc_ready, 1)
                tt(rows[p][:, :, 2 * D:ROW].bitcast(u32).rearrange("p t o -> p (t o)"), token[:, bass.ds(b * T, T)],
                   none[:, 0:1].broadcast_to((P, T)),
                   ALU.add).then_inc(acc_ready, 1)

            def scatter(b, p, t):
                if isinstance(b, int):
                    pool.wait_ge(slot_ready, 5 * (b + 1))
                    pool.wait_ge(acc_ready, 2 * (b + 1))
                    pool.wait_ge(row_scattered, 16 * (2 * b + t))
                pool.indirect_dma_start(dram["by_expert"], bass.IndirectOffsetOnAxis(slot_u[p][:, t:t + 1], 0),
                                        rows[p][:, t, :], None).then_inc(row_scattered, 16)

            def step(b, p):
                q = 1 - p
                if there(b, 2):
                    layer_norm(b + 2, p)
                if there(b, 1):
                    parts(b + 1, q)
                    soft_k(b + 1, q)
                if there(b, -2):
                    scatter(b - 2, p, 0)
                if there(b, -1):
                    finish(b - 1, q)
                if there(b, 2):
                    latent_scale(b + 2, p)
                    rope_q(b + 2, p)
                    soft_shift(b + 2, p)
                if there(b, 1):
                    late_xn(b + 1, q)
                if there(b, -2):
                    scatter(b - 2, p, 1)
                if there(b, 2):
                    rope_k(b + 2, p)

            def prologue():
                pool.memset(none[:, :], 0)
                pool.memset(pad_row[:, 0:2 * D], 0.0).then_inc(setup, 1)
                pool.memset(pad_row[:, 2 * D:ROW].bitcast(u32), NOBODY).then_inc(setup, 1)
                for t_, v in ((zero, 0.0), (mhalf, -0.5), (eps5, 1e-5), (eps6, 1e-6)):
                    pool.memset(t_[:, :], v).then_inc(setup, 1)
                for i in range(2):
                    pool.wait_ge(setup, 6 + i)
                    pool.memset(kst[i][64:ROWS, :], 1.0).then_inc(setup, 1)
                for i in range(2):
                    pool.wait_ge(setup, 8 + i)
                    pool.memset(vals[i][:, :, :, :], 0.0).then_inc(setup, 1)
                pool.wait_ge(setup, 10)
                for t_ in vals:
                    for g in range(2):
                        a = t_[:, :, g * HG:(g + 1) * HG, :]
                        ones_at = bass.AP(tensor=a.tensor, offset=a.offset + HD,
                                          ap=[list(a.ap[0]), [H * P, T], [P + VW, HG], [1, 1]])
                        pool.memset(ones_at, 1.0).then_inc(setup, 1)
                pool.wait_ge(w_loaded, 16 * NW)
                layer_norm(0, 0)
                latent_scale(0, 0)
                rope_q(0, 0)
                soft_shift(0, 0)
                layer_norm(1, 1)
                rope_k(0, 0)
                parts(0, 0)
                soft_k(0, 0)
                late_xn(0, 0)
                latent_scale(1, 1)
                rope_q(1, 1)
                soft_shift(1, 1)
                rope_k(1, 1)

            def last():
                for t in range(T):
                    scatter(B - 2, 0, t)
                finish(B - 1, 1)
                for t in range(T):
                    scatter(B - 1, 1, t)

            steps(pool, step, prologue, last)
            tokens = pool.to_reg(NTOK - 1)
            by_token = out.rearrange("b s d -> (b s) d")

            def store(k):
                pool.indirect_dma_start(by_token, bass.IndirectOffsetOnAxis(out_row[k][:, 0:1], 0), sum_out[k][:, :],
                                        None, bounds_check=tokens, oob_is_err=False).then_inc(out_stored, 16)

            def add_rest(t, k, i):
                pool.wait_ge(y_ready, t + 1)
                if later(t, DEEP):
                    pool.wait_ge(out_stored, 16 * (t - DEEP + 1))
                tt(sum_out[k][:, :], y[k % 2][:, :], tile_in[k][:, D:2 * D], ALU.add).then_inc(sum_ready, 1)
                if later(t, 1):
                    pool.wait_ge(sum_ready, t)
                    pool.wait_ge(row_ready, t)
                if later(t, 2):
                    pool.wait_ge(out_stored, 16 * (t - 1))
                tt(out_row[k][:, :], tile_in[k][:, 2 * D:ROW].bitcast(u32), none[:, :], ALU.add).then_inc(row_ready, 1)
                if later(t, 1):
                    store((k - 1) % DEEP)

            tile_steps(pool, add_rest)
            pool.wait_ge(row_ready, NT)
            pool.wait_ge(sum_ready, NT)
            pool.wait_ge(out_stored, 16 * (NT - 1))
            store((NT - 1) % DEEP)

        @block.scalar
        def _(act):
            def copy(dst, src, scale=1.0):
                return act.activation(dst, src, ACT.Copy, scale=scale)

            def k_copy(b, p):
                act.wait_ge(k_filled, b + 1)
                act.wait_ge(krope_ready, past(2 * (b - 1)))
                copy(kraw[p][:, :, :], m0[:, 0:S].rearrange("p (t n) -> p t n", t=T)).then_inc(k_ready, 1)

            def v_copy(b, p):
                act.wait_ge(v_filled, b + 1)
                act.wait_ge(pv_filled, past(2 * (b - 1)))
                for t in range(T):
                    for g in range(2):
                        a = vals[p][:, t, g * HG:(g + 1) * HG, :]
                        dst = bass.AP(tensor=a.tensor, offset=a.offset, ap=[list(a.ap[0]), [P + VW, HG], [1, HD]])
                        ins = copy(dst, m1[:, t * D + g * D // 2:t * D + (g + 1) * D // 2].rearrange("p (h d) -> p h d", d=HD))
                ins.then_inc(v_ready, 1)

            def part1(b, p):
                act.wait_ge(qkT_filled, b + 1)
                act.wait_ge(qk_saved, past(SAVES * (b - 1)))
                copy(part[p][:, 0, :], m0[:, :]).then_inc(part1_ready, 1)

            def evac(b, filled, ready, dst, src, n=1, k=0, scale=1.0):
                act.wait_ge(filled, n * b + k + 1)
                copy(dst, src, scale).then_inc(ready, 1)

            def exp_chunk(b, p, g, c):
                act.wait_ge(exp_filled, 12 * b + 6 * g + c + 1)
                if c == 0:
                    act.wait_ge(pv_filled, past(2 * (b - 1) + g + 1))
                bank = ps_exp[c % 2]
                if c < 4:
                    dst, src = prob[g][:, 2 * c:2 * c + 2, 0:S], bank[:, :].rearrange("p (h q) -> p h q", h=2)
                else:
                    dst, src = prob[g][:, 4 * c - 16:4 * c - 12, S:S + P], bank[:, :].rearrange("p (h q) -> p h q", h=4)
                act.activation(dst, src, ACT.Exp).then_inc(exp_ready, 1)

            def pv_copy(b, g):
                act.wait_ge(pv_filled, 2 * b + g + 1)
                act.wait_ge(pvT_filled, past(2 * b + g - 1))
                copy(pvs[g][:, :], ps_pv[:, 0:S]).then_inc(pvs_ready, 1)

            def soft_exp(b, p):
                act.wait_ge(qks_ready, b + 1)
                act.activation(eqk[p][:, :, :], qks[p][:, :, :], ACT.Exp).then_inc(eqk_ready, 1)

            def step(b, p):
                q = 1 - p
                if there(b, 1):
                    soft_exp(b + 1, q)
                    part1(b + 1, q)
                    v_copy(b + 1, q)
                if there(b, 2):
                    evac(b + 2, xnT_filled, xnT_ready, xnT[p][:, :], m0[:, 0:S])
                if there(b, -1):
                    pv_copy(b - 1, 1)
                evac(b, mT_filled, mT_ready, mT[0][:, :], m1h[0:PARTS * HG * T, 0:P], 2, 0)
                if there(b, 2):
                    evac(b + 2, projA_filled, projA_ready, qkv[p][:, 0, :], m0[:, 0:3 * D], 2, 0)
                if there(b, -1):
                    evac(b - 1, oT_filled, oT_ready, oT[q][:, :], m2[:, 0:S])
                if there(b, 2):
                    evac(b + 2, projA_filled, projA_ready, qkv[p][:, 1, :], m0[:, 0:3 * D], 2, 1)
                    evac(b + 2, projB_filled, projB_ready, qy[p][:, :, :],
                         m0[:, 0:T * (D + L)].rearrange("p (t n) -> p t n", t=T))
                exp_chunk(b, p, 0, 0)
                exp_chunk(b, p, 0, 1)
                evac(b, mT_filled, mT_ready, mT[1][:, :], m1h[0:PARTS * HG * T, 0:P], 2, 1)
                exp_chunk(b, p, 0, 2)
                if there(b, 1):
                    evac(b + 1, eqT_filled, eqT_ready, eqT[q][:, :], m1[:, 0:S])
                exp_chunk(b, p, 0, 3)
                if there(b, 1):
                    evac(b + 1, klC_filled, klC_ready, klC[q][:, :], m1[:, 0:2 * D])
                if there(b, -1):
                    evac(b - 1, zT_filled, zT_ready, zT[q][:, :], m2[:, 0:S],
                         scale=n2w[:, 0:1])
                exp_chunk(b, p, 0, 4)
                if there(b, 1):
                    evac(b + 1, gram_filled, gram_ready, gram[q][:, :], m1[:, 0:D])
                exp_chunk(b, p, 0, 5)
                if there(b, 1):
                    evac(b + 1, mid_filled, mid_ready, mid[q][:, :], m1[:, 0:D])
                if there(b, 2):
                    evac(b + 2, latT_filled, latT_ready, latT[p][:, :], m0[0:L + 1, 0:S])
                exp_chunk(b, p, 1, 0)
                exp_chunk(b, p, 1, 1)
                if there(b, 2):
                    k_copy(b + 2, p)
                for c in range(2, 6):
                    exp_chunk(b, p, 1, c)
                pv_copy(b, 0)

            def front(b, p):
                evac(b, xnT_filled, xnT_ready, xnT[p][:, :], m0[:, 0:S])
                for t in range(T):
                    evac(b, projA_filled, projA_ready, qkv[p][:, t, :], m0[:, 0:3 * D], 2, t)
                evac(b, projB_filled, projB_ready, qy[p][:, :, :], m0[:, 0:T * (D + L)].rearrange("p (t n) -> p t n", t=T))
                evac(b, latT_filled, latT_ready, latT[p][:, :], m0[0:L + 1, 0:S])

            def prologue():
                act.wait_ge(lnb_filled, 1)
                copy(wkv[L:L + 1, :], m0[L:L + 1, 0:2 * D]).then_inc(bias_ready, 1)
                front(0, 0)
                k_copy(0, 0)
                v_copy(0, 0)
                soft_exp(0, 0)
                part1(0, 0)
                front(1, 1)
                k_copy(1, 1)
                evac(0, eqT_filled, eqT_ready, eqT[0][:, :], m1[:, 0:S])
                evac(0, klC_filled, klC_ready, klC[0][:, :], m1[:, 0:2 * D])
                evac(0, gram_filled, gram_ready, gram[0][:, :], m1[:, 0:D])
                evac(0, mid_filled, mid_ready, mid[0][:, :], m1[:, 0:D])

            def last():
                pv_copy(B - 1, 1)
                evac(B - 1, oT_filled, oT_ready, oT[1][:, :], m2[:, 0:S])
                evac(B - 1, zT_filled, zT_ready, zT[1][:, :], m2[:, 0:S],
                     scale=n2w[:, 0:1])

            steps(act, step, prologue, last)

            def fetch(t, k):
                e = act.value_load(expert_u[0:1, bass.ds(t, 1)], min_val=0, max_val=E - 1)
                if later(t, 2):
                    act.wait_ge(up_filled, t - 1)
                    act.wait_ge(relu_v, t - 1)
                    act.wait_ge(relu_a, t - 1)
                copy(w1c[k % 2][:, :], w1[:, bass.ds(e, 1), :].rearrange("p o f -> p (o f)")).then_inc(w1c_ready, 1)
                copy(b1x[k % 2][:, :], b1c[:, bass.ds(e, 1), :].rearrange("p o f -> p (o f)")).then_inc(w1c_ready, 1)

            def transposed(t, k):
                act.wait_ge(ztT_filled, t + 1)
                if later(t, DEEP):
                    act.wait_ge(up_filled, t - DEEP + 1)
                copy(ztT[k][:, :], m0[:, 0:P], n2w[:, 0:1]).then_inc(ztT_ready, 1)

            def half_relu(t, k, i):
                if more(t):
                    fetch(t + 1, k + 1)
                act.wait_ge(up_filled, t + 1)
                act.wait_ge(w1c_ready, 2 * t + 2)
                if later(t, 2):
                    act.wait_ge(down_filled, t - 1)
                for c in range(FC // 2):
                    ins = act.activation(hT[k % 2][:, c, :], ps_exp[k % 2][:, c * P:(c + 1) * P], ACT.Relu,
                                         bias=b1x[k % 2][:, c:c + 1])
                ins.then_inc(relu_a, 1)
                if more(t, 2):
                    transposed(t + 2, (k + 2) % DEEP)

            act.wait_ge(plan_ready, PLAN)
            act.wait_ge(row_scattered, 2 * 16 * B)
            for e in range(E // 2, E):
                pad = act.value_load(pad_u[0:1, e:e + 1], min_val=0, max_val=E * REGION - P)
                act.dma_start(dram["by_expert"][bass.ds(pad, P), :], pad_row[:, :]).then_inc(pad_stored, 16)
            act.wait_ge(moe_loaded, 2 * 16)
            fetch(0, 0)
            transposed(0, 0)
            transposed(1, 1)
            tile_steps(act, half_relu)

        @block.vector
        def _(dve):
            def stats(src, st, st_ready, src_ready, v):
                dve.wait_ge(src_ready, past(v))
                for t in range(T):
                    dve.bn_stats(st[:, t, :], src[:, t, :]).then_inc(st_ready, 1)

            def aggregate(st, agg, agg_ready):
                for t in range(T):
                    dve.bn_aggr(agg[:, t, :], st[:, t, :]).then_inc(agg_ready, 1)

            def normalise(b, p):
                dve.wait_ge(ln_ready, 6 * b + 2)
                dve.wait_ge(xnl_ready, past(b - 1))
                for t in range(T):
                    dve.tensor_scalar(xn[p][:, t, :], x_in[p][:, t, :], mv[p][:, t, 0:1], ln[p][:, 1, t:t + 1],
                                      ALU.subtract, ALU.mult).then_inc(xn_ready, 1)

            def latent(b, p):
                dve.wait_ge(yln_ready, 5 * b + 5)
                for t in range(T):
                    dve.tensor_scalar(lat[p][:, t, 0:L], qy[p][:, t, D:D + L], ymv[p][:, t, 0:1], yln[p][:, 4, t:t + 1],
                                      ALU.subtract, ALU.mult).then_inc(lat_ready, 1)

            def soft_max(b, p):
                dve.wait_ge(ybn_ready, past(2 * b + 2))
                dve.wait_ge(projA_ready, 2 * b + 2)
                dve.tensor_reduce(nqk[p][:, :, :], qkv[p][:, :, 0:2 * D].rearrange("p t (j d) -> p t j d", j=2),
                                  axis=AX.X, op=ALU.max, negate=True).then_inc(nqk_ready, 1)

            def soft_sum(b, p):
                dve.wait_ge(eqk_ready, b + 1)
                dve.tensor_reduce(sqk[p][:, 0, :, :], eqk[p][:, :, :].rearrange("p t (j d) -> p t j d", j=2),
                                  axis=AX.X, op=ALU.add).then_inc(sqk_ready, 1)
                dve.wait_ge(sqk_ready, 2 * b + 1)
                dve.reciprocal(sqk[p][:, 1, :, :], sqk[p][:, 0, :, :]).then_inc(sqk_ready, 1)

            def max_chunk(b, g, c, also=None, v=0):
                if also is not None:
                    dve.wait_ge(also, past(v))
                dve.wait_ge(max_filled, 12 * b + 6 * g + c + 1)
                if c == 0:
                    dve.wait_ge(msplit_ready, past(4 * (2 * b + g - 1)))
                if c < 2:
                    dst, src = nmax[g][:, 4 * c:4 * c + 4, 0], ps_max[c % 2][:, :].rearrange("p (h k) -> p h k", h=4)
                else:
                    dst, src = nmax[g][:, 2 * c - 4:2 * c - 2, 1], ps_max[c % 2][:, :].rearrange("p (h k) -> p h k", h=2)
                dve.tensor_reduce(dst, src, axis=AX.X, op=ALU.max, negate=True).then_inc(max_read, 1)

            def split_max(b, g):
                n = 4 * (2 * b + g)
                nm = nmax[g][:, :, :].rearrange("p h t -> p (h t)")
                dve.wait_ge(max_read, 12 * b + 6 * g + 6)
                dve.wait_ge(mT_filled, past(2 * b + g - 1))
                dve.tensor_copy(nmp[g][:, 0 * HG * T:1 * HG * T], nm).then_inc(msplit_ready, 1)
                dve.wait_ge(msplit_ready, n + 1)
                dve.tensor_tensor(mres[g][:, :], nm, nmp[g][:, 0 * HG * T:1 * HG * T], ALU.subtract).then_inc(msplit_ready, 1)
                dve.wait_ge(msplit_ready, n + 2)
                dve.tensor_copy(nmp[g][:, 1 * HG * T:2 * HG * T], mres[g][:, :]).then_inc(msplit_ready, 1)
                dve.wait_ge(msplit_ready, n + 3)
                dve.tensor_tensor(nmp[g][:, 2 * HG * T:3 * HG * T], mres[g][:, :], nmp[g][:, 1 * HG * T:2 * HG * T], ALU.subtract).then_inc(msplit_ready, 1)

            def pv_norm(b, p, g):
                v = m2[:, 0:S].rearrange("p (t h e) -> p t h e", t=T, h=HG)
                dve.wait_ge(pvT_filled, 2 * b + g + 1)
                dve.reciprocal(rden[g][:, :, :], v[:, :, :, HD]).then_inc(rden_ready, 1)
                dve.wait_ge(rden_ready, 2 * b + g + 1)
                dve.tensor_tensor(o[p][:, :, g * HG:(g + 1) * HG, :], v[:, :, :, 0:HD], spread(rden[g][:, :, :], HD),
                                  ALU.mult).then_inc(o_ready, 1)

            def residual(b, p):
                dve.wait_ge(wo_filled, b + 1)
                dve.wait_ge(xnl_ready, b + 1)
                dve.wait_ge(acc_ready, past(2 * (b - 1)))
                dve.tensor_tensor(x1[p][:, :, :], m2[:, 0:S].rearrange("p (t n) -> p t n", t=T), xnl[p][:, :, :],
                                  ALU.add).then_inc(x1_ready, 1)
                stats(x1[p], x1bn[p], x1bn_ready, x1_ready, b + 1)

            def residue1(b, p):
                dve.wait_ge(part1_ready, b + 1)
                dve.tensor_tensor(res[p][:, :], m0[:, :], part[p][:, 0, :], ALU.subtract).then_inc(res1_ready, 1)

            def landmark_out(b, p):
                dve.wait_ge(l0_filled, b + 1)
                dve.wait_ge(sqk_ready, 2 * b + 2)
                dve.wait_ge(acc_ready, past(2 * (b - 1)))
                for t in range(T):
                    dve.scalar_tensor_tensor(accx[p][:, t, :], m1[:, t * D:(t + 1) * D], sqk[p][:, 1, t, 0:1],
                                             x_in[p][:, t, :], ALU.mult, ALU.add).then_inc(l0_ready, 1)

            def pick(b, p):
                n = 6 * b
                dve.wait_ge(gate_filled, b + 1)
                dve.tensor_tensor(lg[:, :, :], m2[:, 0:T * E].rearrange("p (t e) -> p t e", e=E),
                                  gate_b[:, :].unsqueeze(1).broadcast_to((P, T, E)), ALU.add).then_inc(top_ready, 1)
                dve.wait_ge(top_ready, n + 1)
                dve.tensor_reduce(lmax[:, :], lg[:, :, :], axis=AX.X, op=ALU.max).then_inc(top_ready, 1)
                dve.wait_ge(top_ready, n + 2)
                dve.tensor_tensor(hit[:, :, :], lg[:, :, :], spread(lmax[:, :], E), ALU.is_ge).then_inc(top_ready, 1)
                dve.wait_ge(top_ready, n + 3)
                dve.tensor_tensor(pref[:, :, :], hit[:, :, :], first[:, :].unsqueeze(1).broadcast_to((P, T, E)),
                                  ALU.mult).then_inc(top_ready, 1)
                dve.wait_ge(top_ready, n + 4)
                dve.tensor_reduce(pmax[:, :], pref[:, :, :], axis=AX.X, op=ALU.max).then_inc(top_ready, 1)
                dve.wait_ge(top_ready, n + 5)
                dve.tensor_tensor(top16[p][:, :, :], pref[:, :, :], spread(pmax[:, :], E), ALU.is_ge).then_inc(top_ready, 1)

            def place(b, p):
                n = 5 * b
                dve.wait_ge(rank_filled, b + 1)
                dve.wait_ge(slot_ready, n)
                dve.tensor_tensor(cand[:, :, :], m2[:, 0:T * E].rearrange("p (t e) -> p t e", e=E),
                                  taken[:, :].unsqueeze(1).broadcast_to((P, T, E)), ALU.add).then_inc(slot_ready, 1)
                dve.wait_ge(slot_ready, n + 1)
                dve.tensor_tensor(taken[:, :], m2[:, T * E:(T + 1) * E], taken[:, :], ALU.add).then_inc(slot_ready, 1)
                dve.tensor_tensor(chosen[:, :, :], cand[:, :, :], top16[p][:, :, :], ALU.mult).then_inc(slot_ready, 1)
                dve.wait_ge(slot_ready, n + 3)
                dve.tensor_reduce(slot[:, :], chosen[:, :, :], axis=AX.X, op=ALU.add).then_inc(slot_ready, 1)
                dve.wait_ge(slot_ready, n + 4)
                dve.tensor_copy(slot_u[p][:, :], slot[:, :]).then_inc(slot_ready, 1)

            def step(b, p):
                q = 1 - p
                max_chunk(b, 0, 0)
                if there(b, 2):
                    stats(x_in[p], bn[p], bn_ready, x_loaded, 16 * (b + 3))
                    max_chunk(b, 0, 1, bn_ready, 2 * (b + 3))
                    aggregate(bn[p], mv[p], mv_ready)
                else:
                    max_chunk(b, 0, 1)
                if there(b, 1):
                    residue1(b + 1, q)
                if there(b, -1):
                    pv_norm(b - 1, q, 0)
                for c in range(2, 5):
                    max_chunk(b, 0, c)
                if there(b, -2):
                    place(b - 2, p)
                max_chunk(b, 0, 5)
                split_max(b, 0)
                if there(b, 2):
                    normalise(b + 2, p)
                max_chunk(b, 1, 0)
                max_chunk(b, 1, 1)
                max_chunk(b, 1, 2)
                if there(b, 1):
                    soft_sum(b + 1, q)
                if there(b, -1):
                    pv_norm(b - 1, q, 1)
                max_chunk(b, 1, 3)
                max_chunk(b, 1, 4)
                if there(b, -1):
                    residual(b - 1, q)
                    max_chunk(b, 1, 5, x1bn_ready, 2 * b)
                    aggregate(x1bn[q], x1mv[q], x1mv_ready)
                else:
                    max_chunk(b, 1, 5)
                split_max(b, 1)
                if there(b, 2):
                    stats(qy[p][:, :, D:D + L], ybn[p], ybn_ready, projB_ready, b + 3)
                    soft_max(b + 2, p)
                    aggregate(ybn[p], ymv[p], ymv_ready)
                    latent(b + 2, p)
                if there(b, -1):
                    pick(b - 1, q)
                if there(b, 1):
                    landmark_out(b + 1, q)

            def front(b, p):
                stats(x_in[p], bn[p], bn_ready, x_loaded, 16 * (b + 1))
                dve.wait_ge(bn_ready, 2 * b + 2)
                aggregate(bn[p], mv[p], mv_ready)
                normalise(b, p)

            def back(b, p):
                stats(qy[p][:, :, D:D + L], ybn[p], ybn_ready, projB_ready, b + 1)
                dve.wait_ge(ybn_ready, 2 * b + 2)
                aggregate(ybn[p], ymv[p], ymv_ready)
                latent(b, p)

            def prologue():
                dve.wait_ge(w_loaded, 16 * NW)
                for t_ in lat:
                    dve.memset(t_[:, :, L:P], 1.0)
                for t_ in nmp:
                    dve.memset(t_[:, :], 0.0)
                dve.memset(ones16[:, :], 1.0)
                dve.memset(all16[:, :], 1.0)
                dve.tensor_copy(tri16[:, :], tri_raw)
                dve.tensor_copy(ident16[:, :], ident[:, :])
                dve.tensor_copy(mask16[:, :, :], mask_raw[:, :, :])
                dve.tensor_scalar(wb[:, :], wb[:, :], n1w[:, 0:1], None, ALU.mult)
                chain = [0]

                def link(ins):
                    chain[0] += 1
                    ins.then_inc(bias_ready_v, 1)
                    dve.wait_ge(bias_ready_v, chain[0])

                link(dve.tensor_copy(bpart[:, 0, :], brow[:, :]))
                link(dve.tensor_tensor(btmp[:, 0, :], brow[:, :], bpart[:, 0, :], ALU.subtract))
                link(dve.tensor_copy(bpart[:, 1, :], btmp[:, 0, :]))
                link(dve.tensor_tensor(bpart[:, 2, :], btmp[:, 0, :], bpart[:, 1, :], ALU.subtract))
                link(dve.tensor_scalar(btmp[:, 0, :], bpart[:, 0, :], part_row[:, 0:1], None, ALU.mult))
                link(dve.scalar_tensor_tensor(btmp[:, 1, :], bpart[:, 1, :], part_row[:, 1:2], btmp[:, 0, :], ALU.mult, ALU.add))
                dve.scalar_tensor_tensor(bias16[:, :], bpart[:, 2, :], part_row[:, 2:3], btmp[:, 1, :], ALU.mult,
                                         ALU.add).then_inc(w_ready, 1)
                front(0, 0)
                dve.wait_ge(bias_ready, 1)
                dve.tensor_scalar(wkv[0:L, :], wkv[0:L, :], ln_g[:, 0:1], None, ALU.mult).then_inc(w_ready, 1)
                back(0, 0)
                soft_max(0, 0)
                front(1, 1)
                residue1(0, 0)
                soft_sum(0, 0)
                back(1, 1)
                soft_max(1, 1)
                landmark_out(0, 0)

            def last():
                pv_norm(B - 1, 1, 0)
                place(B - 2, 0)
                pv_norm(B - 1, 1, 1)
                residual(B - 1, 1)
                dve.wait_ge(x1bn_ready, 2 * B)
                aggregate(x1bn[1], x1mv[1], x1mv_ready)
                pick(B - 1, 1)
                place(B - 1, 1)

            steps(dve, step, prologue, last)

            def plan(ins, n):
                ins.then_inc(plan_ready, 1)
                dve.wait_ge(plan_ready, n)

            dve.wait_ge(slot_ready, 5 * B)
            dve.tensor_copy(pad_u[:, :], taken[:, :]).then_inc(plan_ready, 1)
            plan(dve.tensor_tensor(count[:, :], taken[:, :], region[:, :], ALU.subtract), 2)
            plan(dve.tensor_tensor(over[:, :, :], spread(count[:, :], NTOK // P),
                                   steps128[:, :].unsqueeze(1).broadcast_to((P, E, NTOK // P)), ALU.is_gt), 3)
            plan(dve.tensor_reduce(tiles[:, :], over[:, :, :], axis=AX.X, op=ALU.add), 4)
            dve.tensor_scalar(jump[:, :], tiles[:, :], float(-P), float(REGION), ALU.mult, ALU.add).then_inc(plan_ready, 1)
            plan(dve.tensor_copy(ends[:, 0:1], tiles[:, 0:1]), 6)
            for e in range(1, E):
                plan(dve.tensor_tensor(ends[:, e:e + 1], ends[:, e - 1:e], tiles[:, e:e + 1], ALU.add), 6 + e)
            plan(dve.tensor_tensor(passed[:, :, :], tile_no[:, :].unsqueeze(1).broadcast_to((P, E, NT)),
                                   spread(ends[:, :], NT), ALU.is_ge), 10)
            dve.tensor_reduce(expert_f[:, :], passed[:, 0:E - 1, :].rearrange("p e n -> p n e"), axis=AX.X,
                              op=ALU.add).then_inc(plan_ready, 1)
            dve.tensor_scalar(inside[:, :], tile_no[:, :], ends[:, E - 1:E], float(P), ALU.min, ALU.mult).then_inc(plan_ready, 1)
            plan(dve.tensor_tensor(jumps[:, :, :], passed[:, :, :], spread(jump[:, :], NT), ALU.mult), 13)
            dve.tensor_copy(expert_u[:, :], expert_f[:, :]).then_inc(plan_ready, 1)
            plan(dve.tensor_reduce(jumped[:, :], jumps[:, :, :].rearrange("p e n -> p n e"), axis=AX.X, op=ALU.add), 15)
            plan(dve.tensor_tensor(start_u[:, :], jumped[:, :], inside[:, :], ALU.add), PLAN)

            def fetch(t, k):
                e = dve.value_load(expert_u[0:1, bass.ds(t, 1)], min_val=0, max_val=E - 1)
                if later(t, 2):
                    dve.wait_ge(down_filled, t - 1)
                dve.tensor_copy(w2c[k % 2][:, :], w2[:, bass.ds(e, 1), :].rearrange("p o f -> p (o f)")).then_inc(w2c_ready, 1)

            def half_relu(t, k, i):
                dve.wait_ge(up_filled, t + 1)
                dve.wait_ge(w1c_ready, 2 * t + 2)
                if later(t, 2):
                    dve.wait_ge(down_filled, t - 1)
                for c in range(FC // 2, FC):
                    ins = dve.tensor_scalar(hT[k % 2][:, c, :], (m2, ps_pv)[k % 2][:, c % 2 * P:(c % 2 + 1) * P],
                                            b1x[k % 2][:, c:c + 1], 0.0, ALU.add, ALU.max)
                ins.then_inc(relu_v, 1)
                if more(t):
                    fetch(t + 1, k + 1)
                e = dve.value_load(expert_u[0:1, bass.ds(t, 1)], min_val=0, max_val=E - 1)
                dve.wait_ge(down_filled, t + 1)
                if later(t, 2):
                    dve.wait_ge(sum_ready, t - 1)
                dve.tensor_tensor(y[k % 2][:, :], ps_max[k % 2][:, 0:D], b2b[:, bass.ds(e, 1), :].rearrange("p o d -> p (o d)"),
                                  ALU.add).then_inc(y_ready, 1)

            dve.wait_ge(moe_loaded, 2 * 16)
            fetch(0, 0)
            tile_steps(dve, half_relu)

        @block.tensor
        def _(pe):
            def mm(o_, lhsT, rhs, start=True, stop=True):
                return pe.matmul(o_, lhsT, rhs, start=start, stop=stop)

            def xnT_(b, p):
                pe.wait_ge(xn_ready, 2 * b + 2)
                pe.wait_ge(res1_ready, b)
                for t in range(T):
                    ins = pe.transpose(m0[:, t * P:(t + 1) * P], xn[p][:, t, :], ident[:, :])
                ins.then_inc(xnT_filled, 1)

            def projA(b, p, t):
                pe.wait_ge(xnT_ready, b + 1)
                pe.wait_ge(projA_ready, 2 * b + t)
                mm(m0[:, 0:3 * D], xnT[p][:, t * P:(t + 1) * P], wa[:, :], stop=False)
                mm(m0[:, 0:3 * D], ones16[:, :], bias16[:, 0:3 * D], start=False).then_inc(projA_filled, 1)

            def projB(b, p):
                pe.wait_ge(projA_ready, 2 * b + 2)
                for t in range(T):
                    ins = mm(m0[:, t * (D + L):(t + 1) * (D + L)], xnT[p][:, t * P:(t + 1) * P], wb[:, :])
                ins.then_inc(projB_filled, 1)

            def latT_(b, p):
                pe.wait_ge(lat_ready, 2 * b + 2)
                for t in range(T):
                    ins = pe.transpose(m0[:, t * P:(t + 1) * P], lat[p][:, t, :], ident[:, :])
                ins.then_inc(latT_filled, 1)

            def k_(b, p):
                pe.wait_ge(latT_ready, b + 1)
                for t in range(T):
                    ins = mm(m0[:, t * D:(t + 1) * D], latT[p][:, t * P:(t + 1) * P], wkv[:, 0:D])
                ins.then_inc(k_filled, 1)

            def qkT(b, p):
                pe.wait_ge(qrope_ready, 3 * b + 3)
                pe.wait_ge(krope_ready, 2 * b + 2)
                for t in range(T):
                    pe.transpose(m0[:, t * P:(t + 1) * P], qrot[p][:, t, :], ident[:, :])
                for t in range(T):
                    ins = pe.transpose(m0[:, S + t * P:S + (t + 1) * P], krot[p][:, t, :], ident[:, :])
                ins.then_inc(qkT_filled, 1)

            def max_chunk(b, p, g, c):
                n = 12 * b + 6 * g + c
                if c == 0:
                    pe.wait_ge(q_spread, PARTS * 16 * (b + 1))
                    pe.wait_ge(k_spread, PARTS * 16 * (b + 1))
                pe.wait_ge(max_read, past(n - 1))
                bank = ps_max[c % 2]
                t, nh, h0 = (0, 4, 4 * c) if c < 2 else (1, 2, 2 * c - 4)
                w = 512 // nh
                v = bank[:, :].rearrange("p (h k) -> p h k", h=nh)
                for i in range(nh):
                    col = (g * HG + h0 + i) * S
                    mm(bank[:, i * w:(i + 1) * w], qst[p][0:STACK, col + t * P:col + (t + 1) * P],
                             kst[p][0:STACK, col:col + w], start=(i == 0), stop=False)
                mm(v[:, :, t * P:(t + 1) * P], ident16[:, :], mask16[:, 0:1, :].broadcast_to((P, nh, P)),
                   start=False).then_inc(max_filled, 1)

            def exp_chunk(b, p, g, c):
                n = 12 * b + 6 * g + c
                if c == 0:
                    pe.wait_ge(m_spread, 16 * (2 * b + g + 1))
                pe.wait_ge(exp_ready, past(n - 1))
                bank = ps_exp[c % 2]
                kt, nh, h0 = (0, 2, 2 * c) if c < 4 else (1, 4, 4 * c - 16)
                w = 512 // nh
                v = bank[:, :].rearrange("p (h q) -> p h q", h=nh)
                for i in range(nh):
                    col = (g * HG + h0 + i) * S
                    mm(bank[:, i * w:(i + 1) * w], kst[p][:, col + kt * P:col + (kt + 1) * P],
                       qst[p][:, col + kt * P:col + S], start=(i == 0), stop=False)
                mm(v[:, :, 0:P], ident16[:, :], mask16[:, 1:2, :].broadcast_to((P, nh, P)),
                   start=False).then_inc(exp_filled, 1)

            def pv(b, p, g, heads):
                if heads[0] == 0:
                    pe.wait_ge(pvs_ready, 2 * b + g)
                    pe.wait_ge(exp_ready, 12 * b + 6 * g + 6)
                    pe.wait_ge(v_ready, b + 1)
                for h in heads:
                    mm(ps_pv[:, 0:S], vals[p][:, 0, g * HG + h, :], prob[g][:, h, 0:S], start=(h == 0), stop=False)
                    ins = mm(ps_pv[:, P:S], vals[p][:, 1, g * HG + h, :], prob[g][:, h, S:S + P], start=False,
                             stop=(h == HG - 1))
                if heads[-1] == HG - 1:
                    ins.then_inc(pv_filled, 1)

            def v_(b, p):
                pe.wait_ge(l0_ready, 2 * b)
                pe.wait_ge(latT_ready, b + 1)
                for t in range(T):
                    ins = mm(m1[:, t * D:(t + 1) * D], latT[p][:, t * P:(t + 1) * P], wkv[:, D:2 * D])
                ins.then_inc(v_filled, 1)

            def pvT_(b, g):
                if g == 0:
                    pe.wait_ge(top_ready, past(6 * b - 5))
                else:
                    pe.wait_ge(slot_ready, past(5 * b - 3))
                    pe.wait_ge(o_ready, 2 * b + 1)
                pe.wait_ge(pvs_ready, 2 * b + g + 1)
                for t in range(T):
                    ins = pe.transpose(m2[:, t * P:(t + 1) * P], pvs[g][:, t * P:(t + 1) * P], ident[:, :])
                ins.then_inc(pvT_filled, 1)

            def oT_(b, p):
                pe.wait_ge(o_ready, 2 * b + 2)
                for t in range(T):
                    ins = pe.transpose(m2[:, t * P:(t + 1) * P], o[p][:, t, :, :].rearrange("p h d -> p (h d)"), ident[:, :])
                ins.then_inc(oT_filled, 1)

            def wo_(b, p):
                pe.wait_ge(oT_ready, b + 1)
                for t in range(T):
                    ins = mm(m2[:, t * D:(t + 1) * D], oT[p][:, t * P:(t + 1) * P], wo[:, :])
                ins.then_inc(wo_filled, 1)

            def zT_(b, p):
                pe.wait_ge(z_ready, b + 1)
                for t in range(T):
                    ins = pe.transpose(m2[:, t * P:(t + 1) * P], rows[p][:, t, 0:D], ident[:, :])
                ins.then_inc(zT_filled, 1)

            def gate_(b, p):
                pe.wait_ge(zT_ready, b + 1)
                for t in range(T):
                    ins = mm(m2[:, t * E:(t + 1) * E], zT[p][:, t * P:(t + 1) * P], gate[:, :])
                ins.then_inc(gate_filled, 1)

            def rank_(b, p, bank_free):
                pe.wait_ge(o_ready, bank_free)
                pe.wait_ge(top_ready, 6 * (b + 1))
                to, all_ = m2[:, 0:T * E], m2[:, T * E:(T + 1) * E]
                mm(to, tri16[:, :], top16[p][:, :, :].rearrange("p t e -> p (t e)"), stop=False)
                mm(m2[:, E:2 * E], all16[:, :], top16[p][:, 0, :], start=False)
                mm(all_, all16[:, :], top16[p][:, 0, :], stop=False)
                mm(all_, all16[:, :], top16[p][:, 1, :], start=False).then_inc(rank_filled, 1)

            def mT_(b, g):
                pe.wait_ge(v_ready, (b + 2) if there(b, 1) else B)
                pe.wait_ge(l0_ready, 2 * (b + 1))
                pe.wait_ge(mT_ready, 2 * b + g)
                pe.wait_ge(msplit_ready, 4 * (2 * b + g + 1))
                pe.transpose(m1h[:, 0:P], nmp[g][:, :], ident16[:, :]).then_inc(mT_filled, 1)

            def eqT_(b, p):
                pe.wait_ge(v_ready, b + 1)
                pe.wait_ge(mT_ready, 2 * b)
                pe.wait_ge(eqk_ready, b + 1)
                for t in range(T):
                    ins = pe.transpose(m1[:, t * P:(t + 1) * P], eqk[p][:, t, 0:D], ident[:, :])
                ins.then_inc(eqT_filled, 1)

            def klC_(b, p):
                pe.wait_ge(eqT_ready, b + 1)
                pe.wait_ge(k3_ready, b + 1)
                for t in range(T):
                    mm(m1[:, 0:D], pool4[:, t, :], kh[p][:, t, :], start=(t == 0), stop=(t == T - 1))
                for t in range(T):
                    ins = mm(m1[:, D:2 * D], kh[p][:, t, :], k3[p][:, t, :], start=(t == 0), stop=(t == T - 1))
                ins.then_inc(klC_filled, 1)

            def gram_(b, p):
                pe.wait_ge(klC_ready, b + 1)
                mm(m1[:, 0:D], klC[p][:, 0:D], klC[p][:, 0:D]).then_inc(gram_filled, 1)

            def mid_(b, p):
                pe.wait_ge(gram_ready, b + 1)
                mm(m1[:, 0:D], gram[p][:, :], klC[p][:, D:2 * D]).then_inc(mid_filled, 1)

            def l0_(b, p):
                pe.wait_ge(mid_ready, b + 1)
                for t in range(T):
                    ins = mm(m1[:, t * D:(t + 1) * D], eqT[p][:, t * P:(t + 1) * P], mid[p][:, :])
                ins.then_inc(l0_filled, 1)

            def step(b, p):
                q = 1 - p
                for c in range(6):
                    max_chunk(b, p, 0, c)
                    if c == 0 and there(b, -1):
                        pvT_(b - 1, 0)
                    if c == 1 and there(b, 1):
                        qkT(b + 1, q)
                    if c == 3 and there(b, -2):
                        rank_(b - 2, p, 2 * b - 1)
                    if there(b, -1):
                        pv(b - 1, q, 1, (c,))
                max_chunk(b, p, 1, 0)
                if there(b, -1):
                    pv(b - 1, q, 1, (6,))
                max_chunk(b, p, 1, 1)
                if there(b, -1):
                    pv(b - 1, q, 1, (7,))
                if there(b, 1):
                    v_(b + 1, q)
                if there(b, 2):
                    xnT_(b + 2, p)
                max_chunk(b, p, 1, 2)
                mT_(b, 0)
                if there(b, -1):
                    pvT_(b - 1, 1)
                if there(b, 2):
                    projA(b + 2, p, 0)
                max_chunk(b, p, 1, 3)
                if there(b, -1):
                    oT_(b - 1, q)
                if there(b, 2):
                    projA(b + 2, p, 1)
                max_chunk(b, p, 1, 4)
                if there(b, -1):
                    wo_(b - 1, q)
                if there(b, 2):
                    projB(b + 2, p)
                max_chunk(b, p, 1, 5)
                exp_chunk(b, p, 0, 0)
                exp_chunk(b, p, 0, 1)
                mT_(b, 1)
                exp_chunk(b, p, 0, 2)
                if there(b, 1):
                    eqT_(b + 1, q)
                exp_chunk(b, p, 0, 3)
                if there(b, 1):
                    klC_(b + 1, q)
                if there(b, -1):
                    zT_(b - 1, q)
                exp_chunk(b, p, 0, 4)
                if there(b, 1):
                    gram_(b + 1, q)
                exp_chunk(b, p, 0, 5)
                if there(b, 1):
                    mid_(b + 1, q)
                if there(b, 2):
                    latT_(b + 2, p)
                exp_chunk(b, p, 1, 0)
                if there(b, -1):
                    gate_(b - 1, q)
                exp_chunk(b, p, 1, 1)
                if there(b, 1):
                    l0_(b + 1, q)
                if there(b, 2):
                    k_(b + 2, p)
                for c, heads in ((2, (0, 1)), (3, (2, 3)), (4, (4, 5)), (5, (6, 7))):
                    pv(b, p, 0, heads)
                    exp_chunk(b, p, 1, c)

            def front(b, p):
                xnT_(b, p)
                projA(b, p, 0)
                projA(b, p, 1)
                projB(b, p)
                latT_(b, p)

            def prologue():
                pe.wait_ge(w_ready, 1)
                mm(m0[0:L + 1, 0:2 * D], ln_b[:, :], wkv[0:L, :]).then_inc(lnb_filled, 1)
                pe.wait_ge(bias_ready, 1)
                front(0, 0)
                pe.wait_ge(w_ready, 2)
                k_(0, 0)
                v_(0, 0)
                qkT(0, 0)
                front(1, 1)
                k_(1, 1)
                eqT_(0, 0)
                klC_(0, 0)
                gram_(0, 0)
                mid_(0, 0)
                l0_(0, 0)

            def last():
                pvT_(B - 1, 0)
                pv(B - 1, 1, 1, tuple(range(HG)))
                rank_(B - 2, 0, 2 * B - 1)
                pvT_(B - 1, 1)
                oT_(B - 1, 1)
                wo_(B - 1, 1)
                zT_(B - 1, 1)
                gate_(B - 1, 1)
                rank_(B - 1, 1, 2 * B)

            steps(pe, step, prologue, last)

            def turn(t, k, i):
                pe.wait_ge(tile_loaded[k], 16 * (i + 1))
                if later(t, 1):
                    pe.wait_ge(ztT_ready, t)
                pe.transpose(m0[:, 0:P], tile_in[k][:, 0:D], ident[:, :]).then_inc(ztT_filled, 1)

            def up(t, k):
                pe.wait_ge(w1c_ready, 2 * (t + 1))
                pe.wait_ge(ztT_ready, t + 1)
                if later(t, 2):
                    pe.wait_ge(relu_a, t - 1)
                    pe.wait_ge(relu_v, t - 1)
                for c in range(FC):
                    bank = ps_exp[k % 2] if c < FC // 2 else (m2, ps_pv)[k % 2]
                    ins = mm(bank[:, c % 2 * P:(c % 2 + 1) * P], w1c[k % 2][:, c * P:(c + 1) * P], ztT[k][:, :])
                ins.then_inc(up_filled, 1)

            def up_down(t, k, i):
                if more(t, 2):
                    turn(t + 2, (k + 2) % DEEP, i + (k + 2) // DEEP)
                if more(t):
                    up(t + 1, (k + 1) % DEEP)
                pe.wait_ge(relu_a, t + 1)
                pe.wait_ge(relu_v, t + 1)
                pe.wait_ge(w2c_ready, t + 1)
                if later(t, 2):
                    pe.wait_ge(y_ready, t - 1)
                for c in range(FC):
                    ins = mm(ps_max[k % 2][:, 0:D], hT[k % 2][:, c, :], w2c[k % 2][:, c * D:(c + 1) * D],
                             start=(c == 0), stop=(c == FC - 1))
                ins.then_inc(down_filled, 1)

            turn(0, 0, 0)
            turn(1, 1, 0)
            up(0, 0)
            tile_steps(pe, up_down)


def constants():
    f = np.float32
    half = HD // 2
    pos = np.arange(S, dtype=f)[:, None]
    inv = (f(1.0) / f(10000.0) ** (np.arange(half, dtype=f) / f(half))).astype(f)
    ang = (pos * inv[None, :]).astype(f)
    rope = np.zeros((P, 2, 2, T, 64), f)
    for t in range(T):
        for w, fn in ((0, np.cos), (1, np.sin)):
            tab = np.repeat(fn(ang[t * P:(t + 1) * P]).astype(f), H, axis=1)
            rope[:, 0, w, t] = tab * f(1.0 / np.sqrt(HD))
            rope[:, 1, w, t] = tab
    r, c = np.arange(P)[:, None], np.arange(P)[None, :]
    mask = np.stack([np.where(c > r, MASKED, 0.0), np.where(r > c, MASKED, 0.0)], 1).astype(f)
    pool4 = np.zeros((P, T, P), f)
    for t in range(T):
        pool4[np.arange(P), t, (t * P + np.arange(P)) // (S // L)] = L / S
    every = lambda v: np.broadcast_to(np.asarray(v, f)[None, :], (P, len(v)))
    return {"tri": (r < c).astype(f), "first": every(E - np.arange(E)), "region": every(REGION * np.arange(E)),
            "token": (np.arange(B * T)[None, :] * P + r).astype(np.uint32), "steps128": every(P * np.arange(NTOK // P)),
            "tile_no": every(np.arange(NT)), "ident": np.eye(P, dtype=f), "mask": mask, "pool4": pool4, "rope": rope,
            "part_row": np.eye(PARTS, dtype=f)}


def kernel(**inputs):
    import concourse.bacc as _bacc
    from concourse.bass_utils import run_bass_kernel_spmd as _run

    g = {k.replace("L0_", ""): np.asarray(v) for k, v in inputs.items()}
    by_dim = np.arange(D).reshape(H, HD).T.reshape(-1)
    rows = lambda a, n: np.broadcast_to(a.reshape(1, -1), (n, a.size))
    lnb = np.zeros((L, L + 1), np.float32)
    lnb[:, L] = g["ffn_ln_b"]
    a = constants()
    a.update({
        "x": g["attn_hidden_states"],
        "wa": np.concatenate([g["attn_Wq"], g["attn_Wk"], g["attn_Wv"]], 1),
        "wb": np.concatenate([g["ffn_Wq"].T[:, by_dim], g["ffn_Wdkv"].T], 1),
        "wkv": np.concatenate([g["ffn_Wuk"].T[:, by_dim], g["ffn_Wuv"].T], 1),
        "n1w": g["ffn_norm1_w"][:, None], "n2w": g["ffn_norm2_w"][:, None],
        "ln_g": g["ffn_ln_g"][:, None], "ln_b": lnb,
        "wo": g["ffn_Wo"].T, "gate": g["ffn_gate_w"].T, "gate_b": rows(g["ffn_gate_b"], P),
        "w1": g["ffn_W1"].transpose(2, 0, 1),
        "w2": g["ffn_W2"].reshape(E, D, FC, P).transpose(3, 0, 2, 1).reshape(P, E, F),
        "b2b": np.broadcast_to(g["ffn_b2"][None], (P, E, D)),
        "b1c": g["ffn_b1"].reshape(E, FC, P).transpose(2, 0, 1),
        "brow": rows(np.concatenate([g["attn_bq"], g["attn_bk"], g["attn_bv"]]), PARTS),
    })
    nc = _bacc.Bacc("TRN2", target_bir_lowering=False, num_devices=1)
    arrays, dram = {}, {}
    for n, v in a.items():
        v = np.ascontiguousarray(v)
        arrays[f"in_{n}"] = v
        dram[n] = nc.dram_tensor(f"in_{n}", v.shape, mybir.dt.from_np(v.dtype), kind="ExternalInput").ap()
    for n, parts in (("q_parts", 2 * PARTS - 1), ("k_parts", PARTS)):
        dram[n] = nc.dram_tensor(n, (2, parts, P * S), mybir.dt.bfloat16, kind="Internal").ap()
    dram["by_expert"] = nc.dram_tensor("by_expert", (E * REGION + P, ROW), mybir.dt.float32, kind="Internal").ap()
    out = nc.dram_tensor("out_0", (B, S, D), mybir.dt.float32, kind="ExternalOutput").ap()
    build(nc, dram, out)
    r = _run(nc, [arrays], core_ids=[0])
    return r.results[0]["out_0"]
```
